# Optimizing a Trainium2 kernel written in Bass

```python
import numpy as np
import jax
import jax.numpy as jnp

def _softmax(x, axis=-1):
    return jax.nn.softmax(x, axis=axis)

def _gelu(x):
    return jax.nn.gelu(x, approximate=True)

def _silu(x):
    return jax.nn.silu(x)

def _sigmoid(x):
    return jax.nn.sigmoid(x)

def _layernorm(x, axis=-1, eps=1e-05):
    m = jnp.mean(x, axis=axis, keepdims=True)
    v = jnp.var(x, axis=axis, keepdims=True)
    return (x - m) / jnp.sqrt(v + eps)

def _scatter_add(tgt, idx, src, axis=0):
    return tgt.at[idx].add(src)

def _segment_sum(src, seg, n):
    return jax.ops.segment_sum(src, seg, n)
kernel_name = 'mk_decoder_preln_d2_seqx_r8_a3b786'

def setup_inputs(seed: int=0):
    np.random.seed(seed)
    _w = jnp.asarray

    def _rec_inputs():
        import jax
        import jax.numpy as jnp
        _rk = jax.random.key(seed)
        x = 0.000341 + 1 * jax.random.normal(jax.random.fold_in(_rk, 1), (16, 128, 256), jnp.float32)
        _lenS = 128 - jax.random.randint(jax.random.fold_in(_rk, 7), (16,), 0, max(1, 128 // 4) + 1, jnp.int32)
        _lenS2 = 128 - jax.random.randint(jax.random.fold_in(_rk, 8), (16,), 0, max(1, 128 // 4) + 1, jnp.int32)
        _ctx_2048P = jax.random.normal(jax.random.fold_in(_rk, 11), (16, 16, 256), jnp.float32)
        _ctx_2048c = jax.random.dirichlet(jax.random.fold_in(_rk, 511), 0.3 * jnp.ones((16,), jnp.float32), (16, 128))
        _ctx_2048t = jnp.einsum('bsk,bkd->bsd', _ctx_2048c, _ctx_2048P)
        _ctx_2048t = _ctx_2048t * jax.lax.rsqrt(jnp.mean(jnp.square(_ctx_2048t)) + 1e-12) * 0.953939
        ctx_2048 = -1.47943e-05 + 1.00017 * (_ctx_2048t + 0.3 * jax.random.normal(jax.random.fold_in(_rk, 611), (16, 128, 256), jnp.float32))
        return (x, ctx_2048)
    x, ctx_2048 = _rec_inputs()

    def _L0_attn_setup():
        import jax, jax.numpy as jnp
        import numpy as np
        from jax import lax
        B, S, H = (2, 256, 256)
        EXPAND, N, K, R, NH = (2, 16, 4, 128, 2)
        I = EXPAND * H
        HD = I // NH

        def _mixer(hidden_states, in_proj_w, conv_w, conv_b, x_proj_weight, dt_proj_weight, dt_proj_bias, A_log, D, out_proj_w):
            b, s, _ = hidden_states.shape
            proj = jnp.einsum('bsh,oh->bos', hidden_states, in_proj_w)
            proj = proj.reshape(b, I, 2, s)
            x = proj[:, :, 0, :]
            gate = proj[:, :, 1, :].reshape(b, NH, HD, s).transpose(1, 0, 2, 3)
            xp = jnp.pad(x, ((0, 0), (0, 0), (K - 1, 0)))
            conv = lax.conv_general_dilated(xp, conv_w[:, None, :], window_strides=(1,), padding='VALID', dimension_numbers=('NCH', 'OIH', 'NCH'), feature_group_count=I)
            x = jax.nn.silu(conv + conv_b[None, :, None])
            x = x.reshape(b, NH, HD, s).transpose(1, 0, 2, 3)
            ssm_p = jnp.einsum('hrd,hbds->hbsr', x_proj_weight, x)
            dt_in, Bm, Cm = jnp.split(ssm_p, [R, R + N], axis=-1)
            dt = jnp.einsum('hdr,hbsr->hbds', dt_proj_weight, dt_in) + dt_proj_bias[:, None, :, None]
            dt = jax.nn.softplus(dt)
            A = -jnp.exp(A_log)

            def step(state, inp):
                dt_t, B_t, C_t, x_t = inp
                dA = jnp.exp(A[:, None, :, :] * dt_t[..., None])
                dBu = dt_t[..., None] * B_t[:, :, None, :] * x_t[..., None]
                state = dA * state + dBu
                y = jnp.einsum('hbdn,hbn->hbd', state, C_t)
                return (state, y)
            init = jnp.zeros((NH, b, HD, N), dtype=x.dtype)
            xs = (dt.transpose(3, 0, 1, 2), Bm.transpose(2, 0, 1, 3), Cm.transpose(2, 0, 1, 3), x.transpose(3, 0, 1, 2))
            _, ys = lax.scan(step, init, xs)
            y = ys.transpose(1, 2, 3, 0)
            y = y + x * D[:, None, :, None]
            y = y * jax.nn.silu(gate)
            y = y.transpose(1, 0, 2, 3).reshape(b, I, s).transpose(0, 2, 1)
            return jnp.einsum('bsi,hi->bsh', y, out_proj_w)
        key = jax.random.key(seed)
        ks = jax.random.split(key, 9)
        hidden_states = jax.random.normal(ks[0], (B, S, H), dtype=jnp.float32)
        in_proj_w = jax.random.normal(ks[1], (2 * I, H), dtype=jnp.float32) * H ** (-0.5)
        conv_w = jax.random.normal(ks[2], (I, K), dtype=jnp.float32) * K ** (-0.5)
        conv_b = jax.random.normal(ks[3], (I,), dtype=jnp.float32) * 0.02
        x_proj_weight = jax.random.normal(ks[4], (NH, R + 2 * N, HD), dtype=jnp.float32) * HD ** (-0.5)
        dt_proj_weight = jax.random.normal(ks[5], (NH, HD, R), dtype=jnp.float32) * R ** (-0.5)
        dt_proj_bias = jax.random.normal(ks[6], (NH, HD), dtype=jnp.float32) * 0.02
        A_log = jnp.broadcast_to(jnp.log(jnp.arange(1, N + 1, dtype=jnp.float32))[None, None, :], (NH, HD, N))
        D = jnp.ones((NH, HD), dtype=jnp.float32)
        out_proj_w = jax.random.normal(ks[7], (H, I), dtype=jnp.float32) * I ** (-0.5)
        return {'hidden_states': hidden_states, 'in_proj_w': in_proj_w, 'conv_w': conv_w, 'conv_b': conv_b, 'x_proj_weight': x_proj_weight, 'dt_proj_weight': dt_proj_weight, 'dt_proj_bias': dt_proj_bias, 'A_log': A_log, 'D': D, 'out_proj_w': out_proj_w}
    _L0_attn_all = _L0_attn_setup()
    _L0_attn_in = {k: v for k, v in _L0_attn_all.items() if k in ('in_proj_w', 'conv_w', 'conv_b', 'x_proj_weight', 'dt_proj_weight', 'dt_proj_bias', 'A_log', 'D', 'out_proj_w')}
    del _L0_attn_all

    def _L0_xattn_setup():
        import jax, jax.numpy as jnp
        import numpy as np

        def _wkv(time_decay, time_first, k, v):
            w = -jnp.exp(time_decay)
            u = time_first
            B, T, C = k.shape
            aa = jnp.zeros((B, C), dtype=k.dtype)
            bb = jnp.zeros((B, C), dtype=k.dtype)
            pp = jnp.full((B, C), -1e+38, dtype=k.dtype)

            def step(carry, kv_t):
                aa, bb, pp = carry
                kt, vt = kv_t
                ww = u + kt
                q = jnp.maximum(pp, ww)
                e1 = jnp.exp(pp - q)
                e2 = jnp.exp(ww - q)
                y_t = (e1 * aa + e2 * vt) / (e1 * bb + e2)
                ww2 = pp + w
                q2 = jnp.maximum(ww2, kt)
                e1b = jnp.exp(ww2 - q2)
                e2b = jnp.exp(kt - q2)
                new_carry = (e1b * aa + e2b * vt, e1b * bb + e2b, q2)
                return (new_carry, y_t)
            ks = jnp.transpose(k, (1, 0, 2))
            vs = jnp.transpose(v, (1, 0, 2))
            _, ys = jax.lax.scan(step, (aa, bb, pp), (ks, vs))
            return jnp.transpose(ys, (1, 0, 2))
        key = jax.random.key(seed)
        k1, k2, k3, k4 = jax.random.split(key, 4)
        B, T, C = (8, 128, 256)
        return {'batch_size': B, 'seq_len': T, 'embedding_dim': C, 'time_decay': jax.random.normal(k1, (C,), dtype=jnp.float32), 'time_first': jax.random.normal(k2, (C,), dtype=jnp.float32), 'k': jax.random.normal(k3, (B, T, C), dtype=jnp.float32), 'v': jax.random.normal(k4, (B, T, C), dtype=jnp.float32)}
    _L0_xattn_all = _L0_xattn_setup()
    _L0_xattn_in = {k: v for k, v in _L0_xattn_all.items() if k in ('time_decay', 'time_first')}
    del _L0_xattn_all

    def _L0_ffn_setup():
        import jax, jax.numpy as jnp
        import numpy as np
        B, S, H = (2, 128, 256)
        I = 128
        E = 32
        Z = 32
        K = 8
        SCALE = 1.5
        CAP = 128
        EPS = 1e-20

        def _moe_forward(x, w_cls, bias, w_gate_up, w_down):
            T = x.shape[0] * x.shape[1]
            xf = x.reshape(T, H)
            logits = xf.astype(jnp.float32) @ w_cls.T
            scores = jax.nn.softmax(logits, axis=-1)
            _, topk_idx = jax.lax.top_k(scores + bias[None, :], K)
            w = jnp.take_along_axis(scores, topk_idx, axis=-1)
            w = w / (w.sum(-1, keepdims=True) + EPS) * SCALE
            routed = topk_idx < E
            w_r = jnp.where(routed, w, 0.0)
            w_z = jnp.where(routed, 0.0, w)
            N = T * K
            flat_ids = jnp.where(routed, topk_idx, E).reshape(-1)
            x_exp = jnp.repeat(xf, K, axis=0)
            order = jnp.argsort(flat_ids)
            ids_s = flat_ids[order]
            counts = jax.ops.segment_sum(jnp.ones(N, jnp.int32), flat_ids, num_segments=E + 1)
            starts = jnp.cumsum(counts) - counts
            pos = jnp.arange(N) - starts[ids_s]
            buf = jnp.zeros((E, CAP, H), xf.dtype).at[ids_s, pos].set(x_exp[order], mode='drop')
            gu = jnp.einsum('ech,ehf->ecf', buf, w_gate_up)
            g, u = jnp.split(gu, 2, axis=-1)
            act = jax.nn.silu(g) * u
            y = jnp.einsum('eci,eih->ech', act, w_down)
            valid = (ids_s < E) & (pos < CAP)
            y_tok = jnp.where(valid[:, None], y[jnp.clip(ids_s, 0, E - 1), jnp.clip(pos, 0, CAP - 1)], 0.0)
            y_exp = jnp.zeros((N, H), xf.dtype).at[order].set(y_tok).reshape(T, K, H)
            routed_out = jnp.einsum('tk,tkh->th', w_r, y_exp)
            out = routed_out * (1.0 + w_z.sum(-1, keepdims=True))
            return out.reshape(x.shape)
        key = jax.random.key(seed)
        ks = jax.random.split(key, 5)
        x = jax.random.normal(ks[0], (B, S, H), jnp.float32)
        w_cls = jax.random.normal(ks[1], (E + Z, H), jnp.float32) / np.float32(np.sqrt(H))
        bias = jax.random.normal(ks[2], (E + Z,), jnp.float32) * 0.02
        w_gate_up = jax.random.normal(ks[3], (E, H, 2 * I), jnp.float32) * 0.02
        w_down = jax.random.normal(ks[4], (E, I, H), jnp.float32) * 0.02
        return {'x': x, 'w_cls': w_cls, 'bias': bias, 'w_gate_up': w_gate_up, 'w_down': w_down}
    _L0_ffn_all = _L0_ffn_setup()
    _L0_ffn_in = {k: v for k, v in _L0_ffn_all.items() if k in ('w_cls', 'bias', 'w_gate_up', 'w_down')}
    del _L0_ffn_all

    def _L1_attn_setup():
        import jax, jax.numpy as jnp
        import numpy as np
        D_MODEL = 256
        EXPAND = 2
        HEADDIM = 64
        D_STATE = 64
        D_CONV = 4
        D_INNER = EXPAND * D_MODEL
        NHEADS = D_INNER // HEADDIM
        NGROUPS = 1
        CONV_DIM = D_INNER + 2 * NGROUPS * D_STATE
        D_IN_PROJ = 2 * D_INNER + 2 * NGROUPS * D_STATE + NHEADS
        BATCH = 1
        SEQLEN = 128
        RMS_EPS = 1e-05
        key = jax.random.key(seed)
        ks = jax.random.split(key, 8)
        x = jax.random.normal(ks[0], (BATCH, SEQLEN, D_MODEL), jnp.float32)
        W_in = jax.random.normal(ks[1], (D_IN_PROJ, D_MODEL), jnp.float32) * 0.02
        conv_w = jax.random.normal(ks[2], (CONV_DIM, D_CONV), jnp.float32) * 0.2
        conv_b = jnp.zeros((CONV_DIM,), jnp.float32)
        dt_bias = jax.random.uniform(ks[3], (NHEADS,), jnp.float32, -6.0, -3.0)
        A_log = jnp.log(1.0 + 15.0 * jax.random.uniform(ks[4], (NHEADS,), jnp.float32))
        D = jnp.ones((NHEADS,), jnp.float32)
        norm_w = jnp.ones((D_INNER,), jnp.float32)
        W_out = jax.random.normal(ks[5], (D_MODEL, D_INNER), jnp.float32) * 0.02
        return {'x': x, 'W_in': W_in, 'conv_w': conv_w, 'conv_b': conv_b, 'dt_bias': dt_bias, 'A_log': A_log, 'D': D, 'norm_w': norm_w, 'W_out': W_out}
    _L1_attn_all = _L1_attn_setup()
    _L1_attn_in = {k: v for k, v in _L1_attn_all.items() if k in ('W_in', 'conv_w', 'conv_b', 'dt_bias', 'A_log', 'D', 'norm_w', 'W_out')}
    del _L1_attn_all

    def _L1_xattn_setup():
        import jax, jax.numpy as jnp
        import numpy as np
        key = jax.random.key(seed)
        k1, k2, k3, k4, k5 = jax.random.split(key, 5)
        B, D_MODEL, L = (2, 128, 256)
        HEAD_DIM = 8
        H = D_MODEL // HEAD_DIM
        return {'k': jax.random.normal(k1, (B, D_MODEL, L), dtype=jnp.float32), 'v': jax.random.normal(k2, (B, D_MODEL, L), dtype=jnp.float32), 'q': jax.random.normal(k3, (B, D_MODEL, L), dtype=jnp.float32), 'ssm_kernel': jax.random.normal(k4, (H, L), dtype=jnp.float32), 'D': jax.random.normal(k5, (H,), dtype=jnp.float32), 'head_dim': HEAD_DIM}
    _L1_xattn_all = _L1_xattn_setup()
    _L1_xattn_in = {k: v for k, v in _L1_xattn_all.items() if k in ('ssm_kernel', 'D')}
    del _L1_xattn_all

    def _L1_ffn_setup():
        import jax, jax.numpy as jnp
        import numpy as np
        TOP_K = 4
        NUM_EXPERTS = 16
        key = jax.random.key(seed)
        ks = jax.random.split(key, 6)
        B, S, H, I, E = (2, 128, 256, 224, NUM_EXPERTS)
        return {'x': jax.random.normal(ks[0], (B, S, H), dtype=jnp.float32), 'router_w': jax.random.normal(ks[1], (E, H), dtype=jnp.float32) * 0.02, 'expert_bias': jnp.zeros((E,), dtype=jnp.float32), 'gate_proj': jax.random.normal(ks[2], (E, H, I), dtype=jnp.float32) * 0.02, 'up_proj': jax.random.normal(ks[3], (E, H, I), dtype=jnp.float32) * 0.02, 'down_proj': jax.random.normal(ks[4], (E, I, H), dtype=jnp.float32) * 0.02}
    _L1_ffn_all = _L1_ffn_setup()
    _L1_ffn_in = {k: v for k, v in _L1_ffn_all.items() if k in ('router_w', 'expert_bias', 'gate_proj', 'up_proj', 'down_proj')}
    del _L1_ffn_all
    return {'x': x, 'ctx_2048': ctx_2048, 'L0_attn_in_proj_w': _L0_attn_in['in_proj_w'], 'L0_attn_conv_w': _L0_attn_in['conv_w'], 'L0_attn_conv_b': _L0_attn_in['conv_b'], 'L0_attn_x_proj_weight': _L0_attn_in['x_proj_weight'], 'L0_attn_dt_proj_weight': _L0_attn_in['dt_proj_weight'], 'L0_attn_dt_proj_bias': _L0_attn_in['dt_proj_bias'], 'L0_attn_A_log': _L0_attn_in['A_log'], 'L0_attn_D': _L0_attn_in['D'], 'L0_attn_out_proj_w': _L0_attn_in['out_proj_w'], 'L0_xattn_time_decay': _L0_xattn_in['time_decay'], 'L0_xattn_time_first': _L0_xattn_in['time_first'], 'L0_ffn_w_cls': _L0_ffn_in['w_cls'], 'L0_ffn_bias': _L0_ffn_in['bias'], 'L0_ffn_w_gate_up': _L0_ffn_in['w_gate_up'], 'L0_ffn_w_down': _L0_ffn_in['w_down'], 'L1_attn_W_in': _L1_attn_in['W_in'], 'L1_attn_conv_w': _L1_attn_in['conv_w'], 'L1_attn_conv_b': _L1_attn_in['conv_b'], 'L1_attn_dt_bias': _L1_attn_in['dt_bias'], 'L1_attn_A_log': _L1_attn_in['A_log'], 'L1_attn_D': _L1_attn_in['D'], 'L1_attn_norm_w': _L1_attn_in['norm_w'], 'L1_attn_W_out': _L1_attn_in['W_out'], 'L1_xattn_ssm_kernel': _L1_xattn_in['ssm_kernel'], 'L1_xattn_D': _L1_xattn_in['D'], 'L1_ffn_router_w': _L1_ffn_in['router_w'], 'L1_ffn_expert_bias': _L1_ffn_in['expert_bias'], 'L1_ffn_gate_proj': _L1_ffn_in['gate_proj'], 'L1_ffn_up_proj': _L1_ffn_in['up_proj'], 'L1_ffn_down_proj': _L1_ffn_in['down_proj']}

def reference(x, ctx_2048, L0_attn_in_proj_w, L0_attn_conv_w, L0_attn_conv_b, L0_attn_x_proj_weight, L0_attn_dt_proj_weight, L0_attn_dt_proj_bias, L0_attn_A_log, L0_attn_D, L0_attn_out_proj_w, L0_xattn_time_decay, L0_xattn_time_first, L0_ffn_w_cls, L0_ffn_bias, L0_ffn_w_gate_up, L0_ffn_w_down, L1_attn_W_in, L1_attn_conv_w, L1_attn_conv_b, L1_attn_dt_bias, L1_attn_A_log, L1_attn_D, L1_attn_norm_w, L1_attn_W_out, L1_xattn_ssm_kernel, L1_xattn_D, L1_ffn_router_w, L1_ffn_expert_bias, L1_ffn_gate_proj, L1_ffn_up_proj, L1_ffn_down_proj):
    import jax
    import jax.numpy as jnp

    def _L0_attn_ref(hidden_states, in_proj_w, conv_w, conv_b, x_proj_weight, dt_proj_weight, dt_proj_bias, A_log, D, out_proj_w):
        import jax, jax.numpy as jnp
        import numpy as np
        from jax import lax
        B, S, H = (2, 256, 256)
        EXPAND, N, K, R, NH = (2, 16, 4, 128, 2)
        I = EXPAND * H
        HD = I // NH

        def _mixer(hidden_states, in_proj_w, conv_w, conv_b, x_proj_weight, dt_proj_weight, dt_proj_bias, A_log, D, out_proj_w):
            b, s, _ = hidden_states.shape
            proj = jnp.einsum('bsh,oh->bos', hidden_states, in_proj_w)
            proj = proj.reshape(b, I, 2, s)
            x = proj[:, :, 0, :]
            gate = proj[:, :, 1, :].reshape(b, NH, HD, s).transpose(1, 0, 2, 3)
            xp = jnp.pad(x, ((0, 0), (0, 0), (K - 1, 0)))
            conv = lax.conv_general_dilated(xp, conv_w[:, None, :], window_strides=(1,), padding='VALID', dimension_numbers=('NCH', 'OIH', 'NCH'), feature_group_count=I)
            x = jax.nn.silu(conv + conv_b[None, :, None])
            x = x.reshape(b, NH, HD, s).transpose(1, 0, 2, 3)
            ssm_p = jnp.einsum('hrd,hbds->hbsr', x_proj_weight, x)
            dt_in, Bm, Cm = jnp.split(ssm_p, [R, R + N], axis=-1)
            dt = jnp.einsum('hdr,hbsr->hbds', dt_proj_weight, dt_in) + dt_proj_bias[:, None, :, None]
            dt = jax.nn.softplus(dt)
            A = -jnp.exp(A_log)

            def step(state, inp):
                dt_t, B_t, C_t, x_t = inp
                dA = jnp.exp(A[:, None, :, :] * dt_t[..., None])
                dBu = dt_t[..., None] * B_t[:, :, None, :] * x_t[..., None]
                state = dA * state + dBu
                y = jnp.einsum('hbdn,hbn->hbd', state, C_t)
                return (state, y)
            init = jnp.zeros((NH, b, HD, N), dtype=x.dtype)
            xs = (dt.transpose(3, 0, 1, 2), Bm.transpose(2, 0, 1, 3), Cm.transpose(2, 0, 1, 3), x.transpose(3, 0, 1, 2))
            _, ys = lax.scan(step, init, xs)
            y = ys.transpose(1, 2, 3, 0)
            y = y + x * D[:, None, :, None]
            y = y * jax.nn.silu(gate)
            y = y.transpose(1, 0, 2, 3).reshape(b, I, s).transpose(0, 2, 1)
            return jnp.einsum('bsi,hi->bsh', y, out_proj_w)
        return _mixer(hidden_states, in_proj_w, conv_w, conv_b, x_proj_weight, dt_proj_weight, dt_proj_bias, A_log, D, out_proj_w)

    def _L0_xattn_ref(batch_size, seq_len, embedding_dim, time_decay, time_first, k, v):
        import jax, jax.numpy as jnp
        import numpy as np

        def _wkv(time_decay, time_first, k, v):
            w = -jnp.exp(time_decay)
            u = time_first
            B, T, C = k.shape
            aa = jnp.zeros((B, C), dtype=k.dtype)
            bb = jnp.zeros((B, C), dtype=k.dtype)
            pp = jnp.full((B, C), -1e+38, dtype=k.dtype)

            def step(carry, kv_t):
                aa, bb, pp = carry
                kt, vt = kv_t
                ww = u + kt
                q = jnp.maximum(pp, ww)
                e1 = jnp.exp(pp - q)
                e2 = jnp.exp(ww - q)
                y_t = (e1 * aa + e2 * vt) / (e1 * bb + e2)
                ww2 = pp + w
                q2 = jnp.maximum(ww2, kt)
                e1b = jnp.exp(ww2 - q2)
                e2b = jnp.exp(kt - q2)
                new_carry = (e1b * aa + e2b * vt, e1b * bb + e2b, q2)
                return (new_carry, y_t)
            ks = jnp.transpose(k, (1, 0, 2))
            vs = jnp.transpose(v, (1, 0, 2))
            _, ys = jax.lax.scan(step, (aa, bb, pp), (ks, vs))
            return jnp.transpose(ys, (1, 0, 2))
        assert seq_len <= 128
        return _wkv(time_decay, time_first, k, v)

    def _L0_ffn_ref(x, w_cls, bias, w_gate_up, w_down):
        import jax, jax.numpy as jnp
        import numpy as np
        B, S, H = (2, 128, 256)
        I = 128
        E = 32
        Z = 32
        K = 8
        SCALE = 1.5
        CAP = 128
        EPS = 1e-20

        def _moe_forward(x, w_cls, bias, w_gate_up, w_down):
            T = x.shape[0] * x.shape[1]
            xf = x.reshape(T, H)
            logits = xf.astype(jnp.float32) @ w_cls.T
            scores = jax.nn.softmax(logits, axis=-1)
            _, topk_idx = jax.lax.top_k(scores + bias[None, :], K)
            w = jnp.take_along_axis(scores, topk_idx, axis=-1)
            w = w / (w.sum(-1, keepdims=True) + EPS) * SCALE
            routed = topk_idx < E
            w_r = jnp.where(routed, w, 0.0)
            w_z = jnp.where(routed, 0.0, w)
            N = T * K
            flat_ids = jnp.where(routed, topk_idx, E).reshape(-1)
            x_exp = jnp.repeat(xf, K, axis=0)
            order = jnp.argsort(flat_ids)
            ids_s = flat_ids[order]
            counts = jax.ops.segment_sum(jnp.ones(N, jnp.int32), flat_ids, num_segments=E + 1)
            starts = jnp.cumsum(counts) - counts
            pos = jnp.arange(N) - starts[ids_s]
            buf = jnp.zeros((E, CAP, H), xf.dtype).at[ids_s, pos].set(x_exp[order], mode='drop')
            gu = jnp.einsum('ech,ehf->ecf', buf, w_gate_up)
            g, u = jnp.split(gu, 2, axis=-1)
            act = jax.nn.silu(g) * u
            y = jnp.einsum('eci,eih->ech', act, w_down)
            valid = (ids_s < E) & (pos < CAP)
            y_tok = jnp.where(valid[:, None], y[jnp.clip(ids_s, 0, E - 1), jnp.clip(pos, 0, CAP - 1)], 0.0)
            y_exp = jnp.zeros((N, H), xf.dtype).at[order].set(y_tok).reshape(T, K, H)
            routed_out = jnp.einsum('tk,tkh->th', w_r, y_exp)
            out = routed_out * (1.0 + w_z.sum(-1, keepdims=True))
            return out.reshape(x.shape)
        return _moe_forward(x, w_cls, bias, w_gate_up, w_down)

    def _L1_attn_ref(x, W_in, conv_w, conv_b, dt_bias, A_log, D, norm_w, W_out):
        import jax, jax.numpy as jnp
        import numpy as np
        D_MODEL = 256
        EXPAND = 2
        HEADDIM = 64
        D_STATE = 64
        D_CONV = 4
        D_INNER = EXPAND * D_MODEL
        NHEADS = D_INNER // HEADDIM
        NGROUPS = 1
        CONV_DIM = D_INNER + 2 * NGROUPS * D_STATE
        D_IN_PROJ = 2 * D_INNER + 2 * NGROUPS * D_STATE + NHEADS
        BATCH = 1
        SEQLEN = 128
        RMS_EPS = 1e-05
        B, T, _ = x.shape
        zxbcdt = jnp.einsum('btd,pd->btp', x, W_in)
        z = zxbcdt[..., :D_INNER]
        xBC = zxbcdt[..., D_INNER:D_INNER + CONV_DIM]
        dt = jax.nn.softplus(zxbcdt[..., D_INNER + CONV_DIM:] + dt_bias)
        xp = jnp.pad(xBC, ((0, 0), (D_CONV - 1, 0), (0, 0)))
        conv = conv_b + sum((xp[:, k:k + T, :] * conv_w[:, k] for k in range(D_CONV)))
        xBC = jax.nn.silu(conv)
        xh = xBC[..., :D_INNER].reshape(B, T, NHEADS, HEADDIM)
        Bm = xBC[..., D_INNER:D_INNER + D_STATE]
        Cm = xBC[..., D_INNER + D_STATE:]
        A = -jnp.exp(A_log)
        dA = jnp.exp(dt * A)

        def step(h, inp):
            dA_t, dt_t, B_t, x_t, C_t = inp
            h = h * dA_t[:, :, None, None] + jnp.einsum('bh,bn,bhp->bhpn', dt_t, B_t, x_t)
            y_t = jnp.einsum('bhpn,bn->bhp', h, C_t)
            return (h, y_t)
        h0 = jnp.zeros((B, NHEADS, HEADDIM, D_STATE), x.dtype)
        xs = (dA.transpose(1, 0, 2), dt.transpose(1, 0, 2), Bm.transpose(1, 0, 2), xh.transpose(1, 0, 2, 3), Cm.transpose(1, 0, 2))
        _, ys = jax.lax.scan(step, h0, xs)
        y = ys.transpose(1, 0, 2, 3) + D[None, None, :, None] * xh
        y = y.reshape(B, T, D_INNER)
        y = y * jax.nn.silu(z)
        y = y * jax.lax.rsqrt(jnp.mean(y * y, axis=-1, keepdims=True) + RMS_EPS) * norm_w
        return jnp.einsum('bti,di->btd', y, W_out)

    def _L1_xattn_ref(k, v, q, ssm_kernel, D, head_dim):
        import jax, jax.numpy as jnp
        import numpy as np
        B, HD, L = k.shape
        H = HD // head_dim
        fft_size = 2 * L
        k_ = k.reshape(B, H, head_dim, L)
        v_ = v.reshape(B, H, head_dim, L)
        q_ = q.reshape(B, H, head_dim, L)
        kv = jnp.einsum('bhil,bhjl->bijhl', k_, v_)
        kv_f = jnp.fft.rfft(kv, n=fft_size)
        kernel_f = jnp.fft.rfft(ssm_kernel, n=fft_size)
        y = jnp.fft.irfft(kv_f * kernel_f, n=fft_size)[..., :L]
        out = y + kv * D[None, None, None, :, None]
        out = jnp.einsum('bijhl,bhil->bjhl', out, q_)
        out = jnp.transpose(out, (0, 2, 1, 3)).reshape(B, H * head_dim, L)
        return out.astype(k.dtype)

    def _L1_ffn_ref(x, router_w, expert_bias, gate_proj, up_proj, down_proj):
        import jax, jax.numpy as jnp
        import numpy as np
        TOP_K = 4
        NUM_EXPERTS = 16
        logits = jnp.einsum('bsh,eh->bse', x, router_w) + expert_bias
        scores = jax.nn.softmax(logits, axis=-1)
        top_w, top_idx = jax.lax.top_k(scores, TOP_K)
        top_w = top_w / jnp.sum(top_w, axis=-1, keepdims=True)
        g = jnp.einsum('bsh,khe->bske', x, gate_proj)
        u = jnp.einsum('bsh,khe->bske', x, up_proj)
        act = jax.nn.silu(g) * u
        out = jnp.einsum('bske,keh->bskh', act, down_proj)
        sel = jnp.take_along_axis(out, top_idx[..., None], axis=2)
        return jnp.sum(sel * top_w[..., None], axis=2)
    x = x + _L0_attn_ref(_layernorm(x, axis=-1), L0_attn_in_proj_w, L0_attn_conv_w, L0_attn_conv_b, L0_attn_x_proj_weight, L0_attn_dt_proj_weight, L0_attn_dt_proj_bias, L0_attn_A_log, L0_attn_D, L0_attn_out_proj_w)
    x = x + _L0_xattn_ref(16, 128, 256, L0_xattn_time_decay, L0_xattn_time_first, _layernorm(x, axis=-1), ctx_2048)
    x = x + _L0_ffn_ref(_layernorm(x, axis=-1), L0_ffn_w_cls, L0_ffn_bias, L0_ffn_w_gate_up, L0_ffn_w_down)
    x = x + _L1_attn_ref(_layernorm(x, axis=-1), L1_attn_W_in, L1_attn_conv_w, L1_attn_conv_b, L1_attn_dt_bias, L1_attn_A_log, L1_attn_D, L1_attn_norm_w, L1_attn_W_out)
    x = x + _L1_xattn_ref(ctx_2048, ctx_2048, _layernorm(x, axis=-1), L1_xattn_ssm_kernel, L1_xattn_D, 8)
    x = x + _L1_ffn_ref(_layernorm(x, axis=-1), L1_ffn_router_w, L1_ffn_expert_bias, L1_ffn_gate_proj, L1_ffn_up_proj, L1_ffn_down_proj)
    return x

_drawn_inputs = setup_inputs


def setup_inputs(seed=0):
    import zlib

    import numpy as np

    out = dict(_drawn_inputs(seed))
    spreads = {'L0_attn_D': (1.0, 0.2),
     'L1_attn_conv_b': (0.0, 0.1),
     'L1_attn_D': (1.0, 0.2),
     'L1_attn_norm_w': (1.0, 0.2),
     'L1_ffn_expert_bias': (0.0, 0.8)}
    factors = {'L0_attn_conv_b': 2.982,
     'L0_attn_dt_proj_bias': 6.788,
     'L0_ffn_w_cls': 8.0,
     'L0_ffn_bias': 8.0,
     'L0_ffn_w_gate_up': 8.0,
     'L0_ffn_w_down': 8.0,
     'L1_attn_dt_bias': 8.0,
     'L1_attn_A_log': 8.0,
     'L1_ffn_router_w': 8.0,
     'L1_ffn_gate_proj': 8.0,
     'L1_ffn_up_proj': 8.0,
     'L1_ffn_down_proj': 8.0}
    for name, (base, spread) in spreads.items():
        noise = np.random.default_rng([zlib.crc32(name.encode()), seed]).standard_normal(out[name].shape)
        drawn = base * np.exp(spread * noise) if base else spread * noise
        out[name] = jnp.asarray(drawn.astype(out[name].dtype))
    for name, factor in factors.items():
        out[name] = (out[name] * factor).astype(out[name].dtype)
    return out
```

```python
from contextlib import ExitStack

import concourse.bass as bass
from concourse import mybir

F32 = mybir.dt.float32
BF16 = mybir.dt.bfloat16
U8 = mybir.dt.uint8
ALU = mybir.AluOpType
ACT = mybir.ActivationFunctionType
AX = mybir.AxisListType

P = 128
NB = 16
T = 128
D = 256
KT = D // P
NT = NB * T
TP = T + 1
BANK = 512
NBANK = 8
CH = NT // BANK
BPC = BANK // T
LN_EPS = 1e-5
BIG = 1.0e25

INNER = 512
MT = INNER // P
HEADS0 = 2
MH = MT // HEADS0
NS = 16
RANK = 128
TAPS = 4
HALF = NT // 2
BC = 2 * NS



class Chain:

    def __init__(self, eng, sem):
        self.eng, self.sem, self.n = eng, sem, 0

    def __call__(self, ins):
        ins.then_inc(self.sem, 1)
        self.n += 1
        self.eng.wait_ge(self.sem, self.n)


class Arena:

    def __init__(self, tensor):
        self.tensor, self.at = tensor, 0

    def take(self, words):
        self.at += words
        assert self.at <= self.tensor.shape[1], self.at
        return self.tensor[:, self.at - words:self.at]


def dma_all(eng, pairs, sem):
    for dst, src in pairs:
        eng.dma_start(dst, src).then_inc(sem, 16)
    return 16 * len(pairs)


def norm_stage(nc, ps, ident, x_tok, xn_tok, xn_cols, small, tag):
    with ExitStack() as ctx:
        sem = lambda n: ctx.enter_context(nc.semaphore(f"{n}_{tag}"))
        stats_done, std_done, xn_done, xt_done, xt_copied = map(sem, ("stats", "std", "xn", "xt", "xtc"))
        dve_own = sem("dve_own_ln")
        stats = small[:, 0:NB * 6].rearrange("p (b s) -> p b s", s=6)
        mv = small[:, 96:96 + NB * 2].rearrange("p (b s) -> p b s", s=2)
        std = small[:, 128:128 + NB]
        rstd = small[:, 144:144 + NB]
        eps = small[:, 160:161]
        block = ctx.enter_context(nc.Block())

        @block.vector
        def _(dve):
            chain = Chain(dve, dve_own)
            nc.vector.memset(eps, LN_EPS).then_inc(stats_done, 1)
            for b in range(NB):
                ins = nc.vector.bn_stats(stats[:, b, :], x_tok[:, b, :])
            chain(ins)
            for b in range(NB):
                ins = nc.vector.bn_aggr(mv[:, b, :], stats[:, b, :])
            ins.then_inc(stats_done, 1)
            dve.wait_ge(std_done, 1)
            chain(nc.vector.reciprocal(rstd, std))
            for b in range(NB):
                nc.vector.tensor_scalar(xn_tok[:, b, :], x_tok[:, b, :], mv[:, b, 0:1], rstd[:, b:b + 1],
                                        ALU.subtract, ALU.mult).then_inc(xn_done, 1)

        @block.scalar
        def _(act):
            act.wait_ge(stats_done, 2)
            nc.scalar.activation(std, mv[:, :, 1], ACT.Sqrt, bias=eps).then_inc(std_done, 1)
            for c in range(CH):
                for k in range(KT):
                    act.wait_ge(xt_done, c * KT + k + 1)
                    nc.scalar.activation(xn_cols(k, c), ps[:, c * KT + k, :].rearrange("p (b t) -> p b t", t=T),
                                         ACT.Copy).then_inc(xt_copied, 1)

        @block.tensor
        def _(pe):
            for c in range(CH):
                pe.wait_ge(xn_done, (c + 1) * BPC)
                for k in range(KT):
                    for j in range(BPC):
                        ins = nc.tensor.transpose(ps[:, c * KT + k, j * T:(j + 1) * T],
                                                  xn_tok[:, c * BPC + j, k * P:(k + 1) * P], ident)
                    ins.then_inc(xt_done, 1)


def add_transposed_stage(nc, ps, ident, x_tok, y_cols, tag):
    with ExitStack() as ctx:
        turned = ctx.enter_context(nc.semaphore(f"turned_{tag}"))
        added = ctx.enter_context(nc.semaphore(f"added_{tag}"))
        block = ctx.enter_context(nc.Block())

        @block.tensor
        def _(pe):
            for b in range(NB):
                for k in range(KT):
                    ins = nc.tensor.transpose(ps[:, b // 2, (b % 2) * D + k * P:(b % 2) * D + (k + 1) * P],
                                              y_cols(k, b), ident)
                if b % 2:
                    ins.then_inc(turned, 1)

        @block.vector
        def _(dve):
            for g in range(NB // 2):
                dve.wait_ge(turned, g + 1)
                xs = x_tok[:, 2 * g:2 * g + 2, :].rearrange("p b d -> p (b d)")
                nc.vector.tensor_tensor(xs, ps[:, g, :], xs, ALU.add).then_inc(added, 1)


def conv_stage(nc, ps, xn_t, w_in, nx, put_x, ng, put_gate, cw, cb, pre, acc, tag):
    with ExitStack() as ctx:
        sem = lambda n: ctx.enter_context(nc.semaphore(f"{n}_{tag}"))
        proj_done, pre_copied, gate_done, conv_done, xs_done, pads_zero = map(
            sem, ("proj_done", "pre_copied", "gate_done", "conv_done", "xs_done", "pads_zero"))
        block = ctx.enter_context(nc.Block())

        @block.tensor
        def _(pe):
            for m in range(nx + ng):
                for c in range(CH):
                    if m >= 2:
                        n = (m - 2) * CH + c + 1
                        if m - 2 < nx:
                            pe.wait_ge(pre_copied, n)
                        else:
                            pe.wait_ge(gate_done, n - nx * CH)
                    for k in range(KT):
                        ins = nc.tensor.matmul(ps[:, (m % 2) * CH + c, :], w_in[:, k, m * P:(m + 1) * P],
                                               xn_t[:, k, c * BANK:(c + 1) * BANK],
                                               start=(k == 0), stop=(k == KT - 1))
                    ins.then_inc(proj_done, 1)

        @block.scalar
        def _(act):
            act.wait_ge(pads_zero, 2)

            def take_x(m):
                for c in range(CH):
                    act.wait_ge(proj_done, m * CH + c + 1)
                    bank = ps[:, (m % 2) * CH + c, :]
                    nc.scalar.activation(pre[m % 2][:, c * BPC:(c + 1) * BPC, TAPS - 1:],
                                         bank.rearrange("p (b t) -> p b t", t=T), ACT.Copy)
                    nc.scalar.activation(acc[m % 2][:, c * BANK:(c + 1) * BANK], bank, ACT.Identity,
                                         scale=cw[:, m, TAPS - 1:TAPS], bias=cb[:, m:m + 1])\
                        .then_inc(pre_copied, 1)

            def silu_x(m):
                act.wait_ge(conv_done, (TAPS - 1) * (m + 1))
                for dst, src in put_x(m):
                    ins = nc.scalar.activation(dst, src, ACT.Silu)
                ins.then_inc(xs_done, 1)

            def take_gate(m):
                for c in range(CH):
                    act.wait_ge(proj_done, (nx + m) * CH + c + 1)
                    nc.scalar.activation(put_gate(m, c), ps[:, ((nx + m) % 2) * CH + c, :], ACT.Silu)\
                        .then_inc(gate_done, 1)

            take_x(0)
            take_x(1)
            for m in range(2, nx):
                silu_x(m - 2)
                act.wait_ge(xs_done, m - 1)
                take_x(m)
            if ng:
                take_gate(0)
            silu_x(nx - 2)
            if ng:
                take_gate(1)
            silu_x(nx - 1)
            for m in range(2, ng):
                take_gate(m)

        @block.vector
        def _(dve):
            for q in range(2):
                nc.vector.memset(pre[q][:, :, 0:TAPS - 1], 0.0).then_inc(pads_zero, 1)
            for m in range(nx):
                dve.wait_ge(pre_copied, (m + 1) * CH)
                a3 = acc[m % 2].rearrange("p (b t) -> p b t", t=T)
                for k in range(TAPS - 1):
                    nc.vector.scalar_tensor_tensor(out=a3, in0=pre[m % 2][:, :, k:k + T],
                                                   scalar=cw[:, m, k:k + 1], in1=a3,
                                                   op0=ALU.mult, op1=ALU.add).then_inc(conv_done, 1)
                    dve.wait_ge(conv_done, m * (TAPS - 1) + k + 1)


def scan_layer(nc, ps, ident, arena_at, x_tok, small, w):
    A = Arena(arena_at.tensor)
    A.at = arena_at.at
    big = [A.take(MT * NT) for _ in range(4)]
    xs, gate, dt, u = (r.rearrange("p (i m t) -> p i m t", i=4, m=MH) for r in big)
    xn_tok = big[2][:, 0:NB * D].rearrange("p (b d) -> p b d", d=D)
    xn_t = big[3][:, 0:KT * NT].rearrange("p (k t) -> p k t", k=KT)
    dt_in = big[3][:, KT * NT:KT * NT + HEADS0 * NT].rearrange("p (h t) -> p h t", h=HEADS0)
    bc3 = A.take(HEADS0 * NT // 2).bitcast(BF16).rearrange("p (i t) -> p i t", i=4)
    a4 = A.take(4 * MH * NS).rearrange("p (i n) -> p i n", i=4)
    d4 = A.take(4 * MH).rearrange("p (i m) -> p i m", i=4)
    wo = A.take(MT * D).rearrange("p (m d) -> p m d", m=MT)
    temp0 = A.at
    w_in = A.take(KT * 2 * INNER).rearrange("p (k o) -> p k o", k=KT)
    cw = A.take(MT * TAPS).rearrange("p (m k) -> p m k", k=TAPS)
    cb = A.take(MT)
    wx = A.take(MT * RANK).rearrange("p (m r) -> p m r", m=MT)
    wbc = A.take(MT * 3 * BC).rearrange("p (m r) -> p m r", m=MT)
    wdt = A.take(INNER).rearrange("p (m d) -> p m d", m=MT)
    dtb = A.take(MT)
    pre = [A.take(NB * (T + TAPS - 1)).rearrange("p (b t) -> p b t", b=NB) for _ in range(2)]
    acc = [A.take(NT) for _ in range(2)]
    r1 = pre[0].rearrange("p b t -> p (b t)")[:, 0:2 * BANK].rearrange("p (j t) -> p j t", j=2)
    half16 = pre[0].rearrange("p b t -> p (b t)")[:, 2 * BANK:2 * BANK + BANK].bitcast(BF16)\
        .rearrange("p (j t) -> p j t", j=2)

    with ExitStack() as ctx:
        sem = lambda n: ctx.enter_context(nc.semaphore(n))
        w_here = sem("l0_weights")
        wsrc = [(w_in, w["in_proj"]), (cw, w["conv_w"]), (cb, w["conv_b"]), (wx, w["x_dt"]),
                (wdt, w["dt_proj"]), (dtb, w["dt_bias"]), (wo, w["out_proj"])]
        wsrc += [(wbc[:, :, j * BC:(j + 1) * BC], w["x_bc"]) for j in range(3)]
        wsrc += [(a4[:, j::2, :], w["a_log"]) for j in range(2)] + [(d4[:, j::2, :], w["d"]) for j in range(2)]
        with nc.Block() as block:
            @block.sync
            def _(sp):
                n = dma_all(sp, wsrc, w_here)
                sp.wait_ge(w_here, n)
        norm_stage(nc, ps, ident, x_tok, xn_tok,
                   lambda k, c: xn_t[:, k, c * BANK:(c + 1) * BANK].rearrange("p (b t) -> p b t", t=T),
                   small, "scan")

        def put_x(m):
            return [(xs[:, m // MH * 2:m // MH * 2 + 2, m % MH, :], acc[m % 2].rearrange("p (h t) -> p h t", h=2))]

        def put_gate(m, c):
            return gate[:, m // MH * 2 + c // 2, m % MH, (c % 2) * BANK:(c % 2 + 1) * BANK]

        conv_stage(nc, ps, xn_t, w_in, MT, put_x, MT, put_gate, cw, cb, pre, acc, "m0")

        xp_done, xp_copied, bc_split, dtp_done, pre_done, e_done, one_e, ln_done, dt_done, u_done = map(
            sem, ("xp_done", "xp_copied", "bc_split", "dtp_done", "dtpre_done", "e_done", "one_e", "ln_done",
                  "dt_done", "u_done"))
        dve_own = sem("dve_own_proj")
        act_own = sem("act_own_proj")

        def dtp(m, c):
            return dt[:, m // MH * 2 + c // 2, m % MH, (c % 2) * BANK:(c % 2 + 1) * BANK]

        def rows(t4, m):
            return t4[:, m // MH * 2:m // MH * 2 + 2, m % MH, :]

        with nc.Block() as block:
            @block.tensor
            def _(pe):
                for j in range(HEADS0 * CH):
                    h, c = divmod(j, CH)
                    if j >= 2:
                        pe.wait_ge(xp_copied, j - 1)
                    for k in range(MH):
                        x_in = xs[:, h * 2 + c // 2, k, (c % 2) * BANK:(c % 2 + 1) * BANK]
                        nc.tensor.matmul(ps[:, j % 2, :], wx[:, h * MH + k, :], x_in,
                                         start=(k == 0), stop=(k == MH - 1))
                    if j >= 2:
                        pe.wait_ge(bc_split, j - 1)
                    for k in range(MH):
                        x_in = xs[:, h * 2 + c // 2, k, (c % 2) * BANK:(c % 2 + 1) * BANK]
                        ins = nc.tensor.matmul(ps[0:3 * BC, 2 + j % 2, :], wbc[:, h * MH + k, :], x_in,
                                               start=(k == 0), stop=(k == MH - 1))
                    ins.then_inc(xp_done, 1)
                for m in range(MT):
                    pe.wait_ge(xp_copied, (m // MH + 1) * CH)
                    for c in range(CH):
                        if m >= 1:
                            pe.wait_ge(pre_done, (m - 1) * CH + c + 1)
                        nc.tensor.matmul(ps[:, 4 + c, :], wdt[:, m, :], dt_in[:, m // MH, c * BANK:(c + 1) * BANK],
                                         start=True, stop=True).then_inc(dtp_done, 1)

            @block.scalar
            def _(act):
                own = Chain(act, act_own)
                rates = a4.rearrange("p i n -> p (i n)")
                own(nc.scalar.activation(rates, rates, ACT.Exp))
                own(nc.scalar.mul(rates, rates, -1.0))
                for j in range(HEADS0 * CH):
                    act.wait_ge(xp_done, j + 1)
                    nc.scalar.activation(dt_in[:, j // CH, (j % CH) * BANK:(j % CH + 1) * BANK], ps[:, j % 2, :],
                                         ACT.Copy).then_inc(xp_copied, 1)
                for m in range(MT):
                    for c in range(CH):
                        act.wait_ge(dtp_done, m * CH + c + 1)
                        nc.scalar.activation(dtp(m, c), ps[:, 4 + c, :], ACT.Identity, bias=dtb[:, m:m + 1])\
                            .then_inc(pre_done, 1)
                    if m >= 1:
                        act.wait_ge(dt_done, m)
                    act.wait_ge(pre_done, (m + 1) * CH)
                    e = acc[0].rearrange("p (h t) -> p h t", h=2)
                    own(nc.scalar.activation(e, rows(dt, m), ACT.Abs))
                    nc.scalar.activation(acc[0], acc[0], ACT.Exp, scale=-1.0).then_inc(e_done, 1)
                    act.wait_ge(one_e, m + 1)
                    nc.scalar.activation(pre[1].rearrange("p b t -> p (b t)")[:, 0:NT], acc[1], ACT.Ln)\
                        .then_inc(ln_done, 1)

            @block.vector
            def _(dve):
                own = Chain(dve, dve_own)
                for j in range(HEADS0 * CH):
                    h, c = divmod(j, CH)
                    dve.wait_ge(xp_done, j + 1)
                    bank = ps[0:3 * BC, 2 + j % 2, :]
                    out = bc3[:, h * 2 + c // 2, (c % 2) * BANK:(c % 2 + 1) * BANK]
                    r, s = r1[:, j % 2, :], half16[:, j % 2, :]
                    own(nc.vector.tensor_copy(out[0:3 * BC], bank))
                    nc.vector.tensor_tensor(r[0:3 * BC], bank, out[0:3 * BC], ALU.subtract).then_inc(bc_split, 1)
                    dve.wait_ge(bc_split, j + 1)
                    own(nc.vector.tensor_copy(out[BC:2 * BC], r[BC:2 * BC]))
                    own(nc.vector.tensor_copy(s[2 * BC:3 * BC], r[2 * BC:3 * BC]))
                    own(nc.vector.tensor_tensor(out[2 * BC:3 * BC], r[2 * BC:3 * BC], s[2 * BC:3 * BC],
                                                ALU.subtract))
                ln = pre[1].rearrange("p b t -> p (b t)")[:, 0:NT]
                for m in range(MT):
                    dve.wait_ge(e_done, m + 1)
                    nc.vector.tensor_scalar(acc[1], acc[0], 1.0, None, ALU.add).then_inc(one_e, 1)
                    dve.wait_ge(one_e, m + 1)
                    own(nc.vector.scalar_tensor_tensor(out=acc[0], in0=acc[1], scalar=1.0, in1=acc[0],
                                                       op0=ALU.subtract, op1=ALU.subtract))
                    dve.wait_ge(ln_done, m + 1)
                    own(nc.vector.tensor_tensor(ln, ln, acc[0], ALU.subtract))
                    nc.vector.scalar_tensor_tensor(out=rows(dt, m), in0=rows(dt, m), scalar=0.0,
                                                   in1=ln.rearrange("p (h t) -> p h t", h=2),
                                                   op0=ALU.max, op1=ALU.add).then_inc(dt_done, 1)
                    dve.wait_ge(dt_done, m + 1)
                    if m >= MH:
                        dve.wait_ge(dtp_done, MT * CH)
                    own(nc.vector.tensor_tensor(rows(u, m), rows(dt, m), rows(xs, m), ALU.mult))
                    nc.vector.memset(rows(dt, m).rearrange("p h (b t) -> p h b t", t=T)[:, :, :, 0:1], BIG)\
                        .then_inc(u_done, 1)

        A.at = temp0
        sel = A.take(BC * P // 2).bitcast(BF16).rearrange("p (n q) -> p n q", q=P)
        decay = A.take(2 * MH * HALF).rearrange("p (q m t) -> p q m t", q=2, m=MH)
        state = A.take(MH * HALF).rearrange("p (m t) -> p m t", m=MH)
        hc = A.take(2 * MH * HALF).rearrange("p (q m t) -> p q m t", q=2, m=MH)
        sel_here = sem("sel_here")
        with nc.Block() as block:
            @block.sync
            def _(sp):
                sp.dma_start(sel, w["sel"]).then_inc(sel_here, 16)
                sp.wait_ge(sel_here, 16)
        b_done, c_done, y_done, decay_done, ub_done, scan_done, hc_done, y_taken = map(
            sem, ("b_done", "c_done", "y_done", "decay_done", "ub_done", "scan_done", "hc_done", "y_taken"))
        b_ps = ps[:, 0:2, :].rearrange("p a t -> p (a t)")
        c_ps = ps[:, 2:4, :].rearrange("p a t -> p (a t)")
        STEPS = NS * MH
        with nc.Block() as block:
            @block.tensor
            def _(pe):
                pe.sem_inc(y_done, 1)
                with pe.Fori(0, 4) as i:
                    def broadcast(n, row, bank, done):
                        for a in range(2):
                            ins = nc.tensor.matmul(ps[:, bank + a, :], sel[0:3 * BC, row, :],
                                                   bc3[0:3 * BC, bass.ds(i, 1), a * BANK:(a + 1) * BANK]
                                                   .rearrange("p i t -> p (i t)"), start=True, stop=True)
                        ins.then_inc(done, 1)

                    def sum_states(n):
                        for m in range(MH):
                            pe.wait_ge(hc_done, 1 + i * STEPS + n * MH + m + 1)
                            if n == 0:
                                pe.wait_ge(y_taken, 1 + i * 4)
                            for a in range(2):
                                ins = nc.tensor.matmul(ps[:, 4 + 2 * m + a, :], ident,
                                                       hc[:, n % 2, m, a * BANK:(a + 1) * BANK],
                                                       start=(n == 0), stop=(n == NS - 1))
                            ins.then_inc(y_done, 1)

                    for n in range(NS):
                        pe.wait_ge(ub_done, 1 + i * STEPS + n * MH)
                        broadcast(n, n, 0, b_done)
                        pe.wait_ge(hc_done, 1 + i * STEPS + n * MH)
                        broadcast(n, NS + n, 2, c_done)
                        if n:
                            sum_states(n - 1)
                    sum_states(NS - 1)

            @block.scalar
            def _(act):
                with act.Fori(0, 4) as i:
                    for n in range(NS):
                        for m in range(MH):
                            if n >= 2:
                                act.wait_ge(scan_done, 1 + i * STEPS + (n - 2) * MH + m + 1)
                            else:
                                act.wait_ge(scan_done, 1 + i * STEPS)
                            nc.scalar.activation(decay[:, n % 2, m, :],
                                                 dt[:, bass.ds(i, 1), m, :].rearrange("p i t -> p (i t)"), ACT.Exp,
                                                 scale=a4[:, bass.ds(i, 1), m * NS + n:m * NS + n + 1]
                                                 .rearrange("p i t -> p (i t)")).then_inc(decay_done, 1)

            @block.vector
            def _(dve):
                for first in (ub_done, scan_done, hc_done, y_taken):
                    dve.sem_inc(first, 1)
                with dve.Fori(0, 4) as i:
                    for n in range(NS):
                        dve.wait_ge(b_done, i * NS + n + 1)
                        for m in range(MH):
                            dve.wait_ge(hc_done, 1 + i * STEPS + (max(n * MH - MH + m + 1, 0) if n else 0))
                            nc.vector.tensor_tensor(state[:, m, :], u[:, bass.ds(i, 1), m, :]
                                                    .rearrange("p i t -> p (i t)"), b_ps, ALU.mult)\
                                .then_inc(ub_done, 1)
                        for m in range(MH):
                            dve.wait_ge(ub_done, 1 + i * STEPS + n * MH + m + 1)
                            dve.wait_ge(decay_done, i * STEPS + n * MH + m + 1)
                            nc.vector.tensor_tensor_scan(state[:, m, :], decay[:, n % 2, m, :], state[:, m, :],
                                                         0.0, ALU.mult, ALU.add).then_inc(scan_done, 1)
                        dve.wait_ge(c_done, i * NS + n + 1)
                        for m in range(MH):
                            dve.wait_ge(scan_done, 1 + i * STEPS + n * MH + m + 1)
                            if n >= 2:
                                dve.wait_ge(y_done, 1 + i * STEPS + (n - 2) * MH + m + 1)
                            else:
                                dve.wait_ge(y_done, 1 + i * STEPS)
                            nc.vector.tensor_tensor(hc[:, n % 2, m, :], state[:, m, :], c_ps, ALU.mult)\
                                .then_inc(hc_done, 1)
                    for m in range(MH):
                        dve.wait_ge(y_done, 1 + i * STEPS + STEPS - MH + m + 1)
                        xr = xs[:, bass.ds(i, 1), m, :].rearrange("p i t -> p (i t)")
                        gr = gate[:, bass.ds(i, 1), m, :].rearrange("p i t -> p (i t)")
                        nc.vector.scalar_tensor_tensor(out=xr, in0=xr, scalar=d4[:, bass.ds(i, 1), m:m + 1]
                                                       .rearrange("p i t -> p (i t)"),
                                                       in1=ps[:, 4 + 2 * m:6 + 2 * m, :].rearrange("p a t -> p (a t)"),
                                                       op0=ALU.mult, op1=ALU.add).then_inc(y_taken, 1)
                        dve.wait_ge(y_taken, 1 + i * 4 + 2 * m + 1)
                        nc.vector.tensor_tensor(gr, gr, xr, ALU.mult).then_inc(y_taken, 1)

        out_done, out_added = sem("out0_done"), sem("out0_added")
        with nc.Block() as block:
            @block.tensor
            def _(pe):
                for b in range(NB):
                    for m in range(MT):
                        i = m // MH * 2 + b // 8
                        ins = nc.tensor.matmul(ps[:, b // 2, (b % 2) * D:(b % 2 + 1) * D],
                                               gate[:, i, m % MH, (b % 8) * T:(b % 8 + 1) * T], wo[:, m, :],
                                               start=(m == 0), stop=(m == MT - 1))
                    if b % 2:
                        ins.then_inc(out_done, 1)

            @block.vector
            def _(dve):
                for g in range(NB // 2):
                    dve.wait_ge(out_done, g + 1)
                    xr = x_tok[:, 2 * g:2 * g + 2, :].rearrange("p b d -> p (b d)")
                    nc.vector.tensor_tensor(xr, ps[:, g, :], xr, ALU.add).then_inc(out_added, 1)


def wkv_layer(nc, ps, ident, arena_at, x_tok, small, w):
    A = Arena(arena_at.tensor)
    A.at = arena_at.at
    padded = lambda: A.take(KT * NB * TP).rearrange("p (k b t) -> p k b t", k=KT, b=NB)
    k_pad, top = padded(), padded()
    aa, bb, decay_b, new_b, new_bv = (padded() for _ in range(5))
    flat = lambda r, k: r[:, k, :, :].rearrange("p b t -> p (b t)")
    v = A.take(KT * NT).rearrange("p (k b t) -> p k b t", k=KT, b=NB)
    xn_tok = A.take(NB * D).rearrange("p (b d) -> p b d", d=D)
    e1 = A.take(NT).rearrange("p (b t) -> p b t", b=NB)
    e2 = A.take(NT).rearrange("p (b t) -> p b t", b=NB)
    y = xn_tok.rearrange("p b d -> p (b d)").rearrange("p (k b t) -> p k b t", k=KT, b=NB)
    den = A.take(NT).rearrange("p (b t) -> p b t", b=NB)
    q_top = A.take(NT).rearrange("p (b t) -> p b t", b=NB)
    drop = A.take(NB * TP).rearrange("p (b t) -> p b t", b=NB)
    par = A.take(2 * KT).rearrange("p (j k) -> p j k", k=KT)
    with ExitStack() as ctx:
        sem = lambda n: ctx.enter_context(nc.semaphore(n))
        w_here, dve_own, act_own = sem("wkv_here"), sem("dve_own_wkv"), sem("act_own_wkv")
        with nc.Block() as block:
            @block.sync
            def _(sp):
                n = dma_all(sp, [(v.rearrange("p k b t -> p k (b t)"), w["ctx_t"]), (par[:, 0, :], w["decay"]),
                                 (par[:, 1, :], w["first"])], w_here)
                sp.wait_ge(w_here, n)
        norm_stage(nc, ps, ident, x_tok, xn_tok, lambda k, c: k_pad[:, k, c * BPC:(c + 1) * BPC, 1:TP], small, "wkv")
        rate_done, gaps_done, e12_done, gapsb_done, eb_done, bv_done, den_done, rec_done = map(
            sem, ("wkv_rate", "wkv_gaps", "wkv_e12", "wkv_gapsb", "wkv_eb", "wkv_bv", "wkv_den", "wkv_rec"))
        with nc.Block() as block:
            @block.scalar
            def _(act):
                own = Chain(act, act_own)
                own(nc.scalar.activation(par[:, 0, :], par[:, 0, :], ACT.Exp))
                nc.scalar.mul(par[:, 0, :], par[:, 0, :], -1.0).then_inc(rate_done, 1)
                for k in range(KT):
                    act.wait_ge(gapsb_done, 2 * k + 1)
                    nc.scalar.activation(decay_b[:, k, :, 1:TP], decay_b[:, k, :, 1:TP], ACT.Exp).then_inc(eb_done, 1)
                    act.wait_ge(gapsb_done, 2 * k + 2)
                    nc.scalar.activation(new_b[:, k, :, 1:TP], new_b[:, k, :, 1:TP], ACT.Exp).then_inc(eb_done, 1)
                    act.wait_ge(gaps_done, 2 * k + 1)
                    nc.scalar.activation(e1, e1, ACT.Exp).then_inc(e12_done, 1)
                    act.wait_ge(gaps_done, 2 * k + 2)
                    nc.scalar.activation(e2, e2, ACT.Exp).then_inc(e12_done, 1)
                    act.wait_ge(den_done, k + 1)
                    own(nc.scalar.activation(q_top, den, ACT.Ln))
                    nc.scalar.activation(q_top, q_top, ACT.Exp, scale=-1.0).then_inc(rec_done, 1)

            @block.vector
            def _(dve):
                own = Chain(dve, dve_own)
                dve.wait_ge(rate_done, 1)
                for k in range(KT):
                    w_k, u_k = par[:, 0, k:k + 1], par[:, 1, k:k + 1]
                    now, old = slice(1, TP), slice(0, T)
                    nc.vector.memset(k_pad[:, k, :, 0:1], -1.0e38)
                    for r in (decay_b, new_b, new_bv):
                        nc.vector.memset(r[:, k, :, 0:1], 0.0)
                    own(nc.vector.memset(drop, 0.0))
                    own(nc.vector.tensor_scalar(drop, drop, w_k, None, ALU.add))
                    own(nc.vector.memset(drop[:, :, 0:1], -1.0e38))
                    own(nc.vector.tensor_tensor_scan(flat(top, k), drop.rearrange("p b t -> p (b t)"), flat(k_pad, k),
                                                     -1.0e38, ALU.add, ALU.max))
                    kn, pn, po = k_pad[:, k, :, now], top[:, k, :, now], top[:, k, :, old]
                    nc.vector.scalar_tensor_tensor(out=decay_b[:, k, :, now], in0=po, scalar=w_k, in1=pn,
                                                   op0=ALU.add, op1=ALU.subtract).then_inc(gapsb_done, 1)
                    nc.vector.tensor_tensor(new_b[:, k, :, now], kn, pn, ALU.subtract).then_inc(gapsb_done, 1)
                    own(nc.vector.scalar_tensor_tensor(out=q_top, in0=kn, scalar=u_k, in1=po, op0=ALU.add, op1=ALU.max))
                    nc.vector.tensor_tensor(e1, po, q_top, ALU.subtract).then_inc(gaps_done, 1)
                    nc.vector.scalar_tensor_tensor(out=e2, in0=kn, scalar=u_k, in1=q_top, op0=ALU.add,
                                                   op1=ALU.subtract).then_inc(gaps_done, 1)
                    dve.wait_ge(eb_done, 2 * k + 2)
                    own(nc.vector.tensor_tensor(new_bv[:, k, :, now], new_b[:, k, :, now], v[:, k, :, :], ALU.mult))
                    nc.vector.tensor_tensor_scan(flat(aa, k), flat(decay_b, k), flat(new_bv, k), 0.0, ALU.mult, ALU.add)
                    own(nc.vector.tensor_tensor_scan(flat(bb, k), flat(decay_b, k), flat(new_b, k), 0.0,
                                                     ALU.mult, ALU.add))
                    dve.wait_ge(e12_done, 2 * k + 2)
                    nc.vector.tensor_tensor(aa[:, k, :, old], aa[:, k, :, old], e1, ALU.mult)
                    own(nc.vector.tensor_tensor(bb[:, k, :, old], bb[:, k, :, old], e1, ALU.mult))
                    nc.vector.tensor_tensor(den, bb[:, k, :, old], e2, ALU.add).then_inc(den_done, 1)
                    dve.wait_ge(den_done, k + 1)
                    own(nc.vector.tensor_tensor(e2, e2, v[:, k, :, :], ALU.mult))
                    own(nc.vector.tensor_tensor(e2, e2, aa[:, k, :, old], ALU.add))
                    dve.wait_ge(rec_done, k + 1)
                    own(nc.vector.tensor_tensor(den, den, q_top, ALU.mult))
                    own(nc.vector.scalar_tensor_tensor(out=den, in0=den, scalar=2.0, in1=q_top, op0=ALU.subtract,
                                                       op1=ALU.mult))
                    own(nc.vector.scalar_tensor_tensor(out=y[:, k, :, :], in0=den, scalar=-1.0, in1=e2, op0=ALU.mult,
                                                       op1=ALU.mult))
        add_transposed_stage(nc, ps, ident, x_tok, lambda k, b: y[:, k, b, :], "wkv")


E0, Z0, I0, K0 = 32, 32, 128, 8
SCALE0, CAP0, EPS0 = 1.5, 128, 1e-20
E1, I1, K1 = 16, 224, 4


def ffn0_layer(nc, ps, ident, arena_at, x_tok, small, w):
    A = Arena(arena_at.tensor)
    A.at = arena_at.at
    C = E0 + Z0
    xn_tok = A.take(NB * D).rearrange("p (b d) -> p b d", d=D)
    xn_t = A.take(KT * NT).rearrange("p (k t) -> p k t", k=KT)
    wr = A.take(KT * C).rearrange("p (k c) -> p k c", k=KT)
    bias = A.take(C)
    mask16 = A.take(P).bitcast(BF16).rearrange("p (j t) -> p j t", j=2)
    tok = lambda n: A.take(NB * n).rearrange("p (b c) -> p b c", b=NB)
    sc, biased, left, chosen, top8 = tok(C), tok(C), tok(C), tok(C), tok(8)
    ch16 = A.take(NB * E0 // 2).bitcast(BF16).rearrange("p (b c) -> p b c", b=NB)
    before = A.take(NB * E0 // 2).bitcast(BF16).rearrange("p (b c) -> p b c", b=NB)
    wt = tok(E0)
    row = tok(1)
    row2 = tok(1)
    gu = A.take(2 * KT * 2 * I0).rearrange("p (q k f) -> p q k f", q=2, k=KT)
    dn = A.take(2 * D).rearrange("p (q f) -> p q f", q=2)
    sg = A.take(2 * BANK).rearrange("p (q t) -> p q t", q=2)
    av = A.take(2 * BANK).rearrange("p (q t) -> p q t", q=2)
    with ExitStack() as ctx:
        sem = lambda n: ctx.enter_context(nc.semaphore(n))
        w_here, dve_own = sem("r0_here"), sem("dve_own_r0")
        with nc.Block() as block:
            @block.sync
            def _(sp):
                n = dma_all(sp, [(wr, w["cls"]), (bias, w["bias"].broadcast_to([P, C])), (mask16, w["mask16"])], w_here)
                sp.wait_ge(w_here, n)
        norm_stage(nc, ps, ident, x_tok, xn_tok,
                   lambda k, c: xn_t[:, k, c * BANK:(c + 1) * BANK].rearrange("p (b t) -> p b t", t=T),
                   small, "ffn0")
        logit_done, shifted, exp_done, chosen_done, prefix_done, pos_done = map(
            sem, ("r0_logit", "r0_shift", "r0_exp", "r0_chosen", "r0_prefix", "r0_pos"))
        with nc.Block() as block:
            @block.tensor
            def _(pe):
                for b in range(NB):
                    for k in range(KT):
                        ins = nc.tensor.matmul(ps[:, b // 8, (b % 8) * C:(b % 8 + 1) * C],
                                               xn_t[:, k, b * T:(b + 1) * T], wr[:, k, :],
                                               start=(k == 0), stop=(k == KT - 1))
                ins.then_inc(logit_done, 1)
                pe.wait_ge(prefix_done, 1)
                nc.tensor.matmul(ps[:, 2, :], mask16[:, 0, :], ch16.rearrange("p b c -> p (b c)"), start=True, stop=False)
                nc.tensor.matmul(ps[:, 2, :], mask16[:, 1, :], before.rearrange("p b c -> p (b c)"),
                                 start=False, stop=True).then_inc(pos_done, 1)

            @block.scalar
            def _(act):
                act.wait_ge(shifted, 1)
                nc.scalar.activation(sc, sc, ACT.Exp).then_inc(exp_done, 1)

            @block.vector
            def _(dve):
                own = Chain(dve, dve_own)
                dve.wait_ge(logit_done, 1)
                logits = ps[:, 0:2, :].rearrange("p a (b c) -> p (a b) c", c=C)
                over = lambda r: r.broadcast_to([P, NB, C])
                own(nc.vector.tensor_reduce(row, logits, AX.X, ALU.max))
                nc.vector.tensor_tensor(sc, logits, over(row), ALU.subtract).then_inc(shifted, 1)
                dve.wait_ge(exp_done, 1)
                own(nc.vector.tensor_reduce(row2, sc, AX.X, ALU.add))
                own(nc.vector.reciprocal(row, row2))
                own(nc.vector.tensor_tensor(sc, sc, over(row), ALU.mult))
                own(nc.vector.tensor_tensor(biased, sc, bias.rearrange("p (o c) -> p o c", o=1).broadcast_to([P, NB, C]),
                                            ALU.add))
                for b in range(NB):
                    ins = nc.vector.max(top8[:, b, :], biased[:, b, :])
                own(ins)
                for b in range(NB):
                    ins = nc.vector.match_replace(left[:, b, :], top8[:, b, :], biased[:, b, :], -1.0e30)
                own(ins)
                own(nc.vector.tensor_tensor(chosen, left, biased, ALU.not_equal))
                own(nc.vector.tensor_copy(ch16, chosen[:, :, 0:E0]))
                own(nc.vector.memset(before[:, 0, :], 0.0))
                for b in range(1, NB):
                    ins = nc.vector.tensor_tensor(before[:, b, :], before[:, b - 1, :], ch16[:, b - 1, :], ALU.add)
                    if b < NB - 1:
                        own(ins)
                    else:
                        ins.then_inc(prefix_done, 1)
                own(nc.vector.tensor_tensor(sc, sc, chosen, ALU.mult))
                own(nc.vector.tensor_reduce(row2, sc, AX.X, ALU.add))
                own(nc.vector.tensor_scalar(row2, row2, EPS0, None, ALU.add))
                own(nc.vector.reciprocal(row, row2))
                own(nc.vector.tensor_tensor(sc, sc, over(row), ALU.mult))
                own(nc.vector.tensor_scalar(sc, sc, SCALE0, None, ALU.mult))
                own(nc.vector.tensor_reduce(row, sc[:, :, E0:], AX.X, ALU.add))
                own(nc.vector.tensor_scalar(row, row, 1.0, None, ALU.add))
                own(nc.vector.tensor_tensor(wt, sc[:, :, 0:E0], row.broadcast_to([P, NB, E0]), ALU.mult))
                dve.wait_ge(pos_done, 1)
                own(nc.vector.scalar_tensor_tensor(out=wt.rearrange("p b c -> p (b c)"), in0=ps[:, 2, :],
                                                   scalar=float(CAP0), in1=wt.rearrange("p b c -> p (b c)"),
                                                   op0=ALU.is_lt, op1=ALU.mult))
        dense_experts(nc, ps, x_tok, xn_t, wt, w["gate_up"], w["down"], E0, [I0], gu, dn, sg, av, "e0")


def dense_experts(nc, ps, x_tok, xn_t, wt, w_gu, w_dn, n_exp, widths, gu, dn, sg, av, tag):
    F = len(widths)
    fw = widths[0]
    STEPS = CH * F
    with ExitStack() as ctx:
        sem = lambda n: ctx.enter_context(nc.semaphore(f"{n}_{tag}"))
        w_here = [sem("w_here0"), sem("w_here1")]
        g_done, u_done, silu_done, act_done, out_done, acc_done = map(
            sem, ("g_done", "u_done", "silu_done", "act_done", "out_done", "acc_done"))
        block = ctx.enter_context(nc.Block())

        @block.sync
        def _(sp):
            for q in range(2):
                sp.dma_start(gu[:, q], w_gu[q]).then_inc(w_here[q], 16)
                sp.dma_start(dn[0:fw, q], w_dn[q]).then_inc(w_here[q], 16)
            with sp.Fori(1, n_exp // 2) as j:
                for q in range(2):
                    sp.wait_ge(out_done, ((j - 1) * 2 + q + 1) * NB)
                    sp.dma_start(gu[:, q], w_gu[bass.ds(j * 2 + q, 1)].rearrange("e p k f -> (e p) k f")).then_inc(w_here[q], 16)
                    sp.dma_start(dn[0:fw, q], w_dn[bass.ds(j * 2 + q, 1)].rearrange("e p f -> (e p) f")).then_inc(w_here[q], 16)

        @block.tensor
        def _(pe):
            with pe.Fori(0, n_exp // 2) as j:
                for q in range(2):
                    e = j * 2 + q
                    pe.wait_ge(w_here[q], (j + 1) * 32)

                    def gate_up(c):
                        for f in range(F):
                            s = c * F + f
                            for half, done in ((0, g_done), (1, u_done)):
                                pe.wait_ge(act_done, e * STEPS + s + 1)
                                for k in range(KT):
                                    ins = nc.tensor.matmul(ps[0:fw, 2 * half + s % 2, :],
                                                           gu[:, q, k, (half * F + f) * fw:(half * F + f + 1) * fw],
                                                           xn_t[:, k, c * BANK:(c + 1) * BANK],
                                                           start=(k == 0), stop=(k == KT - 1))
                                ins.then_inc(done, 1)

                    def down(c):
                        pe.wait_ge(act_done, 2 + e * STEPS + (c + 1) * F)
                        for b in range(BPC):
                            s = c * BPC + b
                            pe.wait_ge(acc_done, e * NB + s + NB - 3)
                            for f in range(F):
                                ins = nc.tensor.matmul(ps[:, 4 + s % 4, 0:D],
                                                       av[0:fw, (c % 2) * F + f, b * T:(b + 1) * T],
                                                       dn[0:fw, q, f * D:(f + 1) * D],
                                                       start=(f == 0), stop=(f == F - 1))
                            ins.then_inc(out_done, 1)
                    for c in range(CH):
                        gate_up(c)
                        if c:
                            down(c - 1)
                    down(CH - 1)

        @block.scalar
        def _(act):
            with act.Fori(0, n_exp) as e:
                for s in range(STEPS):
                    act.wait_ge(g_done, e * STEPS + s + 1)
                    act.wait_ge(act_done, e * STEPS + s + 1)
                    nc.scalar.activation(sg[0:fw, s % 2, :], ps[0:fw, s % 2, :], ACT.Silu).then_inc(silu_done, 1)

        @block.vector
        def _(dve):
            dve.sem_inc(act_done, 2)
            dve.sem_inc(acc_done, NB)
            with dve.Fori(0, n_exp) as e:
                def product(c):
                    for f in range(F):
                        s = c * F + f
                        dve.wait_ge(silu_done, e * STEPS + s + 1)
                        dve.wait_ge(u_done, e * STEPS + s + 1)
                        nc.vector.tensor_tensor(av[0:fw, (c % 2) * F + f, :], sg[0:fw, s % 2, :],
                                                ps[0:fw, 2 + s % 2, :], ALU.mult).then_inc(act_done, 1)

                def add(c):
                    for b in range(BPC):
                        s = c * BPC + b
                        dve.wait_ge(out_done, e * NB + s + 1)
                        dve.wait_ge(acc_done, e * NB + s + 1)
                        nc.vector.scalar_tensor_tensor(
                            out=x_tok[:, s, :], in0=ps[:, 4 + s % 4, 0:D],
                            scalar=wt[:, s, bass.ds(e, 1)], in1=x_tok[:, s, :],
                            op0=ALU.mult, op1=ALU.add).then_inc(acc_done, 1)
                for c in range(CH):
                    product(c)
                    if c:
                        add(c - 1)
                add(CH - 1)


HEADS1, HD1, NS1 = 8, 64, 64
XT1 = HEADS1 * HD1 // P
RMS_EPS = 1e-5


def ssd_layer(nc, ps, ident, arena_at, x_tok, small, w):
    A = Arena(arena_at.tensor)
    A.at = arena_at.at
    XC = HEADS1 * HD1
    xn_t = A.take(KT * NT).rearrange("p (k t) -> p k t", k=KT)
    w_z = A.take(KT * XC).rearrange("p (k o) -> p k o", k=KT)
    w_xbc = A.take(KT * (XC + 2 * NS1)).rearrange("p (k o) -> p k o", k=KT)
    w_dt = A.take(KT * HEADS1).rearrange("p (k o) -> p k o", k=KT)
    wo = A.take(XT1 * D).rearrange("p (i d) -> p i d", i=XT1)
    nw = A.take(XT1)
    cw = A.take((XT1 + 1) * TAPS).rearrange("p (m k) -> p m k", k=TAPS)
    cb = A.take(XT1 + 1)
    dtb, rate, skip = A.take(HEADS1), A.take(HEADS1), A.take(HEADS1)
    masks = A.take(2 * P).rearrange("p (j t) -> p j t", j=2)
    b_t, c_t = A.take(NT), A.take(NT)
    tok = lambda n: A.take(NB * n).rearrange("p (b c) -> p b c", b=NB)
    xh, zs = tok(XC), tok(XC)
    dt, da, e, g, ln = tok(HEADS1), tok(HEADS1), tok(HEADS1), tok(HEADS1), tok(HEADS1)
    sq, rstd = A.take(NB), A.take(NB)
    at0 = A.at
    xc = A.take(XT1 * NT).rearrange("p (m t) -> p m t", m=XT1)
    at1 = A.at
    pre = [A.take(NB * (T + TAPS - 1)).rearrange("p (b t) -> p b t", b=NB) for _ in range(2)]
    acc = [A.take(NT) for _ in range(2)]
    A.at = at1
    xn_tok = A.take(NB * D).rearrange("p (b d) -> p b d", d=D)
    A.at = at0
    two = lambda *d: A.take(2 * d[0] * d[1]).rearrange("p (q a c) -> p q a c", q=2, a=d[0])
    gm = two(1, T)
    seg_l, ex = two(HEADS1, T), two(HEADS1, T)
    xdt, dx, yz = two(HEADS1, HD1), two(HEADS1, HD1), two(HEADS1, HD1)
    yz_t = two(XT1, T)
    raw = A.take(NB * D).rearrange("p (b d) -> p b d", d=D)
    junk = A.take(XC)

    with ExitStack() as ctx:
        sem = lambda n: ctx.enter_context(nc.semaphore(n))
        w_here = sem("l1_weights")
        bc = lambda a: a.broadcast_to([P, HEADS1])
        with nc.Block() as block:
            @block.sync
            def _(sp):
                n = dma_all(sp, [(w_z, w["z"]), (w_xbc, w["xbc"]), (w_dt, w["dt"]), (wo, w["out_proj"]), (nw, w["norm_w"]),
                                 (cw, w["conv_w"]), (cb, w["conv_b"]), (dtb, bc(w["dt_bias"])), (rate, bc(w["a_log"])),
                                 (skip, bc(w["d"])), (masks, w["masks"])], w_here)
                sp.wait_ge(w_here, n)
        norm_stage(nc, ps, ident, x_tok, xn_tok,
                   lambda k, c: xn_t[:, k, c * BANK:(c + 1) * BANK].rearrange("p (b t) -> p b t", t=T), small, "ssd")

        def put_x(m):
            if m < XT1:
                return [(xc[:, m, :], acc[m % 2])]
            return [(b_t[0:NS1], acc[m % 2][0:NS1]), (c_t[0:NS1], acc[m % 2][NS1:])]

        conv_stage(nc, ps, xn_t, w_xbc, XT1 + 1, put_x, 0, None, cw, cb, pre, acc, "m1")

        z_done, z_taken, dtp_done, xt_done, xt_taken, dve_own, act_own, ab_done, one_e, ln_done = map(
            sem, ("z_done", "z_taken", "dt1_proj", "x1_turned", "x1_taken", "dve_own_s1", "act_own_s1",
                  "dt1_abs", "dt1_one_e", "dt1_ln"))
        v8 = lambda r: r.rearrange("p (o h) -> p o h", o=1).broadcast_to([P, NB, HEADS1])
        with nc.Block() as block:
            @block.tensor
            def _(pe):
                for b in range(NB):
                    for k in range(KT):
                        ins = nc.tensor.matmul(ps[:, 7, b * HEADS1:(b + 1) * HEADS1], xn_t[:, k, b * T:(b + 1) * T],
                                               w_dt[:, k, :], start=(k == 0), stop=(k == KT - 1))
                ins.then_inc(dtp_done, 1)
                for b in range(NB):
                    if b >= 3:
                        pe.wait_ge(z_taken, b - 2)
                    for k in range(KT):
                        ins = nc.tensor.matmul(ps[:, b % 3, :], xn_t[:, k, b * T:(b + 1) * T], w_z[:, k, :],
                                               start=(k == 0), stop=(k == KT - 1))
                    ins.then_inc(z_done, 1)
                    if b >= 3:
                        pe.wait_ge(xt_taken, b - 2)
                    for m in range(XT1):
                        ins = nc.tensor.transpose(ps[:, 3 + b % 3, m * P:(m + 1) * P], xc[:, m, b * T:(b + 1) * T], ident)
                    ins.then_inc(xt_done, 1)

            @block.scalar
            def _(act):
                own = Chain(act, act_own)
                own(nc.scalar.activation(rate, rate, ACT.Exp))
                nc.scalar.mul(rate, rate, -1.0).then_inc(ab_done, 1)
                act.wait_ge(one_e, 1)
                own(nc.scalar.activation(e, dt, ACT.Abs))
                nc.scalar.activation(e, e, ACT.Exp, scale=-1.0).then_inc(ab_done, 1)
                act.wait_ge(one_e, 2)
                nc.scalar.activation(ln, g, ACT.Ln).then_inc(ln_done, 1)
                for b in range(NB):
                    act.wait_ge(z_done, b + 1)
                    nc.scalar.activation(zs[:, b, :], ps[:, b % 3, :], ACT.Silu).then_inc(z_taken, 1)

            @block.vector
            def _(dve):
                own = Chain(dve, dve_own)
                dve.wait_ge(dtp_done, 1)
                nc.vector.tensor_tensor(dt, ps[:, 7, 0:NB * HEADS1].rearrange("p (b h) -> p b h", b=NB), v8(dtb), ALU.add)\
                    .then_inc(one_e, 1)
                dve.wait_ge(ab_done, 2)
                nc.vector.tensor_scalar(g, e, 1.0, None, ALU.add).then_inc(one_e, 1)
                dve.wait_ge(one_e, 2)
                own(nc.vector.scalar_tensor_tensor(out=e, in0=g, scalar=1.0, in1=e, op0=ALU.subtract, op1=ALU.subtract))
                dve.wait_ge(ln_done, 1)
                own(nc.vector.tensor_tensor(ln, ln, e, ALU.subtract))
                own(nc.vector.scalar_tensor_tensor(out=dt, in0=dt, scalar=0.0, in1=ln, op0=ALU.max, op1=ALU.add))
                own(nc.vector.tensor_tensor(da, dt, v8(rate), ALU.mult))
                for m in range(XT1):
                    own(nc.vector.tensor_scalar(wo[:, m, :], wo[:, m, :], nw[:, m:m + 1], None, ALU.mult))
                for b in range(NB):
                    dve.wait_ge(xt_done, b + 1)
                    nc.vector.tensor_copy(xh[:, b, :], ps[:, 3 + b % 3, :]).then_inc(xt_taken, 1)

        g_done, gm_done, lm_done, xd_done, dx_done, seg_done, ex_done, m_done, y_done, yz_done, sq_done, t_done, \
            t_taken, o_done, o_taken = map(sem, (
                "cb_done", "cb_masked", "seg_left", "xdt_done", "skip_done", "seg_done", "seg_exp", "mix_done", "ssd_y",
                "ssd_gated", "ssd_square", "ssd_turned", "ssd_turn_taken", "ssd_out", "ssd_out_taken"))
        flat = lambda r: r.rearrange("p a c -> p (a c)")
        with nc.Block() as block:
            @block.gpsimd
            def _(pool):
                for b in range(NB):
                    q = b % 2
                    if b >= 2:
                        pool.wait_ge(seg_done, b - 1)
                    nc.gpsimd.tensor_tensor(seg_l[:, q], masks[:, 0:1, :].broadcast_to([P, HEADS1, T]),
                                            da[:, b, :].rearrange("p (h o) -> p h o", o=1).broadcast_to([P, HEADS1, T]),
                                            ALU.mult).then_inc(lm_done, 1)
                    if b >= 2:
                        pool.wait_ge(y_done, b - 1)
                    x3 = xh[:, b, :].rearrange("p (h d) -> p h d", h=HEADS1)
                    nc.gpsimd.tensor_tensor(xdt[:, q], x3, dt[:, b, :].rearrange("p (h o) -> p h o", o=1)
                                            .broadcast_to([P, HEADS1, HD1]), ALU.mult).then_inc(xd_done, 1)
                    if b >= 2:
                        pool.wait_ge(yz_done, 2 * (b - 2) + 1)
                    nc.gpsimd.tensor_tensor(dx[:, q], x3, skip.rearrange("p (h o) -> p h o", o=1)
                                            .broadcast_to([P, HEADS1, HD1]), ALU.mult).then_inc(dx_done, 1)

            @block.tensor
            def _(pe):
                def scores(b):
                    q = b % 2
                    if b >= 1:
                        pe.wait_ge(gm_done, b)
                    nc.tensor.matmul(ps[:, 0, q * T:(q + 1) * T], b_t[0:NS1, b * T:(b + 1) * T],
                                     c_t[0:NS1, b * T:(b + 1) * T], start=True, stop=True).then_inc(g_done, 1)
                    pe.wait_ge(lm_done, b + 1)
                    if b >= 2:
                        pe.wait_ge(ex_done, b - 1)
                    for h in range(HEADS1):
                        ins = nc.tensor.matmul(ps[:, 1 + 2 * q + h // 4, (h % 4) * T:(h % 4 + 1) * T], seg_l[:, q, h, :],
                                               masks[:, 1, :], start=True, stop=True)
                    ins.then_inc(seg_done, 1)

                def mix(b):
                    q = b % 2
                    pe.wait_ge(m_done, b + 1)
                    pe.wait_ge(xd_done, b + 1)
                    if b >= 1:
                        pe.wait_ge(yz_done, 2 * (b - 1) + 1)
                    for h in range(HEADS1):
                        ins = nc.tensor.matmul(ps[:, 5, h * HD1:(h + 1) * HD1], ex[:, q, h, :], xdt[:, q, h, :],
                                               start=True, stop=True)
                    ins.then_inc(y_done, 1)

                def project(b):
                    q = b % 2
                    pe.wait_ge(yz_done, 2 * b + 2)
                    if b >= 1:
                        pe.wait_ge(t_taken, b)
                    for m in range(XT1):
                        ins = nc.tensor.transpose(ps[:, 6, m * P:(m + 1) * P], flat(yz[:, q])[:, m * P:(m + 1) * P], ident)
                    ins.then_inc(t_done, 1)
                    pe.wait_ge(t_taken, b + 1)
                    if b >= 1:
                        pe.wait_ge(o_taken, b)
                    for m in range(XT1):
                        ins = nc.tensor.matmul(ps[:, 7, q * D:(q + 1) * D], yz_t[:, q, m, :], wo[:, m, :],
                                               start=(m == 0), stop=(m == XT1 - 1))
                    ins.then_inc(o_done, 1)
                for s in range(NB + 2):
                    if s < NB:
                        scores(s)
                    if 1 <= s <= NB:
                        mix(s - 1)
                    if s >= 2:
                        project(s - 2)

            @block.scalar
            def _(act):
                for s in range(NB + 2):
                    if s < NB:
                        act.wait_ge(seg_done, s + 1)
                        if s >= 2:
                            act.wait_ge(y_done, s - 1)
                        nc.scalar.activation(flat(ex[:, s % 2]),
                                             ps[:, 1 + 2 * (s % 2):3 + 2 * (s % 2), :].rearrange("p a c -> p (a c)"),
                                             ACT.Exp).then_inc(ex_done, 1)
                    if s >= 2:
                        b = s - 2
                        act.wait_ge(yz_done, 2 * b + 2)
                        if b >= 1:
                            act.wait_ge(sq_done, b)
                        nc.scalar.activation(junk, flat(yz[:, b % 2]), ACT.Square, accum_out=sq[:, b:b + 1])\
                            .then_inc(sq_done, 1)
                        act.wait_ge(t_done, b + 1)
                        if b >= 2:
                            act.wait_ge(o_done, b - 1)
                        nc.scalar.activation(flat(yz_t[:, b % 2]), ps[:, 6, :], ACT.Copy).then_inc(t_taken, 1)

            @block.vector
            def _(dve):
                for s in range(NB + 2):
                    if s < NB:
                        q = s % 2
                        dve.wait_ge(g_done, s + 1)
                        if s >= 2:
                            dve.wait_ge(m_done, s - 1)
                        nc.vector.tensor_tensor(gm[:, q, 0, :], ps[:, 0, q * T:(q + 1) * T], masks[:, 1, :], ALU.mult)\
                            .then_inc(gm_done, 1)
                        dve.wait_ge(gm_done, s + 1)
                        dve.wait_ge(ex_done, s + 1)
                        nc.vector.tensor_tensor(ex[:, q], ex[:, q], gm[:, q].broadcast_to([P, HEADS1, T]), ALU.mult)\
                            .then_inc(m_done, 1)
                    if 1 <= s <= NB:
                        b, q = s - 1, (s - 1) % 2
                        dve.wait_ge(y_done, b + 1)
                        dve.wait_ge(dx_done, b + 1)
                        if b >= 2:
                            dve.wait_ge(t_done, b - 1)
                            dve.wait_ge(sq_done, b - 1)
                        nc.vector.tensor_tensor(flat(yz[:, q]), ps[:, 5, :], flat(dx[:, q]), ALU.add).then_inc(yz_done, 1)
                        dve.wait_ge(yz_done, 2 * b + 1)
                        nc.vector.tensor_tensor(flat(yz[:, q]), flat(yz[:, q]), zs[:, b, :], ALU.mult).then_inc(yz_done, 1)
                    if s >= 2:
                        b = s - 2
                        dve.wait_ge(o_done, b + 1)
                        nc.vector.tensor_copy(raw[:, b, :], ps[:, 7, (b % 2) * D:(b % 2 + 1) * D]).then_inc(o_taken, 1)

        var_done, std_done, own_sem = sem("rms_var"), sem("rms_std"), sem("dve_own_rms")
        with nc.Block() as block:
            @block.vector
            def _(dve):
                own = Chain(dve, own_sem)
                nc.vector.tensor_scalar(sq, sq, 1.0 / XC, RMS_EPS, ALU.mult, ALU.add).then_inc(var_done, 1)
                dve.wait_ge(std_done, 1)
                own(nc.vector.reciprocal(rstd, sq))
                for b in range(NB):
                    ins = nc.vector.scalar_tensor_tensor(out=x_tok[:, b, :], in0=raw[:, b, :], scalar=rstd[:, b:b + 1],
                                                         in1=x_tok[:, b, :], op0=ALU.mult, op1=ALU.add)
                own(ins)

            @block.scalar
            def _(act):
                act.wait_ge(var_done, 1)
                nc.scalar.activation(sq, sq, ACT.Sqrt).then_inc(std_done, 1)


HEADS2, HD2 = 16, 8


def longconv_layer(nc, ps, ident, arena_at, x_tok, small, w):
    A = Arena(arena_at.tensor)
    A.at = arena_at.at
    PAIRS = HD2 * HD2
    xn_tok = A.take(NB * D).rearrange("p (b d) -> p b d", d=D)
    q_t = A.take(KT * NT).rearrange("p (k h i b) -> p k h i b", k=KT, h=HEADS2, i=HD2)
    c_rev = A.take(KT * NT).rearrange("p (k h i b) -> p k h i b", k=KT, h=HEADS2, i=HD2)
    toep = A.take(HEADS2 * 2 * P).rearrange("p (h m) -> p h m", h=HEADS2)
    kv = A.take(2 * KT * PAIRS * NB).rearrange("p (q k i j b) -> p q k i j b", q=2, k=KT, i=HD2, j=HD2)
    prod = A.take(2 * PAIRS * NB).rearrange("p (q i j b) -> p q i j b", q=2, i=HD2, j=HD2)
    y_t = A.take(KT * NT).rearrange("p (k h n) -> p k h n", k=KT, h=HEADS2)
    skip = A.take(HEADS2)
    anti = A.take(P)
    with ExitStack() as ctx:
        sem = lambda n: ctx.enter_context(nc.semaphore(n))
        w_here = sem("conv_here")
        src = w["kernel"]
        toep_src = bass.AP(tensor=src.tensor, offset=0, ap=[[1, P], [src.shape[1], HEADS2], [1, 2 * P]])
        with nc.Block() as block:
            @block.sync
            def _(sp):
                n = dma_all(sp, [(c_rev.rearrange("p k h i b -> p k (h i b)"), w["ctx_rev"]), (toep, toep_src),
                                 (skip, w["d"].broadcast_to([P, HEADS2])), (anti, w["anti"])], w_here)
                sp.wait_ge(w_here, n)
        norm_stage(nc, ps, ident, x_tok, xn_tok,
                   lambda k, c: q_t[:, k].rearrange("p h i b -> p b (h i)")[:, c * BPC:(c + 1) * BPC, :], small, "conv")
        diag_done, kv_done, conv_done, prod_done, red_done = map(
            sem, ("toep_diag", "kv_done", "lconv_done", "lprod_done", "lred_done"))
        with nc.Block() as block:
            @block.gpsimd
            def _(pool):
                for h in range(HEADS2):
                    if h >= 2:
                        pool.wait_ge(conv_done, KT * (h - 1))
                    for k in range(KT):
                        c = c_rev[:, k, h]
                        nc.gpsimd.tensor_tensor(
                            kv[:, h % 2, k],
                            c.rearrange("p i (o b) -> p i o b", o=1).broadcast_to([P, HD2, HD2, NB]),
                            c.rearrange("p (o j) b -> p o j b", o=1).broadcast_to([P, HD2, HD2, NB]), ALU.mult)\
                            .then_inc(kv_done, 1)

            @block.tensor
            def _(pe):
                for h in range(HEADS2):
                    pe.wait_ge(kv_done, KT * (h + 1))
                    pe.wait_ge(diag_done, h + 1)
                    for l in range(KT):
                        s = KT * h + l
                        if s >= 4:
                            pe.wait_ge(prod_done, s - 3)
                        for a in range(2):
                            for k in range(l + 1):
                                mv = kv[:, h % 2, k, a * 4:(a + 1) * 4].rearrange("p i j b -> p (i j b)")
                                ins = nc.tensor.matmul(ps[:, 2 * (s % 4) + a, :], toep[:, h, (l - k) * P:(l - k + 1) * P],
                                                       mv, start=(k == 0), stop=(k == l))
                        ins.then_inc(conv_done, 1)

            @block.vector
            def _(dve):
                for h in range(HEADS2):
                    nc.vector.scalar_tensor_tensor(out=toep[:, h, 0:P], in0=anti, scalar=skip[:, h:h + 1],
                                                   in1=toep[:, h, 0:P], op0=ALU.mult, op1=ALU.add).then_inc(diag_done, 1)
                for h in range(HEADS2):
                    for l in range(KT):
                        s = KT * h + l
                        dve.wait_ge(conv_done, s + 1)
                        if s >= 2:
                            dve.wait_ge(red_done, s - 1)
                        banks = ps[:, 2 * (s % 4):2 * (s % 4) + 2, :].rearrange("p a (i j b) -> p (a i) j b", j=HD2, b=NB)
                        qv = q_t[:, l, h].rearrange("p i (o b) -> p i o b", o=1).broadcast_to([P, HD2, HD2, NB])
                        nc.vector.tensor_tensor(prod[:, s % 2], banks, qv, ALU.mult).then_inc(prod_done, 1)
                        dve.wait_ge(prod_done, s + 1)
                        nc.vector.tensor_reduce(y_t[:, l, h, :], prod[:, s % 2].rearrange("p i j b -> p (j b) i"),
                                                AX.X, ALU.add).then_inc(red_done, 1)
        add_transposed_stage(nc, ps, ident, x_tok,
                             lambda k, b: y_t[:, k].rearrange("p h (j b) -> p b (h j)", b=NB)[:, b, :], "conv")


def ffn1_layer(nc, ps, ident, arena_at, x_tok, small, w):
    A = Arena(arena_at.tensor)
    A.at = arena_at.at
    C, CP, fw = E1, 24, I1 // 2
    xn_tok = A.take(NB * D).rearrange("p (b d) -> p b d", d=D)
    xn_t = A.take(KT * NT).rearrange("p (k t) -> p k t", k=KT)
    wr = A.take(KT * C).rearrange("p (k c) -> p k c", k=KT)
    bias = A.take(C)
    tok = lambda n: A.take(NB * n).rearrange("p (b c) -> p b c", b=NB)
    sc, left, top8, wt, row, row2 = tok(CP), tok(CP), tok(8), tok(C), tok(1), tok(1)
    gu = A.take(2 * KT * 2 * I1).rearrange("p (q k f) -> p q k f", q=2, k=KT)
    dn = A.take(2 * 2 * D).rearrange("p (q f) -> p q f", q=2)
    sg = A.take(2 * BANK).rearrange("p (q t) -> p q t", q=2)
    av = A.take(4 * BANK).rearrange("p (q t) -> p q t", q=4)
    with ExitStack() as ctx:
        sem = lambda n: ctx.enter_context(nc.semaphore(n))
        w_here, dve_own = sem("r1_here"), sem("dve_own_r1")
        with nc.Block() as block:
            @block.sync
            def _(sp):
                n = dma_all(sp, [(wr, w["cls"]), (bias, w["bias"].broadcast_to([P, C]))], w_here)
                sp.wait_ge(w_here, n)
        norm_stage(nc, ps, ident, x_tok, xn_tok,
                   lambda k, c: xn_t[:, k, c * BANK:(c + 1) * BANK].rearrange("p (b t) -> p b t", t=T),
                   small, "ffn1")
        logit_done, shifted, exp_done = map(sem, ("r1_logit", "r1_shift", "r1_exp"))
        with nc.Block() as block:
            @block.tensor
            def _(pe):
                for b in range(NB):
                    for k in range(KT):
                        ins = nc.tensor.matmul(ps[:, 0, b * C:(b + 1) * C], xn_t[:, k, b * T:(b + 1) * T], wr[:, k, :],
                                               start=(k == 0), stop=(k == KT - 1))
                ins.then_inc(logit_done, 1)

            @block.scalar
            def _(act):
                act.wait_ge(shifted, 1)
                nc.scalar.activation(wt, wt, ACT.Exp).then_inc(exp_done, 1)

            @block.vector
            def _(dve):
                own = Chain(dve, dve_own)
                dve.wait_ge(logit_done, 1)
                over = lambda r: r.broadcast_to([P, NB, C])
                own(nc.vector.tensor_tensor(wt, ps[:, 0, 0:NB * C].rearrange("p (b c) -> p b c", b=NB),
                                            bias.rearrange("p (o c) -> p o c", o=1).broadcast_to([P, NB, C]), ALU.add))
                own(nc.vector.tensor_reduce(row, wt, AX.X, ALU.max))
                nc.vector.tensor_tensor(wt, wt, over(row), ALU.subtract).then_inc(shifted, 1)
                own(nc.vector.memset(sc[:, :, C:], -1.0))
                dve.wait_ge(exp_done, 1)
                own(nc.vector.tensor_reduce(row2, wt, AX.X, ALU.add))
                own(nc.vector.reciprocal(row, row2))
                own(nc.vector.tensor_tensor(sc[:, :, 0:C], wt, over(row), ALU.mult))
                for b in range(NB):
                    ins = nc.vector.max(top8[:, b, :], sc[:, b, :])
                own(ins)
                own(nc.vector.memset(top8[:, :, K1:], -1.0))
                for b in range(NB):
                    ins = nc.vector.match_replace(left[:, b, :], top8[:, b, :], sc[:, b, :], -2.0)
                own(ins)
                own(nc.vector.tensor_tensor(left, left, sc, ALU.not_equal))
                own(nc.vector.tensor_tensor(wt, sc[:, :, 0:C], left[:, :, 0:C], ALU.mult))
                own(nc.vector.tensor_reduce(row2, wt, AX.X, ALU.add))
                own(nc.vector.reciprocal(row, row2))
                own(nc.vector.tensor_tensor(wt, wt, over(row), ALU.mult))
        dense_experts(nc, ps, x_tok, xn_t, wt, w["gate_up"], w["down"], E1, [fw, fw], gu, dn, sg, av, "e1")


def build(nc, ins, out):
    with ExitStack() as ctx:
        sbuf = ctx.enter_context(nc.sbuf_tensor("sbuf", [P, 52900], F32))
        ps = ctx.enter_context(nc.psum_tensor("ps", [P, NBANK, BANK], F32))
        A = Arena(sbuf)
        ident = A.take(P)
        small = A.take(176)
        x_tok = A.take(NB * D).rearrange("p (b d) -> p b d", d=D)
        in_here = ctx.enter_context(nc.semaphore("in_here"))
        stored = ctx.enter_context(nc.semaphore("stored"))
        with nc.Block() as block:
            @block.sync
            def _(sp):
                n = dma_all(sp, [(x_tok, ins["x"].rearrange("b t d -> t b d")), (ident, ins["ident"])], in_here)
                sp.wait_ge(in_here, n)
        scan_layer(nc, ps, ident, A, x_tok, small, {k[3:]: v for k, v in ins.items() if k.startswith("m0_")})
        wkv_layer(nc, ps, ident, A, x_tok, small, {k[3:]: v for k, v in ins.items() if k.startswith("c0_")})
        ffn0_layer(nc, ps, ident, A, x_tok, small, {k[3:]: v for k, v in ins.items() if k.startswith("f0_")})
        ssd_layer(nc, ps, ident, A, x_tok, small, {k[3:]: v for k, v in ins.items() if k.startswith("m1_")})
        longconv_layer(nc, ps, ident, A, x_tok, small, {k[3:]: v for k, v in ins.items() if k.startswith("c1_")})
        ffn1_layer(nc, ps, ident, A, x_tok, small, {k[3:]: v for k, v in ins.items() if k.startswith("f1_")})
        with nc.Block() as block:
            @block.sync
            def _(sp):
                sp.dma_start(out.rearrange("b t d -> t b d"), x_tok).then_inc(stored, 16)
                sp.wait_ge(stored, 16)


def _layout(inputs):
    import numpy as np

    def tiles(a):
        return a.reshape(-1, P, a.shape[-1]).transpose(1, 0, 2)

    g = {k: np.asarray(v) for k, v in inputs.items()}
    o = {"x": g["x"], "ident": np.eye(P, dtype=np.float32)}
    w = g["L0_attn_in_proj_w"].reshape(INNER, 2, D)
    o["m0_in_proj"] = tiles(np.concatenate([w[:, 0].T, w[:, 1].T], axis=1))
    o["m0_conv_w"] = tiles(g["L0_attn_conv_w"])
    o["m0_conv_b"] = g["L0_attn_conv_b"].reshape(MT, P).T
    xp = g["L0_attn_x_proj_weight"].transpose(0, 2, 1).reshape(INNER, RANK + BC)
    o["m0_x_dt"] = tiles(xp[:, :RANK])
    o["m0_x_bc"] = tiles(xp[:, RANK:])
    o["m0_dt_proj"] = g["L0_attn_dt_proj_weight"].transpose(2, 0, 1).reshape(RANK, MT, P)
    o["m0_dt_bias"] = g["L0_attn_dt_proj_bias"].reshape(MT, P).T
    o["m0_a_log"] = g["L0_attn_A_log"].reshape(HEADS0, MH, P, NS).transpose(2, 0, 1, 3).reshape(P, HEADS0, MH * NS)
    o["m0_d"] = g["L0_attn_D"].reshape(HEADS0, MH, P).transpose(2, 0, 1)
    o["m0_out_proj"] = tiles(g["L0_attn_out_proj_w"].T)
    rows = np.arange(3 * BC)[:, None, None] % BC == np.arange(BC)[None, :, None]
    sel = np.zeros((P, BC, P), "bfloat16")
    sel[:3 * BC] = rows
    o["m0_sel"] = sel
    ctx = g["ctx_2048"].reshape(NT, D)
    o["c0_ctx_t"] = tiles(ctx.T)
    o["c0_decay"] = g["L0_xattn_time_decay"].reshape(KT, P).T
    o["c0_first"] = g["L0_xattn_time_first"].reshape(KT, P).T
    o["f0_cls"] = tiles(g["L0_ffn_w_cls"].T)
    o["f0_bias"] = g["L0_ffn_bias"].reshape(1, -1)
    before = np.arange(P)[:, None] < np.arange(P)[None, :]
    o["f0_mask16"] = np.stack([before, np.ones((P, P))], axis=1).astype("bfloat16")
    o["f0_gate_up"] = g["L0_ffn_w_gate_up"].reshape(E0, KT, P, 2 * I0).transpose(0, 2, 1, 3)
    o["f0_down"] = g["L0_ffn_w_down"]
    win = g["L1_attn_W_in"]
    xc = HEADS1 * HD1
    o["m1_z"] = tiles(win[:xc].T)
    o["m1_xbc"] = tiles(win[xc:2 * xc + 2 * NS1].T)
    o["m1_dt"] = tiles(win[2 * xc + 2 * NS1:].T)
    o["m1_out_proj"] = tiles(g["L1_attn_W_out"].T)
    o["m1_norm_w"] = g["L1_attn_norm_w"].reshape(XT1, P).T
    o["m1_conv_w"] = tiles(g["L1_attn_conv_w"])
    o["m1_conv_b"] = g["L1_attn_conv_b"].reshape(XT1 + 1, P).T
    for name, key in (("dt_bias", "dt_bias"), ("a_log", "A_log"), ("d", "D")):
        o[f"m1_{name}"] = g[f"L1_attn_{key}"].reshape(1, -1)
    lower = np.arange(P)[:, None] > np.arange(P)[None, :]
    o["m1_masks"] = np.stack([lower, ~lower], axis=1).astype(np.float32)
    o["c1_ctx_rev"] = g["ctx_2048"].transpose(2, 1, 0).reshape(KT, P, NT)[:, ::-1].transpose(1, 0, 2)
    o["c1_kernel"] = np.pad(g["L1_xattn_ssm_kernel"], ((0, 0), (P - 1, 0)))
    o["c1_d"] = g["L1_xattn_D"].reshape(1, -1)
    o["c1_anti"] = np.eye(P, dtype=np.float32)[::-1]
    o["f1_cls"] = tiles(g["L1_ffn_router_w"].T)
    o["f1_bias"] = g["L1_ffn_expert_bias"].reshape(1, -1)
    gu = np.concatenate([g["L1_ffn_gate_proj"], g["L1_ffn_up_proj"]], axis=2)
    o["f1_gate_up"] = gu.reshape(E1, KT, P, 2 * I1).transpose(0, 2, 1, 3)
    o["f1_down"] = g["L1_ffn_down_proj"].reshape(E1, 2, I1 // 2, D).transpose(0, 2, 1, 3).reshape(E1, I1 // 2, 2 * D)
    return {k: np.ascontiguousarray(v) for k, v in o.items()}


def kernel(**inputs):
    import numpy as np
    import concourse.bacc as _bacc
    from concourse.bass_utils import run_bass_kernel_spmd as _run

    nc = _bacc.Bacc("TRN2", target_bir_lowering=False, num_devices=1)
    arrays = _layout(inputs)
    aps = {k: nc.dram_tensor(f"in_{k}", a.shape, mybir.dt.from_np(a.dtype), kind="ExternalInput").ap()
           for k, a in arrays.items()}
    out = nc.dram_tensor("out", (NB, T, D), F32, kind="ExternalOutput").ap()
    build(nc, aps, out)
    got = _run(nc, [{f"in_{k}": a for k, a in arrays.items()}], core_ids=[0])
    return got.results[0]["out"]
```

```python
from contextlib import ExitStack

import concourse.bass as bass
from concourse import mybir

F32 = mybir.dt.float32
BF16 = mybir.dt.bfloat16
U8 = mybir.dt.uint8
ALU = mybir.AluOpType
ACT = mybir.ActivationFunctionType
AX = mybir.AxisListType

P = 128
NB = 16
T = 128
D = 256
KT = D // P
NT = NB * T
TP = T + 1
BANK = 512
NBANK = 8
CH = NT // BANK
BPC = BANK // T
LN_EPS = 1e-5
BIG = 1.0e25

INNER = 512
MT = INNER // P
HEADS0 = 2
MH = MT // HEADS0
NS = 16
RANK = 128
TAPS = 4
PASSES = HEADS0 * CH
RING0 = 4
BC = 2 * NS



class Chain:

    def __init__(self, eng, sem):
        self.eng, self.sem, self.n = eng, sem, 0

    def __call__(self, ins):
        ins.then_inc(self.sem, 1)
        self.n += 1
        self.eng.wait_ge(self.sem, self.n)


class Semaphores:

    def __init__(self, nc):
        self.nc, self.held = nc, []

    def __call__(self, name):
        self.held.append(self.nc.alloc_semaphore(name=name))
        return self.held[-1]

    def clear(self):
        self.nc.clear_and_free_semaphores(self.held)
        self.held = []
        with self.nc.Block():
            pass


class Arena:

    def __init__(self, tensor):
        self.tensor, self.at = tensor, 0

    def take(self, words):
        self.at += words
        assert self.at <= self.tensor.shape[1], self.at
        return self.tensor[:, self.at - words:self.at]


def dma_all(eng, pairs, sem):
    for dst, src in pairs:
        eng.dma_start(dst, src).then_inc(sem, 16)
    return 16 * len(pairs)


def norm_stage(nc, ps, sems, ident, x_tok, xn_tok, xn_cols, small, tag):
    with ExitStack() as ctx:
        sem = lambda n: sems(f"{n}_{tag}")
        stats_done, std_done, xn_done, xt_done, xt_copied = map(sem, ("stats", "std", "xn", "xt", "xtc"))
        dve_own = sem("dve_own_ln")
        stats = small[:, 0:NB * 6].rearrange("p (b s) -> p b s", s=6)
        mv = small[:, 96:96 + NB * 2].rearrange("p (b s) -> p b s", s=2)
        std = small[:, 128:128 + NB]
        rstd = small[:, 144:144 + NB]
        eps = small[:, 160:161]
        block = ctx.enter_context(nc.Block())

        @block.vector
        def _(dve):
            chain = Chain(dve, dve_own)
            nc.vector.memset(eps, LN_EPS).then_inc(stats_done, 1)
            for b in range(NB):
                ins = nc.vector.bn_stats(stats[:, b, :], x_tok[:, b, :])
            chain(ins)
            for b in range(NB):
                ins = nc.vector.bn_aggr(mv[:, b, :], stats[:, b, :])
            ins.then_inc(stats_done, 1)
            dve.wait_ge(std_done, 1)
            chain(nc.vector.reciprocal(rstd, std))
            for b in range(NB):
                nc.vector.tensor_scalar(xn_tok[:, b, :], x_tok[:, b, :], mv[:, b, 0:1], rstd[:, b:b + 1],
                                        ALU.subtract, ALU.mult).then_inc(xn_done, 1)

        @block.scalar
        def _(act):
            act.wait_ge(stats_done, 2)
            nc.scalar.activation(std, mv[:, :, 1], ACT.Sqrt, bias=eps).then_inc(std_done, 1)
            for c in range(CH):
                for k in range(KT):
                    act.wait_ge(xt_done, c * KT + k + 1)
                    nc.scalar.activation(xn_cols(k, c), ps[:, c * KT + k, :].rearrange("p (b t) -> p b t", t=T),
                                         ACT.Copy).then_inc(xt_copied, 1)

        @block.tensor
        def _(pe):
            for c in range(CH):
                pe.wait_ge(xn_done, (c + 1) * BPC)
                for k in range(KT):
                    for j in range(BPC):
                        ins = nc.tensor.transpose(ps[:, c * KT + k, j * T:(j + 1) * T],
                                                  xn_tok[:, c * BPC + j, k * P:(k + 1) * P], ident)
                    ins.then_inc(xt_done, 1)


def add_transposed_stage(nc, ps, sems, ident, x_tok, y_cols, tag):
    with ExitStack() as ctx:
        turned = sems(f"turned_{tag}")
        added = sems(f"added_{tag}")
        block = ctx.enter_context(nc.Block())

        @block.tensor
        def _(pe):
            for b in range(NB):
                for k in range(KT):
                    ins = nc.tensor.transpose(ps[:, b // 2, (b % 2) * D + k * P:(b % 2) * D + (k + 1) * P],
                                              y_cols(k, b), ident)
                if b % 2:
                    ins.then_inc(turned, 1)

        @block.vector
        def _(dve):
            for g in range(NB // 2):
                dve.wait_ge(turned, g + 1)
                xs = x_tok[:, 2 * g:2 * g + 2, :].rearrange("p b d -> p (b d)")
                nc.vector.tensor_tensor(xs, ps[:, g, :], xs, ALU.add).then_inc(added, 1)


def conv_stage(nc, ps, sems, xn_t, w_in, nx, put_x, ng, put_gate, cw, cb, pre, acc, tag):
    with ExitStack() as ctx:
        sem = lambda n: sems(f"{n}_{tag}")
        proj_done, pre_copied, gate_done, conv_done, xs_done, pads_zero = map(
            sem, ("proj_done", "pre_copied", "gate_done", "conv_done", "xs_done", "pads_zero"))
        block = ctx.enter_context(nc.Block())

        @block.tensor
        def _(pe):
            for m in range(nx + ng):
                for c in range(CH):
                    if m >= 2:
                        n = (m - 2) * CH + c + 1
                        if m - 2 < nx:
                            pe.wait_ge(pre_copied, n)
                        else:
                            pe.wait_ge(gate_done, n - nx * CH)
                    for k in range(KT):
                        ins = nc.tensor.matmul(ps[:, (m % 2) * CH + c, :], w_in[:, k, m * P:(m + 1) * P],
                                               xn_t[:, k, c * BANK:(c + 1) * BANK],
                                               start=(k == 0), stop=(k == KT - 1))
                    ins.then_inc(proj_done, 1)

        @block.scalar
        def _(act):
            act.wait_ge(pads_zero, 2)

            def take_x(m):
                for c in range(CH):
                    act.wait_ge(proj_done, m * CH + c + 1)
                    bank = ps[:, (m % 2) * CH + c, :]
                    nc.scalar.activation(pre[m % 2][:, c * BPC:(c + 1) * BPC, TAPS - 1:],
                                         bank.rearrange("p (b t) -> p b t", t=T), ACT.Copy)
                    nc.scalar.activation(acc[m % 2][:, c * BANK:(c + 1) * BANK], bank, ACT.Identity,
                                         scale=cw[:, m, TAPS - 1:TAPS], bias=cb[:, m:m + 1])\
                        .then_inc(pre_copied, 1)

            def silu_x(m):
                act.wait_ge(conv_done, (TAPS - 1) * (m + 1))
                for dst, src in put_x(m):
                    ins = nc.scalar.activation(dst, src, ACT.Silu)
                ins.then_inc(xs_done, 1)

            def take_gate(m):
                for c in range(CH):
                    act.wait_ge(proj_done, (nx + m) * CH + c + 1)
                    nc.scalar.activation(put_gate(m, c), ps[:, ((nx + m) % 2) * CH + c, :], ACT.Silu)\
                        .then_inc(gate_done, 1)

            take_x(0)
            take_x(1)
            for m in range(2, nx):
                silu_x(m - 2)
                act.wait_ge(xs_done, m - 1)
                take_x(m)
            if ng:
                take_gate(0)
            silu_x(nx - 2)
            if ng:
                take_gate(1)
            silu_x(nx - 1)
            for m in range(2, ng):
                take_gate(m)

        @block.vector
        def _(dve):
            for q in range(2):
                nc.vector.memset(pre[q][:, :, 0:TAPS - 1], 0.0).then_inc(pads_zero, 1)
            for m in range(nx):
                dve.wait_ge(pre_copied, (m + 1) * CH)
                a3 = acc[m % 2].rearrange("p (b t) -> p b t", t=T)
                for k in range(TAPS - 1):
                    nc.vector.scalar_tensor_tensor(out=a3, in0=pre[m % 2][:, :, k:k + T],
                                                   scalar=cw[:, m, k:k + 1], in1=a3,
                                                   op0=ALU.mult, op1=ALU.add).then_inc(conv_done, 1)
                    dve.wait_ge(conv_done, m * (TAPS - 1) + k + 1)


def scan_layer(nc, ps, sems, ident, arena_at, x_tok, small, w):
    A = Arena(arena_at.tensor)
    A.at = arena_at.at
    big = [A.take(MT * NT) for _ in range(4)]
    xs, gate, dt, u = (r.rearrange("p (i m t) -> p i m t", i=PASSES, m=MH) for r in big)
    xn_tok = big[2][:, 0:NB * D].rearrange("p (b d) -> p b d", d=D)
    xn_t = big[3][:, 0:KT * NT].rearrange("p (k t) -> p k t", k=KT)
    dt_in = big[3][:, KT * NT:KT * NT + HEADS0 * NT].rearrange("p (h t) -> p h t", h=HEADS0)
    bc3 = A.take(HEADS0 * NT // 2).bitcast(BF16).rearrange("p (i t) -> p i t", i=PASSES)
    rate = A.take(PASSES * MH * NS).rearrange("p (i n) -> p i n", i=PASSES)
    skip = A.take(PASSES * MH).rearrange("p (i m) -> p i m", i=PASSES)
    wo = A.take(MT * D).rearrange("p (m d) -> p m d", m=MT)
    temp0 = A.at
    w_in = A.take(KT * 2 * INNER).rearrange("p (k o) -> p k o", k=KT)
    cw = A.take(MT * TAPS).rearrange("p (m k) -> p m k", k=TAPS)
    cb = A.take(MT)
    wx = A.take(MT * RANK).rearrange("p (m r) -> p m r", m=MT)
    wbc = A.take(MT * 3 * BC).rearrange("p (m r) -> p m r", m=MT)
    wdt = A.take(INNER).rearrange("p (m d) -> p m d", m=MT)
    dtb = A.take(MT)
    pre = [A.take(NB * (T + TAPS - 1)).rearrange("p (b t) -> p b t", b=NB) for _ in range(2)]
    acc = [A.take(NT) for _ in range(2)]
    r1 = pre[0].rearrange("p b t -> p (b t)")[:, 0:2 * BANK].rearrange("p (j t) -> p j t", j=2)
    half16 = pre[0].rearrange("p b t -> p (b t)")[:, 2 * BANK:2 * BANK + BANK].bitcast(BF16)\
        .rearrange("p (j t) -> p j t", j=2)

    with ExitStack() as ctx:
        sem = sems
        w_here = sem("l0_weights")
        wsrc = [(w_in, w["in_proj"]), (cw, w["conv_w"]), (cb, w["conv_b"]), (wx, w["x_dt"]),
                (wdt, w["dt_proj"]), (dtb, w["dt_bias"]), (wo, w["out_proj"])]
        wsrc += [(wbc[:, :, j * BC:(j + 1) * BC], w["x_bc"]) for j in range(3)]
        wsrc += [(rate[:, j::CH, :], w["a_log"]) for j in range(CH)] + [(skip[:, j::CH, :], w["d"]) for j in range(CH)]
        with nc.Block() as block:
            @block.sync
            def _(sp):
                n = dma_all(sp, wsrc, w_here)
                sp.wait_ge(w_here, n)
        norm_stage(nc, ps, sems, ident, x_tok, xn_tok,
                   lambda k, c: xn_t[:, k, c * BANK:(c + 1) * BANK].rearrange("p (b t) -> p b t", t=T),
                   small, "scan")

        def put_x(m):
            return [(xs[:, m // MH * CH:(m // MH + 1) * CH, m % MH, :], acc[m % 2].rearrange("p (c t) -> p c t", c=CH))]

        def put_gate(m, c):
            return gate[:, m // MH * CH + c, m % MH, :]

        conv_stage(nc, ps, sems, xn_t, w_in, MT, put_x, MT, put_gate, cw, cb, pre, acc, "m0")

        xp_done, xp_copied, bc_split, dtp_done, pre_done, e_done, one_e, ln_done, dt_done, u_done = map(
            sem, ("xp_done", "xp_copied", "bc_split", "dtp_done", "dtpre_done", "e_done", "one_e", "ln_done",
                  "dt_done", "u_done"))
        dve_own = sem("dve_own_proj")
        act_own = sem("act_own_proj")

        def dtp(m, c):
            return dt[:, m // MH * CH + c, m % MH, :]

        def rows(t4, m):
            return t4[:, m // MH * CH:(m // MH + 1) * CH, m % MH, :]

        with nc.Block() as block:
            @block.tensor
            def _(pe):
                for j in range(HEADS0 * CH):
                    h = j // CH
                    if j >= 2:
                        pe.wait_ge(xp_copied, j - 1)
                    for k in range(MH):
                        x_in = xs[:, j, k, :]
                        nc.tensor.matmul(ps[:, j % 2, :], wx[:, h * MH + k, :], x_in,
                                         start=(k == 0), stop=(k == MH - 1))
                    if j >= 2:
                        pe.wait_ge(bc_split, j - 1)
                    for k in range(MH):
                        x_in = xs[:, j, k, :]
                        ins = nc.tensor.matmul(ps[0:3 * BC, 2 + j % 2, :], wbc[:, h * MH + k, :], x_in,
                                               start=(k == 0), stop=(k == MH - 1))
                    ins.then_inc(xp_done, 1)
                for m in range(MT):
                    pe.wait_ge(xp_copied, (m // MH + 1) * CH)
                    for c in range(CH):
                        if m >= 1:
                            pe.wait_ge(pre_done, (m - 1) * CH + c + 1)
                        nc.tensor.matmul(ps[:, 4 + c, :], wdt[:, m, :], dt_in[:, m // MH, c * BANK:(c + 1) * BANK],
                                         start=True, stop=True).then_inc(dtp_done, 1)

            @block.scalar
            def _(act):
                own = Chain(act, act_own)
                rates = rate.rearrange("p i n -> p (i n)")
                own(nc.scalar.activation(rates, rates, ACT.Exp))
                own(nc.scalar.mul(rates, rates, -1.0))
                for j in range(HEADS0 * CH):
                    act.wait_ge(xp_done, j + 1)
                    nc.scalar.activation(dt_in[:, j // CH, (j % CH) * BANK:(j % CH + 1) * BANK], ps[:, j % 2, :],
                                         ACT.Copy).then_inc(xp_copied, 1)
                for m in range(MT):
                    for c in range(CH):
                        act.wait_ge(dtp_done, m * CH + c + 1)
                        nc.scalar.activation(dtp(m, c), ps[:, 4 + c, :], ACT.Identity, bias=dtb[:, m:m + 1])\
                            .then_inc(pre_done, 1)
                    if m >= 1:
                        act.wait_ge(dt_done, m)
                    act.wait_ge(pre_done, (m + 1) * CH)
                    e = acc[0].rearrange("p (c t) -> p c t", c=CH)
                    own(nc.scalar.activation(e, rows(dt, m), ACT.Abs))
                    nc.scalar.activation(acc[0], acc[0], ACT.Exp, scale=-1.0).then_inc(e_done, 1)
                    act.wait_ge(one_e, m + 1)
                    nc.scalar.activation(pre[1].rearrange("p b t -> p (b t)")[:, 0:NT], acc[1], ACT.Ln)\
                        .then_inc(ln_done, 1)

            @block.vector
            def _(dve):
                own = Chain(dve, dve_own)
                for j in range(HEADS0 * CH):
                    dve.wait_ge(xp_done, j + 1)
                    bank = ps[0:3 * BC, 2 + j % 2, :]
                    out = bc3[:, j, :]
                    r, s = r1[:, j % 2, :], half16[:, j % 2, :]
                    own(nc.vector.tensor_copy(out[0:3 * BC], bank))
                    nc.vector.tensor_tensor(r[0:3 * BC], bank, out[0:3 * BC], ALU.subtract).then_inc(bc_split, 1)
                    dve.wait_ge(bc_split, j + 1)
                    own(nc.vector.tensor_copy(out[BC:2 * BC], r[BC:2 * BC]))
                    own(nc.vector.tensor_copy(s[2 * BC:3 * BC], r[2 * BC:3 * BC]))
                    own(nc.vector.tensor_tensor(out[2 * BC:3 * BC], r[2 * BC:3 * BC], s[2 * BC:3 * BC],
                                                ALU.subtract))
                ln = pre[1].rearrange("p b t -> p (b t)")[:, 0:NT]
                for m in range(MT):
                    dve.wait_ge(e_done, m + 1)
                    nc.vector.tensor_scalar(acc[1], acc[0], 1.0, None, ALU.add).then_inc(one_e, 1)
                    dve.wait_ge(one_e, m + 1)
                    own(nc.vector.scalar_tensor_tensor(out=acc[0], in0=acc[1], scalar=1.0, in1=acc[0],
                                                       op0=ALU.subtract, op1=ALU.subtract))
                    dve.wait_ge(ln_done, m + 1)
                    own(nc.vector.tensor_tensor(ln, ln, acc[0], ALU.subtract))
                    nc.vector.scalar_tensor_tensor(out=rows(dt, m), in0=rows(dt, m), scalar=0.0,
                                                   in1=ln.rearrange("p (c t) -> p c t", c=CH),
                                                   op0=ALU.max, op1=ALU.add).then_inc(dt_done, 1)
                    dve.wait_ge(dt_done, m + 1)
                    if m >= MH:
                        dve.wait_ge(dtp_done, MT * CH)
                    own(nc.vector.tensor_tensor(rows(u, m), rows(dt, m), rows(xs, m), ALU.mult))
                    nc.vector.memset(rows(dt, m).rearrange("p c (b t) -> p c b t", t=T)[:, :, :, 0:1], BIG)\
                        .then_inc(u_done, 1)

        A.at = temp0
        sel = A.take(BC * P // 2).bitcast(BF16).rearrange("p (n q) -> p n q", q=P)
        state = A.take(RING0 * MH * BANK).rearrange("p (r m t) -> p r m t", r=RING0, m=MH)
        b_copy = A.take(4 * BANK).rearrange("p (q t) -> p q t", q=4)
        sel_here = sem("sel_here")
        with nc.Block() as block:
            @block.sync
            def _(sp):
                sp.dma_start(sel, w["sel"]).then_inc(sel_here, 16)
                sp.wait_ge(sel_here, 16)
        b_done, b_copied, c_done, y_done, decay_done, ub_done, scan_done, hc_done, y_taken = map(
            sem, ("b_done", "b_copied", "c_done", "y_done", "decay_done", "ub_done", "scan_done", "hc_done", "y_taken"))
        ub_paced = sem("ub_paced")
        B_BANK, C_BANK, Y_BANK, DECAY_BANK = 0, 1, 2, 4
        LAST = PASSES - 1
        AHEAD = 2

        def ahead(i, n, by):
            return (i, n + by) if n + by < NS else (i + 1, n + by - NS)

        def at(i):
            return bass.ds(i, 1)

        with nc.Block() as block:
            @block.tensor
            def _(pe):
                def broadcast(i, row, bank, done):
                    nc.tensor.matmul(ps[:, bank, :], sel[0:3 * BC, row, :],
                                     bc3[0:3 * BC, at(i), :].rearrange("p i t -> p (i t)"),
                                     start=True, stop=True).then_inc(done, 1)

                def sum_state(i, n):
                    pe.wait_ge(hc_done, 2 + i * NS + n)
                    if n == 0:
                        pe.wait_ge(y_taken, 1 + i * 3)
                    for m in range(MH):
                        ins = nc.tensor.matmul(ps[:, Y_BANK + m, :], ident, state[:, n % RING0, m, :],
                                               start=(n == 0), stop=(n == NS - 1))
                    ins.then_inc(y_done, 1)

                def run(i, last):
                    for n in range(NS):
                        j, l = ahead(i, n, AHEAD)
                        if not (last and n + AHEAD >= NS):
                            pe.wait_ge(b_copied, 1 + j * NS + l)
                            broadcast(j, l, B_BANK, b_done)
                        pe.wait_ge(hc_done, 1 + i * NS + n)
                        broadcast(i, NS + n, C_BANK, c_done)
                        if n:
                            sum_state(i, n - 1)
                    sum_state(i, NS - 1)

                pe.sem_inc(y_done, RING0)
                for n in range(AHEAD):
                    pe.wait_ge(b_copied, 1 + n)
                    broadcast(0, n, B_BANK, b_done)
                with pe.Fori(0, LAST) as i:
                    run(i, False)
                run(LAST, True)

            @block.scalar
            def _(act):
                def copy_b(i, n):
                    act.wait_ge(b_done, i * NS + n + 1)
                    act.wait_ge(ub_done, i * NS + n - 2)
                    nc.scalar.activation(b_copy[:, n % 4, :], ps[:, B_BANK, :], ACT.Copy).then_inc(b_copied, 1)

                def decays(i, n):
                    act.wait_ge(scan_done, i * NS + n)
                    for m in range(MH):
                        nc.scalar.activation(ps[:, DECAY_BANK + n % 2 * MH + m, :],
                                             dt[:, at(i), m, :].rearrange("p i t -> p (i t)"), ACT.Exp,
                                             scale=rate[:, at(i), m * NS + n:m * NS + n + 1]
                                             .rearrange("p i t -> p (i t)")).then_inc(decay_done, 1)

                def run(i, last):
                    for n in range(NS):
                        if not (last and n + AHEAD >= NS):
                            copy_b(*ahead(i, n, AHEAD))
                        if not (last and n + 1 >= NS):
                            decays(*ahead(i, n, 1))

                act.sem_inc(b_copied, 1)
                for n in range(AHEAD):
                    act.wait_ge(b_done, n + 1)
                    nc.scalar.activation(b_copy[:, n, :], ps[:, B_BANK, :], ACT.Copy).then_inc(b_copied, 1)
                    if n == 0:
                        act.wait_ge(scan_done, 1)
                        decays0 = [nc.scalar.activation(ps[:, DECAY_BANK + m, :], dt[:, 0, m, :], ACT.Exp,
                                                        scale=rate[:, 0, m * NS:m * NS + 1]) for m in range(MH)]
                        for ins in decays0:
                            ins.then_inc(decay_done, 1)
                with act.Fori(0, LAST) as i:
                    run(i, False)
                run(LAST, True)

            @block.gpsimd
            def _(pool):
                pool.sem_inc(ub_done, 1)
                with pool.Fori(0, PASSES) as i:
                    for n in range(NS):
                        pool.wait_ge(b_copied, 2 + i * NS + n)
                        pool.wait_ge(y_done, 1 + i * NS + n)
                        pool.sem_inc(ub_paced, 1)
                        nc.gpsimd.tensor_tensor(state[:, n % RING0],
                                                u[:, at(i)].rearrange("p i m t -> p (i m) t"),
                                                b_copy[:, n % 4:n % 4 + 1, :].broadcast_to([P, MH, BANK]), ALU.mult)\
                            .then_inc(ub_done, 1)

            @block.vector
            def _(dve):
                def take_y(i):
                    dve.wait_ge(y_done, RING0 + (i + 1) * NS)
                    for m in range(MH):
                        xr = xs[:, at(i), m, :].rearrange("p i t -> p (i t)")
                        nc.vector.scalar_tensor_tensor(out=xr, in0=xr, scalar=skip[:, at(i), m:m + 1]
                                                       .rearrange("p i t -> p (i t)"), in1=ps[:, Y_BANK + m, :],
                                                       op0=ALU.mult, op1=ALU.add).then_inc(y_taken, 1)
                    dve.wait_ge(y_taken, 1 + i * 3 + MH)
                    gr = gate[:, at(i)].rearrange("p i m t -> p (i m t)")
                    nc.vector.tensor_tensor(gr, gr, xs[:, at(i)].rearrange("p i m t -> p (i m t)"), ALU.mult)\
                        .then_inc(y_taken, 1)

                def run(i, first):
                    for n in range(NS):
                        st = state[:, n % RING0].rearrange("p m t -> p (m t)")
                        dve.wait_ge(ub_done, 2 + i * NS + n)
                        dve.wait_ge(decay_done, (i * NS + n + 1) * MH)
                        q = DECAY_BANK + n % 2 * MH
                        nc.vector.tensor_tensor_scan(st, ps[:, q:q + MH, :].rearrange("p m t -> p (m t)"), st,
                                                     0.0, ALU.mult, ALU.add).then_inc(scan_done, 1)
                        dve.wait_ge(c_done, i * NS + n + 1)
                        dve.wait_ge(scan_done, 2 + i * NS + n)
                        nc.vector.tensor_tensor(state[:, n % RING0], state[:, n % RING0],
                                                ps[:, C_BANK:C_BANK + 1, :].broadcast_to([P, MH, BANK]), ALU.mult)\
                            .then_inc(hc_done, 1)
                        if n == 0 and not first:
                            take_y(i - 1)

                for one in (scan_done, hc_done, y_taken):
                    dve.sem_inc(one, 1)
                run(0, True)
                with dve.Fori(1, PASSES) as i:
                    run(i, False)
                take_y(LAST)

        out_done, out_added = sem("out0_done"), sem("out0_added")
        with nc.Block() as block:
            @block.tensor
            def _(pe):
                for b in range(NB):
                    for m in range(MT):
                        i = m // MH * CH + b // BPC
                        ins = nc.tensor.matmul(ps[:, b // 2, (b % 2) * D:(b % 2 + 1) * D],
                                               gate[:, i, m % MH, (b % BPC) * T:(b % BPC + 1) * T], wo[:, m, :],
                                               start=(m == 0), stop=(m == MT - 1))
                    if b % 2:
                        ins.then_inc(out_done, 1)

            @block.vector
            def _(dve):
                for g in range(NB // 2):
                    dve.wait_ge(out_done, g + 1)
                    xr = x_tok[:, 2 * g:2 * g + 2, :].rearrange("p b d -> p (b d)")
                    nc.vector.tensor_tensor(xr, ps[:, g, :], xr, ALU.add).then_inc(out_added, 1)


def wkv_layer(nc, ps, sems, ident, arena_at, x_tok, small, w):
    A = Arena(arena_at.tensor)
    A.at = arena_at.at
    padded = lambda: A.take(KT * NB * TP).rearrange("p (k b t) -> p k b t", k=KT, b=NB)
    k_pad, top = padded(), padded()
    aa, bb, decay_b, new_b, new_bv = (padded() for _ in range(5))
    flat = lambda r, k: r[:, k, :, :].rearrange("p b t -> p (b t)")
    v = A.take(KT * NT).rearrange("p (k b t) -> p k b t", k=KT, b=NB)
    xn_tok = A.take(NB * D).rearrange("p (b d) -> p b d", d=D)
    e1 = A.take(NT).rearrange("p (b t) -> p b t", b=NB)
    e2 = A.take(NT).rearrange("p (b t) -> p b t", b=NB)
    y = xn_tok.rearrange("p b d -> p (b d)").rearrange("p (k b t) -> p k b t", k=KT, b=NB)
    den = A.take(NT).rearrange("p (b t) -> p b t", b=NB)
    q_top = A.take(NT).rearrange("p (b t) -> p b t", b=NB)
    drop = A.take(NB * TP).rearrange("p (b t) -> p b t", b=NB)
    par = A.take(2 * KT).rearrange("p (j k) -> p j k", k=KT)
    with ExitStack() as ctx:
        sem = sems
        w_here, dve_own, act_own = sem("wkv_here"), sem("dve_own_wkv"), sem("act_own_wkv")
        with nc.Block() as block:
            @block.sync
            def _(sp):
                n = dma_all(sp, [(v.rearrange("p k b t -> p k (b t)"), w["ctx_t"]), (par[:, 0, :], w["decay"]),
                                 (par[:, 1, :], w["first"])], w_here)
                sp.wait_ge(w_here, n)
        norm_stage(nc, ps, sems, ident, x_tok, xn_tok, lambda k, c: k_pad[:, k, c * BPC:(c + 1) * BPC, 1:TP], small, "wkv")
        rate_done, gaps_done, e12_done, gapsb_done, eb_done, bv_done, den_done, rec_done = map(
            sem, ("wkv_rate", "wkv_gaps", "wkv_e12", "wkv_gapsb", "wkv_eb", "wkv_bv", "wkv_den", "wkv_rec"))
        with nc.Block() as block:
            @block.scalar
            def _(act):
                own = Chain(act, act_own)
                own(nc.scalar.activation(par[:, 0, :], par[:, 0, :], ACT.Exp))
                nc.scalar.mul(par[:, 0, :], par[:, 0, :], -1.0).then_inc(rate_done, 1)
                for k in range(KT):
                    act.wait_ge(gapsb_done, 2 * k + 1)
                    nc.scalar.activation(decay_b[:, k, :, 1:TP], decay_b[:, k, :, 1:TP], ACT.Exp).then_inc(eb_done, 1)
                    act.wait_ge(gapsb_done, 2 * k + 2)
                    nc.scalar.activation(new_b[:, k, :, 1:TP], new_b[:, k, :, 1:TP], ACT.Exp).then_inc(eb_done, 1)
                    act.wait_ge(gaps_done, 2 * k + 1)
                    nc.scalar.activation(e1, e1, ACT.Exp).then_inc(e12_done, 1)
                    act.wait_ge(gaps_done, 2 * k + 2)
                    nc.scalar.activation(e2, e2, ACT.Exp).then_inc(e12_done, 1)
                    act.wait_ge(den_done, k + 1)
                    own(nc.scalar.activation(q_top, den, ACT.Ln))
                    nc.scalar.activation(q_top, q_top, ACT.Exp, scale=-1.0).then_inc(rec_done, 1)

            @block.vector
            def _(dve):
                own = Chain(dve, dve_own)
                dve.wait_ge(rate_done, 1)
                for k in range(KT):
                    w_k, u_k = par[:, 0, k:k + 1], par[:, 1, k:k + 1]
                    now, old = slice(1, TP), slice(0, T)
                    nc.vector.memset(k_pad[:, k, :, 0:1], -1.0e38)
                    for r in (decay_b, new_b, new_bv):
                        nc.vector.memset(r[:, k, :, 0:1], 0.0)
                    own(nc.vector.memset(drop, 0.0))
                    own(nc.vector.tensor_scalar(drop, drop, w_k, None, ALU.add))
                    own(nc.vector.memset(drop[:, :, 0:1], -1.0e38))
                    own(nc.vector.tensor_tensor_scan(flat(top, k), drop.rearrange("p b t -> p (b t)"), flat(k_pad, k),
                                                     -1.0e38, ALU.add, ALU.max))
                    kn, pn, po = k_pad[:, k, :, now], top[:, k, :, now], top[:, k, :, old]
                    nc.vector.scalar_tensor_tensor(out=decay_b[:, k, :, now], in0=po, scalar=w_k, in1=pn,
                                                   op0=ALU.add, op1=ALU.subtract).then_inc(gapsb_done, 1)
                    nc.vector.tensor_tensor(new_b[:, k, :, now], kn, pn, ALU.subtract).then_inc(gapsb_done, 1)
                    own(nc.vector.scalar_tensor_tensor(out=q_top, in0=kn, scalar=u_k, in1=po, op0=ALU.add, op1=ALU.max))
                    nc.vector.tensor_tensor(e1, po, q_top, ALU.subtract).then_inc(gaps_done, 1)
                    nc.vector.scalar_tensor_tensor(out=e2, in0=kn, scalar=u_k, in1=q_top, op0=ALU.add,
                                                   op1=ALU.subtract).then_inc(gaps_done, 1)
                    dve.wait_ge(eb_done, 2 * k + 2)
                    own(nc.vector.tensor_tensor(new_bv[:, k, :, now], new_b[:, k, :, now], v[:, k, :, :], ALU.mult))
                    nc.vector.tensor_tensor_scan(flat(aa, k), flat(decay_b, k), flat(new_bv, k), 0.0, ALU.mult, ALU.add)
                    own(nc.vector.tensor_tensor_scan(flat(bb, k), flat(decay_b, k), flat(new_b, k), 0.0,
                                                     ALU.mult, ALU.add))
                    dve.wait_ge(e12_done, 2 * k + 2)
                    nc.vector.tensor_tensor(aa[:, k, :, old], aa[:, k, :, old], e1, ALU.mult)
                    own(nc.vector.tensor_tensor(bb[:, k, :, old], bb[:, k, :, old], e1, ALU.mult))
                    nc.vector.tensor_tensor(den, bb[:, k, :, old], e2, ALU.add).then_inc(den_done, 1)
                    dve.wait_ge(den_done, k + 1)
                    own(nc.vector.tensor_tensor(e2, e2, v[:, k, :, :], ALU.mult))
                    own(nc.vector.tensor_tensor(e2, e2, aa[:, k, :, old], ALU.add))
                    dve.wait_ge(rec_done, k + 1)
                    own(nc.vector.tensor_tensor(den, den, q_top, ALU.mult))
                    own(nc.vector.scalar_tensor_tensor(out=den, in0=den, scalar=2.0, in1=q_top, op0=ALU.subtract,
                                                       op1=ALU.mult))
                    own(nc.vector.scalar_tensor_tensor(out=y[:, k, :, :], in0=den, scalar=-1.0, in1=e2, op0=ALU.mult,
                                                       op1=ALU.mult))
        add_transposed_stage(nc, ps, sems, ident, x_tok, lambda k, b: y[:, k, b, :], "wkv")


E0, Z0, I0, K0 = 32, 32, 128, 8
SCALE0, CAP0, EPS0 = 1.5, 128, 1e-20
E1, I1, K1 = 16, 224, 4
RING = 8
LAG = 4


def ffn0_layer(nc, ps, sems, ident, arena_at, x_tok, small, w):
    A = Arena(arena_at.tensor)
    A.at = arena_at.at
    C = E0 + Z0
    w_gu = A.take(E0 * KT * 2 * I0).rearrange("p (e k f) -> p e k f", e=E0, k=KT)
    w_dn = A.take(E0 * D).rearrange("p (e f d) -> p e f d", e=E0, f=1)
    cst = A.take(CONST)
    xn_tok = A.take(NB * D).rearrange("p (b d) -> p b d", d=D)
    xn_t = A.take(KT * NT).rearrange("p (k t) -> p k t", k=KT)
    wr = A.take(KT * C).rearrange("p (k c) -> p k c", k=KT)
    bias = A.take(C)
    mask16 = A.take(P).bitcast(BF16).rearrange("p (j t) -> p j t", j=2)
    tok = lambda n: A.take(NB * n).rearrange("p (b c) -> p b c", b=NB)
    sc, biased, left, chosen, top8 = tok(C), tok(C), tok(C), tok(C), tok(8)
    ch16 = A.take(NB * E0 // 2).bitcast(BF16).rearrange("p (b c) -> p b c", b=NB)
    before = A.take(NB * E0 // 2).bitcast(BF16).rearrange("p (b c) -> p b c", b=NB)
    wt, place = tok(E0), tok(E0)
    row = tok(1)
    row2 = tok(1)
    with ExitStack() as ctx:
        sem = sems
        w_here, experts_here, dve_own = sem("r0_here"), sem("experts0_here"), sem("dve_own_r0")
        with nc.Block() as block:
            @block.sync
            def _(sp):
                n = dma_all(sp, [(wr, w["cls"]), (bias, w["bias"].broadcast_to([P, C])), (mask16, w["mask16"]),
                                 (cst, w["const"])], w_here)
                dma_all(sp, [(w_gu, w["gate_up"]), (w_dn, w["down"])], experts_here)
                sp.wait_ge(w_here, n)
        norm_stage(nc, ps, sems, ident, x_tok, xn_tok,
                   lambda k, c: xn_t[:, k, c * BANK:(c + 1) * BANK].rearrange("p (b t) -> p b t", t=T),
                   small, "ffn0")
        logit_done, shifted, exp_done, chosen_done, prefix_done, pos_done = map(
            sem, ("r0_logit", "r0_shift", "r0_exp", "r0_chosen", "r0_prefix", "r0_pos"))
        with nc.Block() as block:
            @block.tensor
            def _(pe):
                for b in range(NB):
                    for k in range(KT):
                        ins = nc.tensor.matmul(ps[:, b // 8, (b % 8) * C:(b % 8 + 1) * C],
                                               xn_t[:, k, b * T:(b + 1) * T], wr[:, k, :],
                                               start=(k == 0), stop=(k == KT - 1))
                ins.then_inc(logit_done, 1)
                pe.wait_ge(prefix_done, 1)
                nc.tensor.matmul(ps[:, 2, :], mask16[:, 0, :], ch16.rearrange("p b c -> p (b c)"), start=True, stop=False)
                nc.tensor.matmul(ps[:, 2, :], mask16[:, 1, :], before.rearrange("p b c -> p (b c)"),
                                 start=False, stop=True).then_inc(pos_done, 1)

            @block.scalar
            def _(act):
                act.wait_ge(shifted, 1)
                nc.scalar.activation(sc, sc, ACT.Exp).then_inc(exp_done, 1)

            @block.vector
            def _(dve):
                own = Chain(dve, dve_own)
                dve.wait_ge(logit_done, 1)
                logits = ps[:, 0:2, :].rearrange("p a (b c) -> p (a b) c", c=C)
                over = lambda r: r.broadcast_to([P, NB, C])
                own(nc.vector.tensor_reduce(row, logits, AX.X, ALU.max))
                nc.vector.tensor_tensor(sc, logits, over(row), ALU.subtract).then_inc(shifted, 1)
                dve.wait_ge(exp_done, 1)
                own(nc.vector.tensor_reduce(row2, sc, AX.X, ALU.add))
                own(nc.vector.reciprocal(row, row2))
                own(nc.vector.tensor_tensor(sc, sc, over(row), ALU.mult))
                own(nc.vector.tensor_tensor(biased, sc, bias.rearrange("p (o c) -> p o c", o=1).broadcast_to([P, NB, C]),
                                            ALU.add))
                for b in range(NB):
                    ins = nc.vector.max(top8[:, b, :], biased[:, b, :])
                own(ins)
                for b in range(NB):
                    ins = nc.vector.match_replace(left[:, b, :], top8[:, b, :], biased[:, b, :], -1.0e30)
                own(ins)
                own(nc.vector.tensor_tensor(chosen, left, biased, ALU.not_equal))
                own(nc.vector.tensor_copy(ch16, chosen[:, :, 0:E0]))
                own(nc.vector.memset(before[:, 0, :], 0.0))
                for b in range(1, NB):
                    ins = nc.vector.tensor_tensor(before[:, b, :], before[:, b - 1, :], ch16[:, b - 1, :], ALU.add)
                    if b < NB - 1:
                        own(ins)
                    else:
                        ins.then_inc(prefix_done, 1)
                own(nc.vector.tensor_tensor(sc, sc, chosen, ALU.mult))
                own(nc.vector.tensor_reduce(row2, sc, AX.X, ALU.add))
                own(nc.vector.tensor_scalar(row2, row2, EPS0, None, ALU.add))
                own(nc.vector.reciprocal(row, row2))
                own(nc.vector.tensor_tensor(sc, sc, over(row), ALU.mult))
                own(nc.vector.tensor_scalar(sc, sc, SCALE0, None, ALU.mult))
                own(nc.vector.tensor_reduce(row, sc[:, :, E0:], AX.X, ALU.add))
                own(nc.vector.tensor_scalar(row, row, 1.0, None, ALU.add))
                own(nc.vector.tensor_tensor(wt, sc[:, :, 0:E0], row.broadcast_to([P, NB, E0]), ALU.mult))
                dve.wait_ge(pos_done, 1)
                own(nc.vector.scalar_tensor_tensor(out=place, in0=ps[:, 2, :].rearrange("p (b c) -> p b c", b=NB),
                                                   scalar=1.0, in1=chosen[:, :, 0:E0], op0=ALU.add, op1=ALU.mult))
                own(nc.vector.tensor_scalar(place, place, -1.0, None, ALU.add))

            @block.sync
            def _(sp):
                sp.wait_ge(experts_here, 32)
        assert CAP0 == P
        sparse_experts(nc, ps, sems, ident, A, x_tok, xn_tok, wt, place, E0, 1, E0, H0, I0, 1,
                       {"w_gu": w_gu, "w_dn": w_dn, "dummy": cst[:, 1:2], "spare": xn_t.rearrange("p k t -> p (k t)")}, expert_const(cst), "e0")



H0, H1 = 16, 64
CONST = 20 + 3 * P + 8
ROUND = 12582912.0


def expert_const(cst):
    wide = lambda j: cst[:, 20 + j * P:20 + (j + 1) * P]
    return cst[:, 0:1], cst[:, 2:19], wide(0), wide(1), wide(2), cst[:, 20 + 3 * P:]


def sparse_experts(nc, ps, sems, ident, A, x_tok, xn_tok, wt, place, n_exp, blocks, n_tiles, H, inner, f_n, w, const, tag):
    fw = inner // f_n
    L, G = P // H, P // H
    W = blocks * L
    NG = n_exp // G
    M = NB * n_exp
    assert G * 2 * W == P
    Q = n_exp * blocks
    ROWS = NT + P
    WIDTH = D + n_exp
    dynamic = blocks > 1
    w_gu = w["w_gu"]
    w_dn = w["w_dn"]
    tok_no, starts, iota, diagonal, spread, low_mask = const
    table = nc.dram_tensor(f"table_{tag}", (ROWS, WIDTH), F32, kind="Internal").ap()
    sums = [nc.dram_tensor(f"sums{j}_{tag}", (ROWS, D), F32, kind="Internal").ap() for j in range(2)]
    idx = A.take(n_tiles).bitcast(mybir.dt.uint32)
    tile_map = A.take(P).bitcast(mybir.dt.int32)
    at0 = A.at
    later = A.take(M * H // 4)
    ups = [r.bitcast(BF16).rearrange("p (b e h) -> p b e h", b=NB // 2, h=H)
           for r in (w["spare"][:, 0:M * H // 4], later)]
    rhs = A.take(M * W).bitcast(BF16).rearrange("p (b e v h) -> p b e v h", b=NB, v=2, h=W)
    cuts = A.take(4 * M)
    S = Arena(later)
    block_no, within, up, code = (cuts[:, j * M:(j + 1) * M] for j in range(4))
    masked = cuts[:, 0:NG * P].rearrange("p (g c) -> p g c", g=NG)
    picked = S.take(NG * P)
    vals = S.take(2 * Q).rearrange("p (e v h) -> p e v h", v=2, h=blocks)
    free_of = S.take(Q).rearrange("p (e h) -> p e h", h=blocks)
    ids = S.take(Q).rearrange("p (e h) -> p e h", h=blocks)
    zero = A.take(WIDTH)
    tiles_of, ends, begins, cmp = (A.take(n_exp) for _ in range(4))
    owns = S.take(Q)
    mp = A.take(8)
    if dynamic:
        col_hot, ids_t, col_t = (S.take(2 * P).rearrange("p (a c) -> p a c", a=2) for _ in range(3))
    A.at = at0
    xe = [A.take(WIDTH) for _ in range(RING)]
    xe_t = [A.take(KT * P).rearrange("p (k s) -> p k s", k=KT) for _ in range(2)]
    sg = [A.take(inner) for _ in range(2)]
    av = [A.take(inner) for _ in range(2)]
    av_t = [A.take(f_n * P).rearrange("p (f s) -> p f s", f=f_n) for _ in range(2)]
    ye = [A.take(D) for _ in range(RING)]
    ixb = A.take(2 * RING).bitcast(mybir.dt.uint32)
    back = xn_tok

    with ExitStack() as ctx:
        sem = lambda n: sems(f"{n}_{tag}")
        own_sem, hot_done, rhs_done, ups_done, found, masked_done, spread_done, zero_done, table_here = map(
            sem, ("own_ix", "hot_done", "rhs_done", "ups_done", "found", "masked_done", "spread_done", "zero_done",
                  "table_here"))
        map_done, map_turned, map_taken, sorted_done = map(sem, ("map_done", "map_turned", "map_taken", "sorted_done"))
        MB = NG * P // BANK
        with nc.Block() as block:
            @block.vector
            def _(dve):
                own = Chain(dve, own_sem)
                nc.vector.memset(zero, 0.0).then_inc(zero_done, 1)
                pl = place.rearrange("p b e -> p (b e)")

                def whole_part(out, src, step):
                    own(nc.vector.tensor_scalar(out, src, 1.0 / step, -(step - 1) / (2.0 * step), ALU.mult, ALU.add))
                    own(nc.vector.tensor_scalar(out, out, ROUND, None, ALU.add))
                    own(nc.vector.tensor_scalar(out, out, ROUND, None, ALU.subtract))

                def rest(out, whole, step, src):
                    own(nc.vector.scalar_tensor_tensor(out=out, in0=whole, scalar=float(-step), in1=src,
                                                       op0=ALU.mult, op1=ALU.add))

                whole_part(block_no, pl, P)
                rest(within, block_no, P, pl)
                whole_part(up, within, L)
                rest(within, up, L, within)
                rest(code, block_no, -L, within)
                one_hot = lambda out, v, m, n: nc.vector.tensor_tensor(
                    out.rearrange("p b e h -> p (b e) h"), v.rearrange("p (b o) -> p b o", o=1).broadcast_to([P, m, n]),
                    iota[:, 0:n].rearrange("p (o h) -> p o h", o=1).broadcast_to([P, m, n]), ALU.is_equal)
                one_hot(rhs[:, :, :, 0, :], code, M, W).then_inc(hot_done, 1)
                for j in range(2):
                    one_hot(ups[j], up[:, j * M // 2:(j + 1) * M // 2], M // 2, H).then_inc(ups_done, 1)
                dve.wait_ge(found, NG)
                own(nc.vector.tensor_tensor(masked, ps[:, 4:4 + MB, :].rearrange("p a (g c) -> p (a g) c", c=P),
                                            diagonal.rearrange("p (o c) -> p o c", o=1).broadcast_to([P, NG, P]),
                                            ALU.mult))
                dve.sem_inc(masked_done, 1)
                dve.wait_ge(spread_done, 1)
                own(nc.vector.tensor_tensor(picked.rearrange("p (c l) -> p c l", l=L),
                                            ps[:, 6:6 + MB, :].rearrange("p a (c l) -> p (a c) l", l=L),
                                            low_mask[:, 0:L].rearrange("p (o l) -> p o l", o=1)
                                            .broadcast_to([P, NG * P // L, L]), ALU.mult))
                own(nc.vector.tensor_reduce(vals.rearrange("p e v h -> p (e v h)"),
                                            picked.rearrange("p (c l) -> p c l", l=L), AX.X, ALU.add))
                own(nc.vector.tensor_scalar(free_of, vals[:, :, 1, :], 0.0, w["dummy"], ALU.is_equal, ALU.mult))
                own(nc.vector.scalar_tensor_tensor(out=ids, in0=vals[:, :, 1, :], scalar=float(T), in1=vals[:, :, 0, :],
                                                   op0=ALU.mult, op1=ALU.add))
                if not dynamic:
                    own(nc.vector.scalar_tensor_tensor(out=idx.rearrange("p (e h) -> p e h", h=blocks), in0=ids,
                                                       scalar=-float(T), in1=free_of, op0=ALU.add, op1=ALU.add))
                else:
                    own(nc.vector.tensor_tensor(ids, ids, free_of, ALU.add))
                    own(nc.vector.tensor_scalar(ids, ids, w["dummy"], None, ALU.subtract))
                    t3 = owns.rearrange("p (e h) -> p e h", h=blocks)
                    own(nc.vector.tensor_tensor(t3, w["queue"].rearrange("p (e o) -> p e o", o=1)
                                                .broadcast_to([P, n_exp, blocks]),
                                                starts[:, 0:blocks].rearrange("p (o h) -> p o h", o=1)
                                                .broadcast_to([P, n_exp, blocks]), ALU.is_gt))
                    own(nc.vector.tensor_reduce(tiles_of, t3, AX.X, ALU.add))
                    own(nc.vector.memset(cmp, 1.0))
                    own(nc.vector.tensor_tensor_scan(ends, cmp, tiles_of, 0.0, ALU.mult, ALU.add))
                    own(nc.vector.tensor_tensor(begins, ends, tiles_of, ALU.subtract))
                    own(nc.vector.tensor_scalar(cmp, begins, tok_no, None, ALU.is_le))
                    own(nc.vector.tensor_reduce(mp[:, 0:1], cmp, AX.X, ALU.add))
                    own(nc.vector.tensor_scalar(mp[:, 0:1], mp[:, 0:1], -1.0, None, ALU.add))
                    own(nc.vector.tensor_tensor(cmp, cmp, begins, ALU.mult))
                    own(nc.vector.tensor_reduce(mp[:, 2:3], cmp, AX.X, ALU.max))
                    own(nc.vector.tensor_scalar(mp[:, 3:4], mp[:, 0:1], float(blocks), tok_no, ALU.mult, ALU.add))
                    own(nc.vector.tensor_tensor(mp[:, 3:4], mp[:, 3:4], mp[:, 2:3], ALU.subtract))
                    own(nc.vector.tensor_tensor(mp[:, 4:5], tok_no, ends[:, n_exp - 1:n_exp], ALU.is_lt))
                    own(nc.vector.tensor_scalar(mp[:, 1:2], mp[:, 3:4], -float(P), None, ALU.add))
                    for a, at in ((0, 3), (1, 1)):
                        own(nc.vector.tensor_scalar(col_hot[:, a, :], iota, mp[:, at:at + 1], mp[:, 4:5],
                                                    ALU.is_equal, ALU.mult))
                    dve.sem_inc(map_done, 1)
                    dve.wait_ge(map_turned, 1)
                    own(nc.vector.tensor_copy(tile_map[0:1, :], ps[0:1, 0, 0:P]))
                    own(nc.vector.tensor_copy(ids_t.rearrange("p a c -> p (a c)"), ps[:, 1, 0:2 * P]))
                    own(nc.vector.tensor_copy(col_t.rearrange("p a c -> p (a c)"), ps[:, 2, 0:2 * P]))
                    dve.sem_inc(map_taken, 1)
                    dve.wait_ge(sorted_done, 1)
                    own(nc.vector.tensor_scalar(idx, ps[:, 3, 0:n_tiles], w["dummy"], -float(T), ALU.add, ALU.add))

            @block.scalar
            def _(act):
                act.wait_ge(hot_done, 1)
                for b in range(NB):
                    nc.scalar.activation(rhs[:, b, :, 1, :], rhs[:, b, :, 0, :], ACT.Copy, scale=float(b + 1))\
                        .then_inc(rhs_done, 1)
                act.wait_ge(rhs_done, NB)
                nc.scalar.activation(rhs[:, :, :, 0, :].rearrange("p b e h -> p (b e) h"),
                                     rhs[:, :, :, 0, :].rearrange("p b e h -> p (b e) h"), ACT.Copy, scale=tok_no)\
                    .then_inc(rhs_done, 1)

            @block.tensor
            def _(pe):
                pe.wait_ge(ups_done, 2)
                pe.wait_ge(rhs_done, NB + 1)
                for g in range(NG):
                    c = g * P % BANK
                    for b in range(NB):
                        ins = nc.tensor.matmul(ps[:, 4 + g * P // BANK, c:c + P],
                                               ups[b // (NB // 2)][:, b % (NB // 2), g * G:(g + 1) * G, :].rearrange("p e h -> p (e h)"),
                                               rhs[:, b, g * G:(g + 1) * G].rearrange("p e v h -> p (e v h)"),
                                               start=(b == 0), stop=(b == NB - 1))
                    ins.then_inc(found, 1)
                pe.wait_ge(masked_done, 1)
                for a in range(MB):
                    ins = nc.tensor.matmul(ps[:, 6 + a, :], spread, masked.rearrange("p g c -> p (g c)")
                                           [:, a * BANK:(a + 1) * BANK], start=True, stop=True)
                ins.then_inc(spread_done, 1)
                if dynamic:
                    pe.wait_ge(map_done, 1)
                    nc.tensor.transpose(ps[0:1, 0, 0:P], mp[:, 0:1], ident)
                    for a in range(2):
                        nc.tensor.transpose(ps[:, 1, a * P:(a + 1) * P],
                                            ids.rearrange("p e h -> p (e h)")[:, a * P:(a + 1) * P], ident)
                        ins = nc.tensor.transpose(ps[:, 2, a * P:(a + 1) * P], col_hot[:, a, :], ident)
                    ins.then_inc(map_turned, 1)
                    pe.wait_ge(map_taken, 1)
                    for a in range(2):
                        ins = nc.tensor.matmul(ps[:, 3, 0:n_tiles], ids_t[:, a, :], col_t[:, a, 0:n_tiles],
                                               start=(a == 0), stop=(a == 1))
                    ins.then_inc(sorted_done, 1)

            @block.sync
            def _(sp):
                by_seq = lambda t: t[0:NT].rearrange("(b t) d -> t b d", t=T)
                n = dma_all(sp, [(by_seq(table)[:, :, 0:D], xn_tok), (by_seq(table)[:, :, D:], wt),
                                 (by_seq(sums[0]), x_tok)], table_here)
                sp.wait_ge(zero_done, 1)
                z3 = zero[:, 0:D].rearrange("p (o d) -> p o d", o=1)
                n += dma_all(sp, [(table[NT:], zero), (sums[0][NT:], zero[:, 0:D]), (sums[1][NT:], zero[:, 0:D]),
                                  (by_seq(sums[1]), z3.broadcast_to([P, NB, D]))], table_here)
                sp.wait_ge(table_here, n)

        idx_here, turned, xt_taken, gu_done, silu_done, av_done, a_turned, a_taken, down_done, y_taken = map(
            sem, ("idx_here", "turned", "xt_taken", "gu_done", "silu_done", "av_done", "a_turned", "a_taken",
                  "down_done", "y_taken"))
        gathered = [sem(f"gathered{r}") for r in range(RING)]
        added = [sem("added0"), sem("added1")]
        paced = sem("paced")
        n = n_tiles
        assert n % (2 * RING) == 0 and fw <= P

        def expert(eng, i):
            return eng.value_load(tile_map[0:1, bass.ds(i, 1)], min_val=0, max_val=n_exp - 1) if dynamic else i

        with nc.Block() as block:
            @block.gpsimd
            def _(pool):
                def take_index(i, k):
                    nc.gpsimd.tensor_copy(ixb[:, k * RING:(k + 1) * RING], idx[:, bass.ds(i, RING)])\
                        .then_inc(idx_here, 1)

                def gather(r, k):
                    pool.sem_inc(paced, 1)
                    nc.gpsimd.indirect_dma_start(xe[r], None, table, bass.IndirectOffsetOnAxis(ap=ixb[:, k:k + 1], axis=0))\
                        .then_inc(gathered[r], 16)

                def add(i, r, k, before):
                    pool.wait_ge(y_taken, i + 1)
                    if not isinstance(before, int) or before:
                        pool.wait_ge(added[r % 2], before * 16)
                    pool.sem_inc(paced, 1)
                    nc.gpsimd.indirect_dma_start(sums[r % 2], bass.IndirectOffsetOnAxis(ap=ixb[:, k:k + 1], axis=0),
                                                 ye[r], None, compute_op=ALU.add)\
                        .then_inc(added[r % 2], 16)

                R2 = 2 * RING
                for k in range(R2):
                    r = k % RING
                    if r == 0:
                        take_index(k, k // RING)
                        pool.wait_ge(idx_here, k // RING + 1)
                    if k >= RING:
                        pool.wait_ge(turned, k - RING + 1)
                        pool.wait_ge(av_done, k - RING + 1)
                        pool.wait_ge(added[r % 2], ((k - RING) // 2 + 1) * 16)
                    gather(r, k)
                    if k >= LAG:
                        add(k - LAG, (k - LAG) % RING, k - LAG, (k - LAG) // 2)
                with pool.Fori(1, n // R2) as j:
                    for k in range(R2):
                        i, r = R2 * j + k, k % RING
                        if r == 0:
                            take_index(i, k // RING)
                            pool.wait_ge(idx_here, 2 * j + k // RING + 1)
                        pool.wait_ge(turned, i - RING + 1)
                        pool.wait_ge(av_done, i - RING + 1)
                        pool.wait_ge(added[r % 2], (RING * j + (k - RING) // 2 + 1) * 16)
                        gather(r, k)
                        add(i - LAG, (r - LAG) % RING, (k - LAG) % R2, RING * j + (k - LAG) // 2)
                for i in range(n - LAG, n):
                    add(i, i % RING, i % R2, i // 2)
                for q in range(2):
                    pool.wait_ge(added[q], n // 2 * 16)

            @block.tensor
            def _(pe):
                def turn(q, r, fills):
                    pe.wait_ge(gathered[r], fills * 16)
                    for k in range(KT):
                        ins = nc.tensor.transpose(ps[:, q, k * P:(k + 1) * P], xe[r][:, k * P:(k + 1) * P], ident)
                    ins.then_inc(turned, 1)

                def gate_up(i, q):
                    e = expert(pe, i)
                    pe.wait_ge(xt_taken, i + 1)
                    for k in range(KT):
                        ins = nc.tensor.matmul(ps[:, 2 + q, 0:2 * inner], xe_t[q][:, k, :],
                                               w_gu[:, bass.ds(e, 1), k, :].rearrange("p e f -> p (e f)"),
                                               start=(k == 0), stop=(k == KT - 1))
                    ins.then_inc(gu_done, 1)

                def turn_a(i, q):
                    pe.wait_ge(av_done, i + 1)
                    for f in range(f_n):
                        ins = nc.tensor.transpose(ps[0:fw, 4 + q, f * P:(f + 1) * P], av[q][:, f * fw:(f + 1) * fw], ident)
                    ins.then_inc(a_turned, 1)

                def down(i, q):
                    e = expert(pe, i)
                    pe.wait_ge(a_taken, i + 1)
                    for f in range(f_n):
                        ins = nc.tensor.matmul(ps[:, 6 + q, 0:D], av_t[q][0:fw, f, :],
                                               w_dn[0:fw, bass.ds(e, 1), f, :].rearrange("p e d -> p (e d)"),
                                               start=(f == 0), stop=(f == f_n - 1))
                    ins.then_inc(down_done, 1)

                def step(i, r, fills, first=False, last=False):
                    q = r % 2
                    gate_up(i, q)
                    turn_a(i - 1, 1 - q)
                    if not last:
                        turn(1 - q, (r + 1) % RING, fills)
                    if not first:
                        down(i - 2, q)

                turn(0, 0, 1)
                turn(1, 1, 1)
                gate_up(0, 0)
                for i in range(1, RING):
                    step(i, i, (i + 1) // RING + 1, first=(i == 1))
                with pe.Fori(1, n // RING - 1) as j:
                    for r in range(RING):
                        step(RING * j + r, r, j + 1 + (r + 1) // RING)
                for i in range(n - RING, n):
                    step(i, i % RING, (i + 1) // RING + 1, last=(i == n - 1))
                turn_a(n - 1, 1)
                down(n - 2, 0)
                down(n - 1, 1)

            @block.scalar
            def _(act):
                def gate(i, q):
                    act.wait_ge(gu_done, i + 1)
                    nc.scalar.activation(sg[q], ps[:, 2 + q, 0:inner], ACT.Silu).then_inc(silu_done, 1)

                def take_a(i, q):
                    act.wait_ge(a_turned, i + 1)
                    nc.scalar.activation(av_t[q][0:fw].rearrange("p f s -> p (f s)"), ps[0:fw, 4 + q, 0:f_n * P], ACT.Copy)\
                        .then_inc(a_taken, 1)

                def take_y(i, r):
                    act.wait_ge(down_done, i + 1)
                    nc.scalar.activation(ye[r], ps[:, 6 + r % 2, 0:D], ACT.Copy).then_inc(y_taken, 1)

                def step(i, r):
                    gate(i, r % 2)
                    take_a(i - 1, (r - 1) % 2)
                    take_y(i - 2, (r - 2) % RING)

                gate(0, 0)
                gate(1, 1)
                take_a(0, 0)
                for i in range(2, RING):
                    step(i, i)
                with act.Fori(1, n // RING) as j:
                    for r in range(RING):
                        step(RING * j + r, r)
                take_a(n - 1, 1)
                take_y(n - 2, RING - 2)
                take_y(n - 1, RING - 1)

            @block.vector
            def _(dve):
                def take(i, q):
                    dve.wait_ge(turned, i + 1)
                    nc.vector.tensor_copy(xe_t[q].rearrange("p k s -> p (k s)"), ps[:, q, 0:KT * P]).then_inc(xt_taken, 1)

                def product(i, q, r):
                    e = expert(dve, i)
                    dve.wait_ge(silu_done, i + 1)
                    nc.vector.scalar_tensor_tensor(out=av[q], in0=ps[:, 2 + q, inner:2 * inner],
                                                   scalar=xe[r][:, bass.ds(D + e, 1)], in1=sg[q],
                                                   op0=ALU.mult, op1=ALU.mult).then_inc(av_done, 1)

                take(0, 0)
                for i in range(RING):
                    take(i + 1, (i + 1) % 2)
                    product(i, i % 2, i)
                with dve.Fori(1, n // RING - 1) as j:
                    for r in range(RING):
                        take(RING * j + r + 1, (r + 1) % 2)
                        product(RING * j + r, r % 2, r)
                for i in range(n - RING, n):
                    if i < n - 1:
                        take(i + 1, (i + 1) % 2)
                    product(i, i % 2, i % RING)

        back_here, back_added = sem("back_here"), sem("back_added")
        with nc.Block() as block:
            @block.sync
            def _(sp):
                by_seq = lambda t: t[0:NT].rearrange("(b t) d -> t b d", t=T)
                dma_all(sp, [(x_tok, by_seq(sums[0])), (back, by_seq(sums[1]))], back_here)

            @block.vector
            def _(dve):
                dve.wait_ge(back_here, 32)
                nc.vector.tensor_tensor(x_tok, x_tok, back, ALU.add).then_inc(back_added, 1)



HEADS1, HD1, NS1 = 8, 64, 64
XT1 = HEADS1 * HD1 // P
RMS_EPS = 1e-5


def ssd_layer(nc, ps, sems, ident, arena_at, x_tok, small, w):
    A = Arena(arena_at.tensor)
    A.at = arena_at.at
    XC = HEADS1 * HD1
    xn_t = A.take(KT * NT).rearrange("p (k t) -> p k t", k=KT)
    w_z = A.take(KT * XC).rearrange("p (k o) -> p k o", k=KT)
    w_xbc = A.take(KT * (XC + 2 * NS1)).rearrange("p (k o) -> p k o", k=KT)
    w_dt = A.take(KT * HEADS1).rearrange("p (k o) -> p k o", k=KT)
    wo = A.take(XT1 * D).rearrange("p (i d) -> p i d", i=XT1)
    nw = A.take(XT1)
    cw = A.take((XT1 + 1) * TAPS).rearrange("p (m k) -> p m k", k=TAPS)
    cb = A.take(XT1 + 1)
    dtb, rate, skip = A.take(HEADS1), A.take(HEADS1), A.take(HEADS1)
    masks = A.take(2 * P).rearrange("p (j t) -> p j t", j=2)
    b_t, c_t = A.take(NT), A.take(NT)
    tok = lambda n: A.take(NB * n).rearrange("p (b c) -> p b c", b=NB)
    xh, zs = tok(XC), tok(XC)
    dt, da, e, g, ln = tok(HEADS1), tok(HEADS1), tok(HEADS1), tok(HEADS1), tok(HEADS1)
    sq, rstd = A.take(NB), A.take(NB)
    at0 = A.at
    xc = A.take(XT1 * NT).rearrange("p (m t) -> p m t", m=XT1)
    at1 = A.at
    pre = [A.take(NB * (T + TAPS - 1)).rearrange("p (b t) -> p b t", b=NB) for _ in range(2)]
    acc = [A.take(NT) for _ in range(2)]
    A.at = at1
    xn_tok = A.take(NB * D).rearrange("p (b d) -> p b d", d=D)
    A.at = at0
    two = lambda *d: A.take(2 * d[0] * d[1]).rearrange("p (q a c) -> p q a c", q=2, a=d[0])
    gm = two(1, T)
    seg_l, ex = two(HEADS1, T), two(HEADS1, T)
    xdt, dx, yz = two(HEADS1, HD1), two(HEADS1, HD1), two(HEADS1, HD1)
    yz_t = two(XT1, T)
    raw = A.take(NB * D).rearrange("p (b d) -> p b d", d=D)
    junk = A.take(XC)

    with ExitStack() as ctx:
        sem = sems
        w_here = sem("l1_weights")
        bc = lambda a: a.broadcast_to([P, HEADS1])
        with nc.Block() as block:
            @block.sync
            def _(sp):
                n = dma_all(sp, [(w_z, w["z"]), (w_xbc, w["xbc"]), (w_dt, w["dt"]), (wo, w["out_proj"]), (nw, w["norm_w"]),
                                 (cw, w["conv_w"]), (cb, w["conv_b"]), (dtb, bc(w["dt_bias"])), (rate, bc(w["a_log"])),
                                 (skip, bc(w["d"])), (masks, w["masks"])], w_here)
                sp.wait_ge(w_here, n)
        norm_stage(nc, ps, sems, ident, x_tok, xn_tok,
                   lambda k, c: xn_t[:, k, c * BANK:(c + 1) * BANK].rearrange("p (b t) -> p b t", t=T), small, "ssd")

        def put_x(m):
            if m < XT1:
                return [(xc[:, m, :], acc[m % 2])]
            return [(b_t[0:NS1], acc[m % 2][0:NS1]), (c_t[0:NS1], acc[m % 2][NS1:])]

        conv_stage(nc, ps, sems, xn_t, w_xbc, XT1 + 1, put_x, 0, None, cw, cb, pre, acc, "m1")

        z_done, z_taken, dtp_done, xt_done, xt_taken, dve_own, act_own, ab_done, one_e, ln_done = map(
            sem, ("z_done", "z_taken", "dt1_proj", "x1_turned", "x1_taken", "dve_own_s1", "act_own_s1",
                  "dt1_abs", "dt1_one_e", "dt1_ln"))
        v8 = lambda r: r.rearrange("p (o h) -> p o h", o=1).broadcast_to([P, NB, HEADS1])
        with nc.Block() as block:
            @block.tensor
            def _(pe):
                for b in range(NB):
                    for k in range(KT):
                        ins = nc.tensor.matmul(ps[:, 7, b * HEADS1:(b + 1) * HEADS1], xn_t[:, k, b * T:(b + 1) * T],
                                               w_dt[:, k, :], start=(k == 0), stop=(k == KT - 1))
                ins.then_inc(dtp_done, 1)
                for b in range(NB):
                    if b >= 3:
                        pe.wait_ge(z_taken, b - 2)
                    for k in range(KT):
                        ins = nc.tensor.matmul(ps[:, b % 3, :], xn_t[:, k, b * T:(b + 1) * T], w_z[:, k, :],
                                               start=(k == 0), stop=(k == KT - 1))
                    ins.then_inc(z_done, 1)
                    if b >= 3:
                        pe.wait_ge(xt_taken, b - 2)
                    for m in range(XT1):
                        ins = nc.tensor.transpose(ps[:, 3 + b % 3, m * P:(m + 1) * P], xc[:, m, b * T:(b + 1) * T], ident)
                    ins.then_inc(xt_done, 1)

            @block.scalar
            def _(act):
                own = Chain(act, act_own)
                own(nc.scalar.activation(rate, rate, ACT.Exp))
                nc.scalar.mul(rate, rate, -1.0).then_inc(ab_done, 1)
                act.wait_ge(one_e, 1)
                own(nc.scalar.activation(e, dt, ACT.Abs))
                nc.scalar.activation(e, e, ACT.Exp, scale=-1.0).then_inc(ab_done, 1)
                act.wait_ge(one_e, 2)
                nc.scalar.activation(ln, g, ACT.Ln).then_inc(ln_done, 1)
                for b in range(NB):
                    act.wait_ge(z_done, b + 1)
                    nc.scalar.activation(zs[:, b, :], ps[:, b % 3, :], ACT.Silu).then_inc(z_taken, 1)

            @block.vector
            def _(dve):
                own = Chain(dve, dve_own)
                dve.wait_ge(dtp_done, 1)
                nc.vector.tensor_tensor(dt, ps[:, 7, 0:NB * HEADS1].rearrange("p (b h) -> p b h", b=NB), v8(dtb), ALU.add)\
                    .then_inc(one_e, 1)
                dve.wait_ge(ab_done, 2)
                nc.vector.tensor_scalar(g, e, 1.0, None, ALU.add).then_inc(one_e, 1)
                dve.wait_ge(one_e, 2)
                own(nc.vector.scalar_tensor_tensor(out=e, in0=g, scalar=1.0, in1=e, op0=ALU.subtract, op1=ALU.subtract))
                dve.wait_ge(ln_done, 1)
                own(nc.vector.tensor_tensor(ln, ln, e, ALU.subtract))
                own(nc.vector.scalar_tensor_tensor(out=dt, in0=dt, scalar=0.0, in1=ln, op0=ALU.max, op1=ALU.add))
                own(nc.vector.tensor_tensor(da, dt, v8(rate), ALU.mult))
                for m in range(XT1):
                    own(nc.vector.tensor_scalar(wo[:, m, :], wo[:, m, :], nw[:, m:m + 1], None, ALU.mult))
                for b in range(NB):
                    dve.wait_ge(xt_done, b + 1)
                    nc.vector.tensor_copy(xh[:, b, :], ps[:, 3 + b % 3, :]).then_inc(xt_taken, 1)

        g_done, gm_done, lm_done, xd_done, dx_done, seg_done, ex_done, m_done, y_done, yz_done, sq_done, t_done, \
            t_taken, o_done, o_taken = map(sem, (
                "cb_done", "cb_masked", "seg_left", "xdt_done", "skip_done", "seg_done", "seg_exp", "mix_done", "ssd_y",
                "ssd_gated", "ssd_square", "ssd_turned", "ssd_turn_taken", "ssd_out", "ssd_out_taken"))
        flat = lambda r: r.rearrange("p a c -> p (a c)")
        with nc.Block() as block:
            @block.gpsimd
            def _(pool):
                for b in range(NB):
                    q = b % 2
                    if b >= 2:
                        pool.wait_ge(seg_done, b - 1)
                    nc.gpsimd.tensor_tensor(seg_l[:, q], masks[:, 0:1, :].broadcast_to([P, HEADS1, T]),
                                            da[:, b, :].rearrange("p (h o) -> p h o", o=1).broadcast_to([P, HEADS1, T]),
                                            ALU.mult).then_inc(lm_done, 1)
                    if b >= 2:
                        pool.wait_ge(y_done, b - 1)
                    x3 = xh[:, b, :].rearrange("p (h d) -> p h d", h=HEADS1)
                    nc.gpsimd.tensor_tensor(xdt[:, q], x3, dt[:, b, :].rearrange("p (h o) -> p h o", o=1)
                                            .broadcast_to([P, HEADS1, HD1]), ALU.mult).then_inc(xd_done, 1)
                    if b >= 2:
                        pool.wait_ge(yz_done, 2 * (b - 2) + 1)
                    nc.gpsimd.tensor_tensor(dx[:, q], x3, skip.rearrange("p (h o) -> p h o", o=1)
                                            .broadcast_to([P, HEADS1, HD1]), ALU.mult).then_inc(dx_done, 1)

            @block.tensor
            def _(pe):
                def scores(b):
                    q = b % 2
                    if b >= 1:
                        pe.wait_ge(gm_done, b)
                    nc.tensor.matmul(ps[:, 0, q * T:(q + 1) * T], b_t[0:NS1, b * T:(b + 1) * T],
                                     c_t[0:NS1, b * T:(b + 1) * T], start=True, stop=True).then_inc(g_done, 1)
                    pe.wait_ge(lm_done, b + 1)
                    if b >= 2:
                        pe.wait_ge(ex_done, b - 1)
                    for h in range(HEADS1):
                        ins = nc.tensor.matmul(ps[:, 1 + 2 * q + h // 4, (h % 4) * T:(h % 4 + 1) * T], seg_l[:, q, h, :],
                                               masks[:, 1, :], start=True, stop=True)
                    ins.then_inc(seg_done, 1)

                def mix(b):
                    q = b % 2
                    pe.wait_ge(m_done, b + 1)
                    pe.wait_ge(xd_done, b + 1)
                    if b >= 1:
                        pe.wait_ge(yz_done, 2 * (b - 1) + 1)
                    for h in range(HEADS1):
                        ins = nc.tensor.matmul(ps[:, 5, h * HD1:(h + 1) * HD1], ex[:, q, h, :], xdt[:, q, h, :],
                                               start=True, stop=True)
                    ins.then_inc(y_done, 1)

                def project(b):
                    q = b % 2
                    pe.wait_ge(yz_done, 2 * b + 2)
                    if b >= 1:
                        pe.wait_ge(t_taken, b)
                    for m in range(XT1):
                        ins = nc.tensor.transpose(ps[:, 6, m * P:(m + 1) * P], flat(yz[:, q])[:, m * P:(m + 1) * P], ident)
                    ins.then_inc(t_done, 1)
                    pe.wait_ge(t_taken, b + 1)
                    if b >= 1:
                        pe.wait_ge(o_taken, b)
                    for m in range(XT1):
                        ins = nc.tensor.matmul(ps[:, 7, q * D:(q + 1) * D], yz_t[:, q, m, :], wo[:, m, :],
                                               start=(m == 0), stop=(m == XT1 - 1))
                    ins.then_inc(o_done, 1)
                for s in range(NB + 2):
                    if s < NB:
                        scores(s)
                    if 1 <= s <= NB:
                        mix(s - 1)
                    if s >= 2:
                        project(s - 2)

            @block.scalar
            def _(act):
                for s in range(NB + 2):
                    if s < NB:
                        act.wait_ge(seg_done, s + 1)
                        if s >= 2:
                            act.wait_ge(y_done, s - 1)
                        nc.scalar.activation(flat(ex[:, s % 2]),
                                             ps[:, 1 + 2 * (s % 2):3 + 2 * (s % 2), :].rearrange("p a c -> p (a c)"),
                                             ACT.Exp).then_inc(ex_done, 1)
                    if s >= 2:
                        b = s - 2
                        act.wait_ge(yz_done, 2 * b + 2)
                        if b >= 1:
                            act.wait_ge(sq_done, b)
                        nc.scalar.activation(junk, flat(yz[:, b % 2]), ACT.Square, accum_out=sq[:, b:b + 1])\
                            .then_inc(sq_done, 1)
                        act.wait_ge(t_done, b + 1)
                        if b >= 2:
                            act.wait_ge(o_done, b - 1)
                        nc.scalar.activation(flat(yz_t[:, b % 2]), ps[:, 6, :], ACT.Copy).then_inc(t_taken, 1)

            @block.vector
            def _(dve):
                for s in range(NB + 2):
                    if s < NB:
                        q = s % 2
                        dve.wait_ge(g_done, s + 1)
                        if s >= 2:
                            dve.wait_ge(m_done, s - 1)
                        nc.vector.tensor_tensor(gm[:, q, 0, :], ps[:, 0, q * T:(q + 1) * T], masks[:, 1, :], ALU.mult)\
                            .then_inc(gm_done, 1)
                        dve.wait_ge(gm_done, s + 1)
                        dve.wait_ge(ex_done, s + 1)
                        nc.vector.tensor_tensor(ex[:, q], ex[:, q], gm[:, q].broadcast_to([P, HEADS1, T]), ALU.mult)\
                            .then_inc(m_done, 1)
                    if 1 <= s <= NB:
                        b, q = s - 1, (s - 1) % 2
                        dve.wait_ge(y_done, b + 1)
                        dve.wait_ge(dx_done, b + 1)
                        if b >= 2:
                            dve.wait_ge(t_done, b - 1)
                            dve.wait_ge(sq_done, b - 1)
                        nc.vector.tensor_tensor(flat(yz[:, q]), ps[:, 5, :], flat(dx[:, q]), ALU.add).then_inc(yz_done, 1)
                        dve.wait_ge(yz_done, 2 * b + 1)
                        nc.vector.tensor_tensor(flat(yz[:, q]), flat(yz[:, q]), zs[:, b, :], ALU.mult).then_inc(yz_done, 1)
                    if s >= 2:
                        b = s - 2
                        dve.wait_ge(o_done, b + 1)
                        nc.vector.tensor_copy(raw[:, b, :], ps[:, 7, (b % 2) * D:(b % 2 + 1) * D]).then_inc(o_taken, 1)

        var_done, std_done, own_sem = sem("rms_var"), sem("rms_std"), sem("dve_own_rms")
        with nc.Block() as block:
            @block.vector
            def _(dve):
                own = Chain(dve, own_sem)
                nc.vector.tensor_scalar(sq, sq, 1.0 / XC, RMS_EPS, ALU.mult, ALU.add).then_inc(var_done, 1)
                dve.wait_ge(std_done, 1)
                own(nc.vector.reciprocal(rstd, sq))
                for b in range(NB):
                    ins = nc.vector.scalar_tensor_tensor(out=x_tok[:, b, :], in0=raw[:, b, :], scalar=rstd[:, b:b + 1],
                                                         in1=x_tok[:, b, :], op0=ALU.mult, op1=ALU.add)
                own(ins)

            @block.scalar
            def _(act):
                act.wait_ge(var_done, 1)
                nc.scalar.activation(sq, sq, ACT.Sqrt).then_inc(std_done, 1)


HEADS2, HD2 = 16, 8


def longconv_layer(nc, ps, sems, ident, arena_at, x_tok, small, w):
    A = Arena(arena_at.tensor)
    A.at = arena_at.at
    PAIRS = HD2 * HD2
    xn_tok = A.take(NB * D).rearrange("p (b d) -> p b d", d=D)
    q_t = A.take(KT * NT).rearrange("p (k h i b) -> p k h i b", k=KT, h=HEADS2, i=HD2)
    c_rev = A.take(KT * NT).rearrange("p (k h i b) -> p k h i b", k=KT, h=HEADS2, i=HD2)
    toep = A.take(HEADS2 * 2 * P).rearrange("p (h m) -> p h m", h=HEADS2)
    kv = A.take(2 * KT * PAIRS * NB).rearrange("p (q k i j b) -> p q k i j b", q=2, k=KT, i=HD2, j=HD2)
    prod = A.take(2 * PAIRS * NB).rearrange("p (q i j b) -> p q i j b", q=2, i=HD2, j=HD2)
    y_t = A.take(KT * NT).rearrange("p (k h n) -> p k h n", k=KT, h=HEADS2)
    skip = A.take(HEADS2)
    anti = A.take(P)
    with ExitStack() as ctx:
        sem = sems
        w_here = sem("conv_here")
        src = w["kernel"]
        toep_src = bass.AP(tensor=src.tensor, offset=0, ap=[[1, P], [src.shape[1], HEADS2], [1, 2 * P]])
        with nc.Block() as block:
            @block.sync
            def _(sp):
                n = dma_all(sp, [(c_rev.rearrange("p k h i b -> p k (h i b)"), w["ctx_rev"]), (toep, toep_src),
                                 (skip, w["d"].broadcast_to([P, HEADS2])), (anti, w["anti"])], w_here)
                sp.wait_ge(w_here, n)
        norm_stage(nc, ps, sems, ident, x_tok, xn_tok,
                   lambda k, c: q_t[:, k].rearrange("p h i b -> p b (h i)")[:, c * BPC:(c + 1) * BPC, :], small, "conv")
        diag_done, kv_done, conv_done, prod_done, red_done = map(
            sem, ("toep_diag", "kv_done", "lconv_done", "lprod_done", "lred_done"))
        with nc.Block() as block:
            @block.gpsimd
            def _(pool):
                for h in range(HEADS2):
                    if h >= 2:
                        pool.wait_ge(conv_done, KT * (h - 1))
                    for k in range(KT):
                        c = c_rev[:, k, h]
                        nc.gpsimd.tensor_tensor(
                            kv[:, h % 2, k],
                            c.rearrange("p i (o b) -> p i o b", o=1).broadcast_to([P, HD2, HD2, NB]),
                            c.rearrange("p (o j) b -> p o j b", o=1).broadcast_to([P, HD2, HD2, NB]), ALU.mult)\
                            .then_inc(kv_done, 1)

            @block.tensor
            def _(pe):
                for h in range(HEADS2):
                    pe.wait_ge(kv_done, KT * (h + 1))
                    pe.wait_ge(diag_done, h + 1)
                    for l in range(KT):
                        s = KT * h + l
                        if s >= 4:
                            pe.wait_ge(prod_done, s - 3)
                        for a in range(2):
                            for k in range(l + 1):
                                mv = kv[:, h % 2, k, a * 4:(a + 1) * 4].rearrange("p i j b -> p (i j b)")
                                ins = nc.tensor.matmul(ps[:, 2 * (s % 4) + a, :], toep[:, h, (l - k) * P:(l - k + 1) * P],
                                                       mv, start=(k == 0), stop=(k == l))
                        ins.then_inc(conv_done, 1)

            @block.vector
            def _(dve):
                for h in range(HEADS2):
                    nc.vector.scalar_tensor_tensor(out=toep[:, h, 0:P], in0=anti, scalar=skip[:, h:h + 1],
                                                   in1=toep[:, h, 0:P], op0=ALU.mult, op1=ALU.add).then_inc(diag_done, 1)
                for h in range(HEADS2):
                    for l in range(KT):
                        s = KT * h + l
                        dve.wait_ge(conv_done, s + 1)
                        if s >= 2:
                            dve.wait_ge(red_done, s - 1)
                        banks = ps[:, 2 * (s % 4):2 * (s % 4) + 2, :].rearrange("p a (i j b) -> p (a i) j b", j=HD2, b=NB)
                        qv = q_t[:, l, h].rearrange("p i (o b) -> p i o b", o=1).broadcast_to([P, HD2, HD2, NB])
                        nc.vector.tensor_tensor(prod[:, s % 2], banks, qv, ALU.mult).then_inc(prod_done, 1)
                        dve.wait_ge(prod_done, s + 1)
                        nc.vector.tensor_reduce(y_t[:, l, h, :], prod[:, s % 2].rearrange("p i j b -> p (j b) i"),
                                                AX.X, ALU.add).then_inc(red_done, 1)
        add_transposed_stage(nc, ps, sems, ident, x_tok,
                             lambda k, b: y_t[:, k].rearrange("p h (j b) -> p b (h j)", b=NB)[:, b, :], "conv")


def ffn1_layer(nc, ps, sems, ident, arena_at, x_tok, small, w):
    A = Arena(arena_at.tensor)
    A.at = arena_at.at
    C, CP, fw = E1, 24, I1 // 2
    BLOCKS, TILES = NT // P, K1 * NT // P + E1
    w_gu = A.take(E1 * KT * 2 * I1).rearrange("p (e k f) -> p e k f", e=E1, k=KT)
    w_dn = A.take(E1 * 2 * D).rearrange("p (e f d) -> p e f d", e=E1, f=2)
    cst = A.take(CONST)
    mask16 = A.take(P).bitcast(BF16).rearrange("p (j t) -> p j t", j=2)
    xn_tok = A.take(NB * D).rearrange("p (b d) -> p b d", d=D)
    xn_t = A.take(KT * NT).rearrange("p (k t) -> p k t", k=KT)
    wr = A.take(KT * C).rearrange("p (k c) -> p k c", k=KT)
    bias = A.take(C)
    tok = lambda n: A.take(NB * n).rearrange("p (b c) -> p b c", b=NB)
    sc, left, top8, wt, row, row2, place = tok(CP), tok(CP), tok(8), tok(C), tok(1), tok(1), tok(C)
    ch16, before = (A.take(NB * C // 2).bitcast(BF16).rearrange("p (b c) -> p b c", b=NB) for _ in range(2))
    all16 = A.take(C // 2).bitcast(BF16)
    queue = A.take(C)
    with ExitStack() as ctx:
        sem = sems
        w_here, experts_here, dve_own = sem("r1_here"), sem("experts1_here"), sem("dve_own_r1")
        with nc.Block() as block:
            @block.sync
            def _(sp):
                n = dma_all(sp, [(wr, w["cls"]), (bias, w["bias"].broadcast_to([P, C])), (mask16, w["mask16"]),
                                 (cst, w["const"])], w_here)
                dma_all(sp, [(w_gu, w["gate_up"]), (w_dn[0:fw], w["down"])], experts_here)
                sp.wait_ge(w_here, n)
        norm_stage(nc, ps, sems, ident, x_tok, xn_tok,
                   lambda k, c: xn_t[:, k, c * BANK:(c + 1) * BANK].rearrange("p (b t) -> p b t", t=T),
                   small, "ffn1")
        logit_done, shifted, exp_done, prefix_done, pos_done = map(
            sem, ("r1_logit", "r1_shift", "r1_exp", "r1_prefix", "r1_pos"))
        with nc.Block() as block:
            @block.tensor
            def _(pe):
                for b in range(NB):
                    for k in range(KT):
                        ins = nc.tensor.matmul(ps[:, 0, b * C:(b + 1) * C], xn_t[:, k, b * T:(b + 1) * T], wr[:, k, :],
                                               start=(k == 0), stop=(k == KT - 1))
                ins.then_inc(logit_done, 1)
                pe.wait_ge(prefix_done, 1)
                places = ps[:, 2, 0:NB * C]
                nc.tensor.matmul(places, mask16[:, 0, :], ch16.rearrange("p b c -> p (b c)"), start=True, stop=False)
                nc.tensor.matmul(places, mask16[:, 1, :], before.rearrange("p b c -> p (b c)"), start=False, stop=True)
                nc.tensor.matmul(ps[:, 3, 0:C], mask16[:, 1, :], all16, start=True, stop=True).then_inc(pos_done, 1)

            @block.scalar
            def _(act):
                act.wait_ge(shifted, 1)
                nc.scalar.activation(wt, wt, ACT.Exp).then_inc(exp_done, 1)

            @block.vector
            def _(dve):
                own = Chain(dve, dve_own)
                dve.wait_ge(logit_done, 1)
                over = lambda r: r.broadcast_to([P, NB, C])
                own(nc.vector.tensor_tensor(wt, ps[:, 0, 0:NB * C].rearrange("p (b c) -> p b c", b=NB),
                                            bias.rearrange("p (o c) -> p o c", o=1).broadcast_to([P, NB, C]), ALU.add))
                own(nc.vector.tensor_reduce(row, wt, AX.X, ALU.max))
                nc.vector.tensor_tensor(wt, wt, over(row), ALU.subtract).then_inc(shifted, 1)
                own(nc.vector.memset(sc[:, :, C:], -1.0))
                dve.wait_ge(exp_done, 1)
                own(nc.vector.tensor_reduce(row2, wt, AX.X, ALU.add))
                own(nc.vector.reciprocal(row, row2))
                own(nc.vector.tensor_tensor(sc[:, :, 0:C], wt, over(row), ALU.mult))
                for b in range(NB):
                    ins = nc.vector.max(top8[:, b, :], sc[:, b, :])
                own(ins)
                own(nc.vector.memset(top8[:, :, K1:], -1.0))
                for b in range(NB):
                    ins = nc.vector.match_replace(left[:, b, :], top8[:, b, :], sc[:, b, :], -2.0)
                own(ins)
                own(nc.vector.tensor_tensor(left, left, sc, ALU.not_equal))
                own(nc.vector.tensor_copy(ch16, left[:, :, 0:C]))
                own(nc.vector.memset(before[:, 0, :], 0.0))
                for b in range(1, NB):
                    own(nc.vector.tensor_tensor(before[:, b, :], before[:, b - 1, :], ch16[:, b - 1, :], ALU.add))
                nc.vector.tensor_tensor(all16, before[:, NB - 1, :], ch16[:, NB - 1, :], ALU.add).then_inc(prefix_done, 1)
                own(nc.vector.tensor_tensor(wt, sc[:, :, 0:C], left[:, :, 0:C], ALU.mult))
                own(nc.vector.tensor_reduce(row2, wt, AX.X, ALU.add))
                own(nc.vector.reciprocal(row, row2))
                own(nc.vector.tensor_tensor(wt, wt, over(row), ALU.mult))
                dve.wait_ge(pos_done, 1)
                own(nc.vector.scalar_tensor_tensor(out=place, in0=ps[:, 2, 0:NB * C].rearrange("p (b c) -> p b c", b=NB),
                                                   scalar=1.0, in1=left[:, :, 0:C], op0=ALU.add, op1=ALU.mult))
                own(nc.vector.tensor_scalar(place, place, -1.0, None, ALU.add))
                own(nc.vector.tensor_copy(queue, ps[:, 3, 0:C]))

            @block.sync
            def _(sp):
                sp.wait_ge(experts_here, 32)
        sparse_experts(nc, ps, sems, ident, A, x_tok, xn_tok, wt, place, E1, BLOCKS, TILES, H1, I1, 2,
                       {"w_gu": w_gu, "w_dn": w_dn, "dummy": cst[:, 1:2], "spare": xn_t.rearrange("p k t -> p (k t)"), "queue": queue}, expert_const(cst), "e1")


def build(nc, ins, out):
    with ExitStack() as ctx:
        sbuf = ctx.enter_context(nc.sbuf_tensor("sbuf", [P, 52900], F32))
        ps = ctx.enter_context(nc.psum_tensor("ps", [P, NBANK, BANK], F32))
        A = Arena(sbuf)
        ident = A.take(P)
        small = A.take(176)
        x_tok = A.take(NB * D).rearrange("p (b d) -> p b d", d=D)
        sems = Semaphores(nc)
        in_here = nc.alloc_semaphore(name="in_here")
        stored = nc.alloc_semaphore(name="stored")
        with nc.Block() as block:
            @block.sync
            def _(sp):
                n = dma_all(sp, [(x_tok, ins["x"].rearrange("b t d -> t b d")), (ident, ins["ident"])], in_here)
                sp.wait_ge(in_here, n)
        scan_layer(nc, ps, sems, ident, A, x_tok, small, {k[3:]: v for k, v in ins.items() if k.startswith("m0_")})
        sems.clear()
        wkv_layer(nc, ps, sems, ident, A, x_tok, small, {k[3:]: v for k, v in ins.items() if k.startswith("c0_")})
        sems.clear()
        ffn0_layer(nc, ps, sems, ident, A, x_tok, small, {k[3:]: v for k, v in ins.items() if k.startswith("f0_")})
        sems.clear()
        ssd_layer(nc, ps, sems, ident, A, x_tok, small, {k[3:]: v for k, v in ins.items() if k.startswith("m1_")})
        sems.clear()
        longconv_layer(nc, ps, sems, ident, A, x_tok, small, {k[3:]: v for k, v in ins.items() if k.startswith("c1_")})
        sems.clear()
        ffn1_layer(nc, ps, sems, ident, A, x_tok, small, {k[3:]: v for k, v in ins.items() if k.startswith("f1_")})
        with nc.Block() as block:
            @block.sync
            def _(sp):
                sp.dma_start(out.rearrange("b t d -> t b d"), x_tok).then_inc(stored, 16)
                sp.wait_ge(stored, 16)


def _layout(inputs):
    import numpy as np

    def tiles(a):
        return a.reshape(-1, P, a.shape[-1]).transpose(1, 0, 2)

    g = {k: np.asarray(v) for k, v in inputs.items()}
    o = {"x": g["x"], "ident": np.eye(P, dtype=np.float32)}
    w = g["L0_attn_in_proj_w"].reshape(INNER, 2, D)
    o["m0_in_proj"] = tiles(np.concatenate([w[:, 0].T, w[:, 1].T], axis=1))
    o["m0_conv_w"] = tiles(g["L0_attn_conv_w"])
    o["m0_conv_b"] = g["L0_attn_conv_b"].reshape(MT, P).T
    xp = g["L0_attn_x_proj_weight"].transpose(0, 2, 1).reshape(INNER, RANK + BC)
    o["m0_x_dt"] = tiles(xp[:, :RANK])
    o["m0_x_bc"] = tiles(xp[:, RANK:])
    o["m0_dt_proj"] = g["L0_attn_dt_proj_weight"].transpose(2, 0, 1).reshape(RANK, MT, P)
    o["m0_dt_bias"] = g["L0_attn_dt_proj_bias"].reshape(MT, P).T
    o["m0_a_log"] = g["L0_attn_A_log"].reshape(HEADS0, MH, P, NS).transpose(2, 0, 1, 3).reshape(P, HEADS0, MH * NS)
    o["m0_d"] = g["L0_attn_D"].reshape(HEADS0, MH, P).transpose(2, 0, 1)
    o["m0_out_proj"] = tiles(g["L0_attn_out_proj_w"].T)
    rows = np.arange(3 * BC)[:, None, None] % BC == np.arange(BC)[None, :, None]
    sel = np.zeros((P, BC, P), "bfloat16")
    sel[:3 * BC] = rows
    o["m0_sel"] = sel
    ctx = g["ctx_2048"].reshape(NT, D)
    o["c0_ctx_t"] = tiles(ctx.T)
    o["c0_decay"] = g["L0_xattn_time_decay"].reshape(KT, P).T
    o["c0_first"] = g["L0_xattn_time_first"].reshape(KT, P).T
    o["f0_cls"] = tiles(g["L0_ffn_w_cls"].T)
    o["f0_bias"] = g["L0_ffn_bias"].reshape(1, -1)
    before = np.arange(P)[:, None] < np.arange(P)[None, :]
    o["f0_mask16"] = np.stack([before, np.ones((P, P))], axis=1).astype("bfloat16")
    o["f0_gate_up"] = g["L0_ffn_w_gate_up"].reshape(E0, KT, P, 2 * I0).transpose(2, 0, 1, 3)
    o["f0_down"] = g["L0_ffn_w_down"].reshape(E0, 1, I0, D).transpose(2, 0, 1, 3)
    def expert_table(up_values, blocks):
        low_values, part = P // up_values, np.arange(P)
        const = np.zeros((P, CONST), np.float32)
        const[:, 0] = part
        const[:, 1] = part + NT + P
        const[:, 2:19] = np.arange(17) * P
        const[:, 20:20 + P] = part
        cols = part // (2 * blocks * low_values)
        const[:, 20 + P:20 + 2 * P] = (part // up_values)[:, None] == cols
        const[:, 20 + 2 * P:20 + 3 * P] = (part % up_values)[:, None] == part // low_values
        const[:, 20 + 3 * P:20 + 3 * P + low_values] = (part % low_values)[:, None] == np.arange(low_values)
        return const

    o["f0_const"] = expert_table(H0, 1)
    o["f1_const"] = expert_table(H1, NT // P)
    win = g["L1_attn_W_in"]
    xc = HEADS1 * HD1
    o["m1_z"] = tiles(win[:xc].T)
    o["m1_xbc"] = tiles(win[xc:2 * xc + 2 * NS1].T)
    o["m1_dt"] = tiles(win[2 * xc + 2 * NS1:].T)
    o["m1_out_proj"] = tiles(g["L1_attn_W_out"].T)
    o["m1_norm_w"] = g["L1_attn_norm_w"].reshape(XT1, P).T
    o["m1_conv_w"] = tiles(g["L1_attn_conv_w"])
    o["m1_conv_b"] = g["L1_attn_conv_b"].reshape(XT1 + 1, P).T
    for name, key in (("dt_bias", "dt_bias"), ("a_log", "A_log"), ("d", "D")):
        o[f"m1_{name}"] = g[f"L1_attn_{key}"].reshape(1, -1)
    lower = np.arange(P)[:, None] > np.arange(P)[None, :]
    o["m1_masks"] = np.stack([lower, ~lower], axis=1).astype(np.float32)
    o["c1_ctx_rev"] = g["ctx_2048"].transpose(2, 1, 0).reshape(KT, P, NT)[:, ::-1].transpose(1, 0, 2)
    o["c1_kernel"] = np.pad(g["L1_xattn_ssm_kernel"], ((0, 0), (P - 1, 0)))
    o["c1_d"] = g["L1_xattn_D"].reshape(1, -1)
    o["c1_anti"] = np.eye(P, dtype=np.float32)[::-1]
    o["f1_cls"] = tiles(g["L1_ffn_router_w"].T)
    o["f1_bias"] = g["L1_ffn_expert_bias"].reshape(1, -1)
    gu = np.concatenate([g["L1_ffn_gate_proj"], g["L1_ffn_up_proj"]], axis=2)
    o["f1_gate_up"] = gu.reshape(E1, KT, P, 2 * I1).transpose(2, 0, 1, 3)
    o["f1_down"] = g["L1_ffn_down_proj"].reshape(E1, 2, I1 // 2, D).transpose(2, 0, 1, 3)
    o["f1_mask16"] = o["f0_mask16"]
    return {k: np.ascontiguousarray(v) for k, v in o.items()}


def kernel(**inputs):
    import numpy as np
    import concourse.bacc as _bacc
    from concourse.bass_utils import run_bass_kernel_spmd as _run

    nc = _bacc.Bacc("TRN2", target_bir_lowering=False, num_devices=1)
    arrays = _layout(inputs)
    aps = {k: nc.dram_tensor(f"in_{k}", a.shape, mybir.dt.from_np(a.dtype), kind="ExternalInput").ap()
           for k, a in arrays.items()}
    out = nc.dram_tensor("out", (NB, T, D), F32, kind="ExternalOutput").ap()
    build(nc, aps, out)
    got = _run(nc, [{f"in_{k}": a for k, a in arrays.items()}], core_ids=[0])
    return got.results[0]["out"]
```

```python
from contextlib import ExitStack

import concourse.bass as bass
from concourse import mybir

F32 = mybir.dt.float32
BF16 = mybir.dt.bfloat16
ALU = mybir.AluOpType
ACT = mybir.ActivationFunctionType
AX = mybir.AxisListType

P = 128
NB = 16
T = 128
D = 256
KT = D // P
NT = NB * T
TP = T + 1
BANK = 512
NBANK = 8
CH = NT // BANK
BPC = BANK // T
LN_EPS = 1e-5
BIG = 1.0e25

INNER = 512
MT = INNER // P
HEADS0 = 2
MH = MT // HEADS0
NS = 16
RANK = 128
TAPS = 4
PASSES = HEADS0 * CH
RING0 = 8
BC = 2 * NS


class Chain:

    def __init__(self, eng, sem):
        self.eng, self.sem, self.n = eng, sem, 0

    def __call__(self, ins):
        ins.then_inc(self.sem, 1)
        self.n += 1
        self.eng.wait_ge(self.sem, self.n)


class Semaphores:

    def __init__(self, nc):
        self.nc, self.held = nc, []

    def __call__(self, name):
        self.held.append(self.nc.alloc_semaphore(name=name))
        return self.held[-1]

    def clear(self):
        self.nc.clear_and_free_semaphores(self.held)
        self.held = []
        with self.nc.Block():
            pass


class Arena:

    def __init__(self, tensor):
        self.tensor, self.at = tensor, 0

    def take(self, words):
        self.at += words
        assert self.at <= self.tensor.shape[1], self.at
        return self.tensor[:, self.at - words:self.at]


def dma_all(eng, pairs, sem):
    for dst, src in pairs:
        eng.dma_start(dst, src).then_inc(sem, 16)
    return 16 * len(pairs)


def norm_stage(nc, ps, sems, ident, x_tok, xn_tok, xn_cols, small, tag, load):
    with ExitStack() as ctx:
        sem = lambda n: sems(f"{n}_{tag}")
        stats_done, std_done, xn_done, xt_done, xt_copied = map(sem, ("stats", "std", "xn", "xt", "xtc"))
        dve_own = sem("dve_own_ln")
        stats = small[:, 0:NB * 6].rearrange("p (b s) -> p b s", s=6)
        mv = small[:, 96:96 + NB * 2].rearrange("p (b s) -> p b s", s=2)
        std = small[:, 128:128 + NB]
        rstd = small[:, 144:144 + NB]
        eps = small[:, 160:161]
        block = ctx.enter_context(nc.Block())

        @block.sync
        def _(sp):
            load(sp)

        @block.vector
        def _(dve):
            chain = Chain(dve, dve_own)
            nc.vector.memset(eps, LN_EPS).then_inc(stats_done, 1)
            for b in range(NB):
                ins = nc.vector.bn_stats(stats[:, b, :], x_tok[:, b, :])
            chain(ins)
            for b in range(NB):
                ins = nc.vector.bn_aggr(mv[:, b, :], stats[:, b, :])
            ins.then_inc(stats_done, 1)
            dve.wait_ge(std_done, 1)
            chain(nc.vector.reciprocal(rstd, std))
            for b in range(NB):
                nc.vector.tensor_scalar(xn_tok[:, b, :], x_tok[:, b, :], mv[:, b, 0:1], rstd[:, b:b + 1],
                                        ALU.subtract, ALU.mult).then_inc(xn_done, 1)

        @block.scalar
        def _(act):
            act.wait_ge(stats_done, 2)
            nc.scalar.activation(std, mv[:, :, 1], ACT.Sqrt, bias=eps).then_inc(std_done, 1)
            for c in range(CH):
                for k in range(KT):
                    act.wait_ge(xt_done, c * KT + k + 1)
                    nc.scalar.activation(xn_cols(k, c), ps[:, c * KT + k, :].rearrange("p (b t) -> p b t", t=T),
                                         ACT.Copy).then_inc(xt_copied, 1)

        @block.tensor
        def _(pe):
            for c in range(CH):
                pe.wait_ge(xn_done, (c + 1) * BPC)
                for k in range(KT):
                    for j in range(BPC):
                        ins = nc.tensor.transpose(ps[:, c * KT + k, j * T:(j + 1) * T],
                                                  xn_tok[:, c * BPC + j, k * P:(k + 1) * P], ident)
                    ins.then_inc(xt_done, 1)


def add_transposed_stage(nc, ps, sems, ident, x_tok, y_cols, tag):
    with ExitStack() as ctx:
        turned = sems(f"turned_{tag}")
        added = sems(f"added_{tag}")
        block = ctx.enter_context(nc.Block())

        @block.tensor
        def _(pe):
            for b in range(NB):
                for k in range(KT):
                    ins = nc.tensor.transpose(ps[:, b // 2, (b % 2) * D + k * P:(b % 2) * D + (k + 1) * P],
                                              y_cols(k, b), ident)
                if b % 2:
                    ins.then_inc(turned, 1)

        @block.vector
        def _(dve):
            for g in range(NB // 2):
                dve.wait_ge(turned, g + 1)
                xs = x_tok[:, 2 * g:2 * g + 2, :].rearrange("p b d -> p (b d)")
                nc.vector.tensor_tensor(xs, ps[:, g, :], xs, ALU.add).then_inc(added, 1)


def conv_stage(nc, ps, sems, xn_t, w_in, nx, put_x, ng, put_gate, cw, cb, pre, acc, tag, z=None):
    with ExitStack() as ctx:
        sem = lambda n: sems(f"{n}_{tag}")
        proj_done, pre_copied, gate_done, conv_done, xs_done, pads_zero = map(
            sem, ("proj_done", "pre_copied", "gate_done", "conv_done", "xs_done", "pads_zero"))
        block = ctx.enter_context(nc.Block())

        @block.tensor
        def _(pe):
            for m in range(nx + ng):
                for c in range(CH):
                    if m >= 2:
                        n = (m - 2) * CH + c + 1
                        if m - 2 < nx:
                            pe.wait_ge(pre_copied, n)
                        else:
                            pe.wait_ge(gate_done, n - nx * CH)
                    for k in range(KT):
                        ins = nc.tensor.matmul(ps[:, (m % 2) * CH + c, :], w_in[:, k, m * P:(m + 1) * P],
                                               xn_t[:, k, c * BANK:(c + 1) * BANK],
                                               start=(k == 0), stop=(k == KT - 1))
                    ins.then_inc(proj_done, 1)

            if z is not None:
                w_z, _, w_dt, z_done, z_taken, dt_there = z
                pe.wait_ge(pre_copied, (nx - 1) * CH)
                for b in range(NB):
                    if b >= 3:
                        pe.wait_ge(z_taken, b - 2)
                    for dst, w, done in ((ps[:, 4 + b % 3, :], w_z, z_done),
                                         (ps[:, 7, b * HEADS1:(b + 1) * HEADS1], w_dt, dt_there)):
                        for k in range(KT):
                            ins = nc.tensor.matmul(dst, xn_t[:, k, b * T:(b + 1) * T], w[:, k, :],
                                                   start=(k == 0), stop=(k == KT - 1))
                        ins.then_inc(done, 1)

        @block.scalar
        def _(act):
            act.wait_ge(pads_zero, 2)

            def take_x(m):
                for c in range(CH):
                    act.wait_ge(proj_done, m * CH + c + 1)
                    bank = ps[:, (m % 2) * CH + c, :]
                    nc.scalar.activation(pre[m % 2][:, c * BPC:(c + 1) * BPC, TAPS - 1:],
                                         bank.rearrange("p (b t) -> p b t", t=T), ACT.Copy)
                    nc.scalar.activation(acc[m % 2][:, c * BANK:(c + 1) * BANK], bank, ACT.Identity,
                                         scale=cw[:, m, TAPS - 1:TAPS], bias=cb[:, m:m + 1])\
                        .then_inc(pre_copied, 1)

            def silu_x(m):
                act.wait_ge(conv_done, (TAPS - 1) * (m + 1))
                for dst, src in put_x(m):
                    ins = nc.scalar.activation(dst, src, ACT.Silu)
                ins.then_inc(xs_done, 1)

            def take_gate(m):
                for c in range(CH):
                    act.wait_ge(proj_done, (nx + m) * CH + c + 1)
                    nc.scalar.activation(put_gate(m, c), ps[:, ((nx + m) % 2) * CH + c, :], ACT.Silu)\
                        .then_inc(gate_done, 1)

            def take_z(b):
                act.wait_ge(z[3], b + 1)
                nc.scalar.activation(z[1][:, b, :], ps[:, 4 + b % 3, :], ACT.Silu).then_inc(z[4], 1)

            take_x(0)
            take_x(1)
            for m in range(2, nx):
                silu_x(m - 2)
                act.wait_ge(xs_done, m - 1)
                take_x(m)
            if ng:
                take_gate(0)
            silu_x(nx - 2)
            if ng:
                take_gate(1)
            if z is not None:
                for b in range(5):
                    take_z(b)
            silu_x(nx - 1)
            if z is not None:
                for b in range(5, NB):
                    take_z(b)
            for m in range(2, ng):
                take_gate(m)

        @block.vector
        def _(dve):
            for q in range(2):
                nc.vector.memset(pre[q][:, :, 0:TAPS - 1], 0.0).then_inc(pads_zero, 1)
            for m in range(nx):
                dve.wait_ge(pre_copied, (m + 1) * CH)
                a3 = acc[m % 2].rearrange("p (b t) -> p b t", t=T)
                for k in range(TAPS - 1):
                    nc.vector.scalar_tensor_tensor(out=a3, in0=pre[m % 2][:, :, k:k + T],
                                                   scalar=cw[:, m, k:k + 1], in1=a3,
                                                   op0=ALU.mult, op1=ALU.add).then_inc(conv_done, 1)
                    dve.wait_ge(conv_done, m * (TAPS - 1) + k + 1)


def scan_layer(nc, ps, sems, ident, arena_at, x_tok, small, w):
    A = Arena(arena_at.tensor)
    A.at = arena_at.at
    big = [A.take(MT * NT) for _ in range(4)]
    xs, gate, dt, u = (r.rearrange("p (i m t) -> p i m t", i=PASSES, m=MH) for r in big)
    xn_tok = big[2][:, 0:NB * D].rearrange("p (b d) -> p b d", d=D)
    xn_t = big[3][:, 0:KT * NT].rearrange("p (k t) -> p k t", k=KT)
    dt_in = big[3][:, KT * NT:KT * NT + HEADS0 * NT].rearrange("p (h t) -> p h t", h=HEADS0)
    bc3 = A.take(HEADS0 * NT // 2).bitcast(BF16).rearrange("p (i t) -> p i t", i=PASSES)
    rate = A.take(PASSES * MH * NS).rearrange("p (i n) -> p i n", i=PASSES)
    skip = A.take(PASSES * MH).rearrange("p (i m) -> p i m", i=PASSES)
    wo = A.take(MT * D).rearrange("p (m d) -> p m d", m=MT)
    unit = A.take(BC // 2).bitcast(BF16)
    temp0 = A.at
    w_in = A.take(KT * 2 * INNER).rearrange("p (k o) -> p k o", k=KT)
    sel = w_in.rearrange("p k o -> p (k o)")[:, 0:BC * P // 2].bitcast(BF16).rearrange("p (n q) -> p n q", q=P)
    cw = A.take(MT * TAPS).rearrange("p (m k) -> p m k", k=TAPS)
    cb = A.take(MT)
    wx = A.take(MT * RANK).rearrange("p (m r) -> p m r", m=MT)
    wbc = A.take(MT * 3 * BC).rearrange("p (m r) -> p m r", m=MT)
    wdt = A.take(INNER).rearrange("p (m d) -> p m d", m=MT)
    dtb = A.take(MT)
    pre = [A.take(NB * (T + TAPS - 1)).rearrange("p (b t) -> p b t", b=NB) for _ in range(2)]
    acc = [A.take(NT) for _ in range(2)]
    r1 = pre[0].rearrange("p b t -> p (b t)")[:, 0:2 * BANK].rearrange("p (j t) -> p j t", j=2)
    temp_e = [acc[0], pre[1].rearrange("p b t -> p (b t)")[:, 0:NT]]
    temp_g = [acc[1], big[3][:, 0:NT], acc[1], big[3][:, KT * NT:KT * NT + NT]]
    half16 = pre[0].rearrange("p b t -> p (b t)")[:, 2 * BANK:2 * BANK + BANK].bitcast(BF16)\
        .rearrange("p (j t) -> p j t", j=2)

    with ExitStack() as ctx:
        sem = sems
        w_here = sem("l0_weights")
        wsrc = [(w_in, w["in_proj"]), (cw, w["conv_w"]), (cb, w["conv_b"]), (wx, w["x_dt"]),
                (wdt, w["dt_proj"]), (dtb, w["dt_bias"]), (wo, w["out_proj"]), (unit, w["sel"])]
        wsrc += [(wbc[:, :, j * BC:(j + 1) * BC], w["x_bc"]) for j in range(3)]
        wsrc += [(rate[:, j::CH, :], w["a_log"]) for j in range(CH)] + [(skip[:, j::CH, :], w["d"]) for j in range(CH)]

        def load(sp):
            n = dma_all(sp, wsrc, w_here)
            sp.wait_ge(w_here, n)

        norm_stage(nc, ps, sems, ident, x_tok, xn_tok,
                   lambda k, c: xn_t[:, k, c * BANK:(c + 1) * BANK].rearrange("p (b t) -> p b t", t=T),
                   small, "scan", load)
        def put_x(m):
            return [(xs[:, m // MH * CH:(m // MH + 1) * CH, m % MH, :], acc[m % 2].rearrange("p (c t) -> p c t", c=CH))]

        def put_gate(m, c):
            return gate[:, m // MH * CH + c, m % MH, :]

        conv_stage(nc, ps, sems, xn_t, w_in, MT, put_x, MT, put_gate, cw, cb, pre, acc, "m0")

        xp_done, xp_copied, bc_split, dtp_done, pre_done, e_done, one_e, ln_done, dt_done, u_done = map(
            sem, ("xp_done", "xp_copied", "bc_split", "dtp_done", "dtpre_done", "e_done", "one_e", "ln_done",
                  "dt_done", "u_done"))
        dve_own = sem("dve_own_proj")
        act_own = sem("act_own_proj")
        sel_done = sem("sel_done")

        def dtp(m, c):
            return dt[:, m // MH * CH + c, m % MH, :]

        def rows(t4, m):
            return t4[:, m // MH * CH:(m // MH + 1) * CH, m % MH, :]

        with nc.Block() as block:
            @block.tensor
            def _(pe):
                for h in range(HEADS0):
                    for j in range(h * CH, (h + 1) * CH):
                        if j >= 2:
                            pe.wait_ge(xp_copied, j - 1)
                        for k in range(MH):
                            nc.tensor.matmul(ps[:, j % 2, :], wx[:, h * MH + k, :], xs[:, j, k, :],
                                             start=(k == 0), stop=(k == MH - 1))
                        if j >= 2:
                            pe.wait_ge(bc_split, j - 1)
                        for k in range(MH):
                            ins = nc.tensor.matmul(ps[0:3 * BC, 2 + j % 2, :], wbc[:, h * MH + k, :], xs[:, j, k, :],
                                                   start=(k == 0), stop=(k == MH - 1))
                        ins.then_inc(xp_done, 1)
                    for m in range(h * MH, (h + 1) * MH):
                        pe.wait_ge(xp_copied, (h + 1) * CH)
                        for c in range(CH):
                            if m >= 1:
                                pe.wait_ge(pre_done, (m - 1) * CH + c + 1)
                            nc.tensor.matmul(ps[:, 4 + c, :], wdt[:, m, :], dt_in[:, h, c * BANK:(c + 1) * BANK],
                                             start=True, stop=True).then_inc(dtp_done, 1)

            @block.gpsimd
            def _(pool):
                nc.gpsimd.tensor_copy(sel, unit.rearrange("p (n o) -> p n o", o=1).broadcast_to([P, BC, P]))\
                    .then_inc(sel_done, 1)

            @block.scalar
            def _(act):
                own = Chain(act, act_own)
                rates = rate.rearrange("p i n -> p (i n)")
                own(nc.scalar.activation(rates, rates, ACT.Exp))
                own(nc.scalar.mul(rates, rates, -1.0))
                def take_dt_in(j):
                    act.wait_ge(xp_done, j + 1)
                    nc.scalar.activation(dt_in[:, j // CH, (j % CH) * BANK:(j % CH + 1) * BANK], ps[:, j % 2, :],
                                         ACT.Copy).then_inc(xp_copied, 1)

                def decay_exp(m):
                    for c in range(CH):
                        act.wait_ge(dtp_done, m * CH + c + 1)
                        nc.scalar.activation(dtp(m, c), ps[:, 4 + c, :], ACT.Identity, bias=dtb[:, m:m + 1])\
                            .then_inc(pre_done, 1)
                    if m >= 2:
                        act.wait_ge(dt_done, m - 1)
                    act.wait_ge(pre_done, (m + 1) * CH)
                    own(nc.scalar.activation(temp_e[m % 2].rearrange("p (c t) -> p c t", c=CH), rows(dt, m), ACT.Abs))
                    nc.scalar.activation(temp_e[m % 2], temp_e[m % 2], ACT.Exp, scale=-1.0).then_inc(e_done, 1)

                def log_of(m):
                    act.wait_ge(one_e, m + 1)
                    nc.scalar.activation(temp_g[m], temp_g[m], ACT.Ln).then_inc(ln_done, 1)

                for j in range(CH):
                    take_dt_in(j)
                decay_exp(0)
                decay_exp(1)
                take_dt_in(CH)
                log_of(0)
                take_dt_in(CH + 1)
                log_of(1)
                take_dt_in(CH + 2)
                take_dt_in(CH + 3)
                decay_exp(2)
                decay_exp(3)
                log_of(2)
                log_of(3)

            @block.vector
            def _(dve):
                own = Chain(dve, dve_own)
                def split(j):
                    dve.wait_ge(xp_done, j + 1)
                    bank = ps[0:3 * BC, 2 + j % 2, :]
                    out = bc3[:, j, :]
                    r, s = r1[:, j % 2, :], half16[:, j % 2, :]
                    own(nc.vector.tensor_copy(out[0:3 * BC], bank))
                    nc.vector.tensor_tensor(r[0:3 * BC], bank, out[0:3 * BC], ALU.subtract).then_inc(bc_split, 1)
                    dve.wait_ge(bc_split, j + 1)
                    own(nc.vector.tensor_copy(out[BC:2 * BC], r[BC:2 * BC]))
                    own(nc.vector.tensor_copy(s[2 * BC:3 * BC], r[2 * BC:3 * BC]))
                    own(nc.vector.tensor_tensor(out[2 * BC:3 * BC], r[2 * BC:3 * BC], s[2 * BC:3 * BC],
                                                ALU.subtract))
                def rounded(m):
                    e, g = temp_e[m % 2], temp_g[m]
                    dve.wait_ge(e_done, m + 1)
                    own(nc.vector.tensor_scalar(g, e, 1.0, None, ALU.add))
                    nc.vector.scalar_tensor_tensor(out=e, in0=g, scalar=1.0, in1=e, op0=ALU.subtract,
                                                   op1=ALU.subtract).then_inc(one_e, 1)
                    dve.wait_ge(one_e, m + 1)

                def soft(m):
                    e, g = temp_e[m % 2], temp_g[m]
                    dve.wait_ge(ln_done, m + 1)
                    own(nc.vector.tensor_tensor(g, g, e, ALU.subtract))
                    nc.vector.scalar_tensor_tensor(out=rows(dt, m), in0=rows(dt, m), scalar=0.0,
                                                   in1=g.rearrange("p (c t) -> p c t", c=CH),
                                                   op0=ALU.max, op1=ALU.add).then_inc(dt_done, 1)

                def weigh(m):
                    dve.wait_ge(dt_done, m // MH * MH + MH)
                    own(nc.vector.tensor_tensor(rows(u, m), rows(dt, m), rows(xs, m), ALU.mult))
                    nc.vector.memset(rows(dt, m).rearrange("p c (b t) -> p c b t", t=T)[:, :, :, 0:1], BIG)\
                        .then_inc(u_done, 1)

                for j in range(CH):
                    split(j)
                rounded(0)
                rounded(1)
                split(CH)
                split(CH + 1)
                soft(0)
                split(CH + 2)
                soft(1)
                weigh(0)
                split(CH + 3)
                weigh(1)
                rounded(2)
                rounded(3)
                soft(2)
                soft(3)
                weigh(2)
                weigh(3)

        A.at = temp0 + BC * P // 2
        state = A.take(RING0 * MH * BANK).rearrange("p (r m t) -> p r m t", r=RING0, m=MH)
        b_copy = A.take(4 * BANK).rearrange("p (q t) -> p q t", q=4)
        b_done, b_copied, c_done, y_done, decay_done, ub_done, scan_done, hc_done, y_taken = map(
            sem, ("b_done", "b_copied", "c_done", "y_done", "decay_done", "ub_done", "scan_done", "hc_done", "y_taken"))
        ub_paced = sem("ub_paced")
        B_BANK, C_BANK, Y_BANK, DECAY_BANK = 0, 1, 2, 4
        LAST = PASSES - 1
        AHEAD = 3

        def ahead(i, n, by):
            return (i, n + by) if n + by < NS else (i + 1, n + by - NS)

        def at(i):
            return bass.ds(i, 1)

        with nc.Block() as block:
            @block.tensor
            def _(pe):
                def broadcast(i, row, bank, done):
                    nc.tensor.matmul(ps[:, bank, :], sel[0:3 * BC, row, :],
                                     bc3[0:3 * BC, at(i), :].rearrange("p i t -> p (i t)"),
                                     start=True, stop=True).then_inc(done, 1)

                def sum_state(i, n):
                    pe.wait_ge(hc_done, 2 + i * NS + n)
                    for m in range(MH):
                        if n == 0:
                            pe.wait_ge(y_taken, 1 + i * 3 + m)
                        ins = nc.tensor.matmul(ps[:, Y_BANK + m, :], ident, state[:, n % RING0, m, :],
                                               start=(n == 0), stop=(n == NS - 1))
                    ins.then_inc(y_done, 1)

                def run(i, last):
                    for n in range(NS):
                        j, l = ahead(i, n, AHEAD)
                        if not (last and n + AHEAD >= NS):
                            pe.wait_ge(b_copied, 1 + j * NS + l)
                            broadcast(j, l, B_BANK, b_done)
                        pe.wait_ge(hc_done, 1 + i * NS + n)
                        broadcast(i, NS + n, C_BANK, c_done)
                        if n:
                            sum_state(i, n - 1)
                    sum_state(i, NS - 1)

                pe.sem_inc(y_done, RING0)
                for n in range(AHEAD):
                    pe.wait_ge(b_copied, 1 + n)
                    broadcast(0, n, B_BANK, b_done)
                with pe.Fori(0, LAST) as i:
                    run(i, False)
                run(LAST, True)

            @block.scalar
            def _(act):
                def copy_b(i, n):
                    act.wait_ge(b_done, i * NS + n + 1)
                    act.wait_ge(ub_done, i * NS + n - 2)
                    nc.scalar.activation(b_copy[:, n % 4, :], ps[:, B_BANK, :], ACT.Copy).then_inc(b_copied, 1)

                def decays(i, n):
                    act.wait_ge(scan_done, i * NS + n)
                    for m in range(MH):
                        nc.scalar.activation(ps[:, DECAY_BANK + n % 2 * MH + m, :],
                                             dt[:, at(i), m, :].rearrange("p i t -> p (i t)"), ACT.Exp,
                                             scale=rate[:, at(i), m * NS + n:m * NS + n + 1]
                                             .rearrange("p i t -> p (i t)")).then_inc(decay_done, 1)

                def run(i, last):
                    for n in range(NS):
                        if not (last and n + AHEAD >= NS):
                            copy_b(*ahead(i, n, AHEAD))
                        if not (last and n + 2 >= NS):
                            decays(*ahead(i, n, 2))

                act.sem_inc(b_copied, 1)
                for n in range(AHEAD):
                    act.wait_ge(b_done, n + 1)
                    nc.scalar.activation(b_copy[:, n, :], ps[:, B_BANK, :], ACT.Copy).then_inc(b_copied, 1)
                    if n < 2:
                        for m in range(MH):
                            nc.scalar.activation(ps[:, DECAY_BANK + n * MH + m, :], dt[:, 0, m, :], ACT.Exp,
                                                 scale=rate[:, 0, m * NS + n:m * NS + n + 1]).then_inc(decay_done, 1)
                with act.Fori(0, LAST) as i:
                    run(i, False)
                run(LAST, True)

            @block.gpsimd
            def _(pool):
                pool.sem_inc(ub_done, 1)
                with pool.Fori(0, PASSES) as i:
                    for n in range(NS):
                        pool.wait_ge(b_copied, 2 + i * NS + n)
                        pool.wait_ge(y_done, 1 + i * NS + n)
                        pool.sem_inc(ub_paced, 1)
                        nc.gpsimd.tensor_tensor(state[:, n % RING0],
                                                u[:, at(i)].rearrange("p i m t -> p (i m) t"),
                                                b_copy[:, n % 4:n % 4 + 1, :].broadcast_to([P, MH, BANK]), ALU.mult)\
                            .then_inc(ub_done, 1)

            @block.vector
            def _(dve):
                def take_y(i):
                    dve.wait_ge(y_done, RING0 + (i + 1) * NS)
                    for m in range(MH):
                        xr = xs[:, at(i), m, :].rearrange("p i t -> p (i t)")
                        nc.vector.scalar_tensor_tensor(out=xr, in0=xr, scalar=skip[:, at(i), m:m + 1]
                                                       .rearrange("p i t -> p (i t)"), in1=ps[:, Y_BANK + m, :],
                                                       op0=ALU.mult, op1=ALU.add).then_inc(y_taken, 1)
                    dve.wait_ge(y_taken, 3 + i * 3 + MH)
                    gr = gate[:, at(i)].rearrange("p i m t -> p (i m t)")
                    nc.vector.tensor_tensor(gr, gr, xs[:, at(i)].rearrange("p i m t -> p (i m t)"), ALU.mult)\
                        .then_inc(y_taken, 1)

                def scan(i, n):
                    st = state[:, n % RING0].rearrange("p m t -> p (m t)")
                    dve.wait_ge(ub_done, 2 + i * NS + n)
                    dve.wait_ge(decay_done, (i * NS + n + 1) * MH)
                    q = DECAY_BANK + n % 2 * MH
                    nc.vector.tensor_tensor_scan(st, ps[:, q:q + MH, :].rearrange("p m t -> p (m t)"), st,
                                                 0.0, ALU.mult, ALU.add).then_inc(scan_done, 1)

                def run(i, first=False, last=False):
                    for n in range(NS):
                        if not (last and n + 1 >= NS):
                            scan(*ahead(i, n, 1))
                        dve.wait_ge(c_done, i * NS + n + 1)
                        dve.wait_ge(scan_done, 2 + i * NS + n)
                        nc.vector.tensor_tensor(state[:, n % RING0], state[:, n % RING0],
                                                ps[:, C_BANK:C_BANK + 1, :].broadcast_to([P, MH, BANK]), ALU.mult)\
                            .then_inc(hc_done, 1)
                        if n == 0 and not first:
                            take_y(i - 1)

                dve.sem_inc(scan_done, 1)
                dve.sem_inc(hc_done, 1)
                dve.sem_inc(y_taken, 3)
                scan(0, 0)
                run(0, first=True)
                with dve.Fori(1, LAST) as i:
                    run(i)
                run(LAST, last=True)
                take_y(LAST)

        out_done, out_added = sem("out0_done"), sem("out0_added")
        with nc.Block() as block:
            @block.tensor
            def _(pe):
                for b in range(NB):
                    for m in range(MT):
                        i = m // MH * CH + b // BPC
                        ins = nc.tensor.matmul(ps[:, b // 2, (b % 2) * D:(b % 2 + 1) * D],
                                               gate[:, i, m % MH, (b % BPC) * T:(b % BPC + 1) * T], wo[:, m, :],
                                               start=(m == 0), stop=(m == MT - 1))
                    if b % 2:
                        ins.then_inc(out_done, 1)

            @block.vector
            def _(dve):
                for g in range(NB // 2):
                    dve.wait_ge(out_done, g + 1)
                    xr = x_tok[:, 2 * g:2 * g + 2, :].rearrange("p b d -> p (b d)")
                    nc.vector.tensor_tensor(xr, ps[:, g, :], xr, ALU.add).then_inc(out_added, 1)


def wkv_layer(nc, ps, sems, ident, arena_at, x_tok, small, w):
    A = Arena(arena_at.tensor)
    A.at = arena_at.at
    padded = lambda: A.take(KT * NB * TP).rearrange("p (k b t) -> p k b t", k=KT, b=NB)
    k_pad, top, aa, bb, decay_b, new_b, new_bv, drop = (padded() for _ in range(8))
    flat = lambda r, k: r[:, k, :, :].rearrange("p b t -> p (b t)")
    v = A.take(KT * NT).rearrange("p (k b t) -> p k b t", k=KT, b=NB)
    e2 = A.take(KT * NT).rearrange("p (k b t) -> p k b t", k=KT, b=NB)
    xn_tok = A.take(NB * D).rearrange("p (b d) -> p b d", d=D)
    y = xn_tok.rearrange("p b d -> p (b d)").rearrange("p (k b t) -> p k b t", k=KT, b=NB)
    par = A.take(2 * KT).rearrange("p (j k) -> p j k", k=KT)
    now, old = slice(1, TP), slice(0, T)
    e1 = y
    den, rec = decay_b[:, :, :, now], new_b[:, :, :, now]
    with ExitStack() as ctx:
        sem = sems
        w_here, dve_own, act_own = sem("wkv_here"), sem("dve_own_wkv"), sem("act_own_wkv")

        def load(sp):
            n = dma_all(sp, [(v.rearrange("p k b t -> p k (b t)"), w["ctx_t"]), (par[:, 0, :], w["decay"]),
                             (par[:, 1, :], w["first"])], w_here)
            sp.wait_ge(w_here, n)

        norm_stage(nc, ps, sems, ident, x_tok, xn_tok, lambda k, c: k_pad[:, k, c * BPC:(c + 1) * BPC, 1:TP],
                   small, "wkv", load)
        zeros_done, drop_done, state_gap, out_gap, eb_done, e12_done, den_done, rec_done, y_done = map(
            sem, ("wkv_zeros", "wkv_drop", "wkv_state_gap", "wkv_out_gap", "wkv_eb", "wkv_e12", "wkv_den", "wkv_rec",
                  "wkv_y"))
        with nc.Block() as block:
            @block.scalar
            def _(act):
                own = Chain(act, act_own)
                own(nc.scalar.activation(par[:, 0, :], par[:, 0, :], ACT.Exp))
                own(nc.scalar.mul(par[:, 0, :], par[:, 0, :], -1.0))
                for k in range(KT):
                    act.wait_ge(zeros_done, 1)
                    nc.scalar.activation(drop[:, k, :, now], aa[:, 1, :, now], ACT.Identity, bias=par[:, 0, k:k + 1])\
                        .then_inc(drop_done, 1)

                def factors(first, second, done):
                    own(nc.scalar.activation(first, second, ACT.Relu, scale=-1.0))
                    own(nc.scalar.activation(second, second, ACT.Relu))
                    nc.scalar.activation(first, first, ACT.Exp, scale=-1.0).then_inc(done, 1)
                    nc.scalar.activation(second, second, ACT.Exp, scale=-1.0).then_inc(done, 1)

                for k in range(KT):
                    act.wait_ge(state_gap, k + 1)
                    factors(decay_b[:, k, :, now], new_b[:, k, :, now], eb_done)
                    act.wait_ge(out_gap, k + 1)
                    factors(e2[:, k], e1[:, k], e12_done)
                for k in range(KT):
                    act.wait_ge(den_done, k + 1)
                    own(nc.scalar.activation(rec[:, k], den[:, k], ACT.Ln))
                    nc.scalar.activation(rec[:, k], rec[:, k], ACT.Exp, scale=-1.0).then_inc(rec_done, 1)

            @block.vector
            def _(dve):
                own = Chain(dve, dve_own)
                nc.vector.memset(aa[:, 1, :, now], 0.0).then_inc(zeros_done, 1)
                nc.vector.memset(k_pad[:, :, :, 0:1], -1.0e38)
                nc.vector.memset(drop[:, :, :, 0:1], -1.0e38)
                for r in (decay_b, new_b, new_bv):
                    ins = nc.vector.memset(r[:, :, :, 0:1], 0.0)
                own(ins)
                for k in range(KT):
                    w_k, u_k = par[:, 0, k:k + 1], par[:, 1, k:k + 1]
                    kn, po = k_pad[:, k, :, now], top[:, k, :, old]
                    dve.wait_ge(drop_done, k + 1)
                    own(nc.vector.tensor_tensor_scan(flat(top, k), flat(drop, k), flat(k_pad, k), -1.0e38,
                                                     ALU.add, ALU.max))
                    nc.vector.scalar_tensor_tensor(out=new_b[:, k, :, now], in0=po, scalar=w_k, in1=kn,
                                                   op0=ALU.add, op1=ALU.subtract).then_inc(state_gap, 1)
                    nc.vector.scalar_tensor_tensor(out=e1[:, k], in0=kn, scalar=u_k, in1=po, op0=ALU.add,
                                                   op1=ALU.subtract).then_inc(out_gap, 1)
                for k in range(KT):
                    dve.wait_ge(eb_done, 2 * k + 2)
                    own(nc.vector.tensor_tensor(new_bv[:, k, :, now], new_b[:, k, :, now], v[:, k], ALU.mult))
                    nc.vector.tensor_tensor_scan(flat(aa, k), flat(decay_b, k), flat(new_bv, k), 0.0, ALU.mult, ALU.add)
                    own(nc.vector.tensor_tensor_scan(flat(bb, k), flat(decay_b, k), flat(new_b, k), 0.0,
                                                     ALU.mult, ALU.add))
                    dve.wait_ge(e12_done, 2 * k + 2)
                    own(nc.vector.tensor_tensor(bb[:, k, :, old], bb[:, k, :, old], e1[:, k], ALU.mult))
                    nc.vector.tensor_tensor(den[:, k], bb[:, k, :, old], e2[:, k], ALU.add).then_inc(den_done, 1)
                    own(nc.vector.tensor_tensor(aa[:, k, :, old], aa[:, k, :, old], e1[:, k], ALU.mult))
                    dve.wait_ge(den_done, k + 1)
                    own(nc.vector.tensor_tensor(e2[:, k], e2[:, k], v[:, k], ALU.mult))
                    own(nc.vector.tensor_tensor(e2[:, k], e2[:, k], aa[:, k, :, old], ALU.add))
                for k in range(KT):
                    dve.wait_ge(rec_done, k + 1)
                    own(nc.vector.tensor_tensor(den[:, k], den[:, k], rec[:, k], ALU.mult))
                    own(nc.vector.scalar_tensor_tensor(out=den[:, k], in0=den[:, k], scalar=2.0, in1=rec[:, k],
                                                       op0=ALU.subtract, op1=ALU.mult))
                    nc.vector.scalar_tensor_tensor(out=y[:, k], in0=den[:, k], scalar=-1.0, in1=e2[:, k],
                                                   op0=ALU.mult, op1=ALU.mult).then_inc(y_done, 1)
        add_transposed_stage(nc, ps, sems, ident, x_tok, lambda k, b: y[:, k, b, :], "wkv")


E0, Z0, I0, K0 = 32, 32, 128, 8
SCALE0, CAP0, EPS0 = 1.5, 128, 1e-20
E1, I1, K1 = 16, 224, 4
RING = 8
LAG = 5


def ffn0_layer(nc, ps, sems, ident, arena_at, x_tok, small, w):
    A = Arena(arena_at.tensor)
    A.at = arena_at.at
    C = E0 + Z0
    w_gu = A.take(E0 * KT * 2 * I0).rearrange("p (e k f) -> p e k f", e=E0, k=KT)
    w_dn = A.take(E0 * D).rearrange("p (e f d) -> p e f d", e=E0, f=1)
    cst = A.take(CONST)
    xn_tok = A.take(NB * D).rearrange("p (b d) -> p b d", d=D)
    xn_t = A.take(KT * NT).rearrange("p (k t) -> p k t", k=KT)
    wr = A.take(KT * C).rearrange("p (k c) -> p k c", k=KT)
    bias = A.take(C)
    mask16 = A.take(P).bitcast(BF16).rearrange("p (j t) -> p j t", j=2)
    tok = lambda n: A.take(NB * n).rearrange("p (b c) -> p b c", b=NB)
    sc, biased, left, chosen, top8 = tok(C), tok(C), tok(C), tok(C), tok(8)
    ch16 = A.take(NB * E0 // 2).bitcast(BF16).rearrange("p (b c) -> p b c", b=NB)
    before = A.take(NB * E0 // 2).bitcast(BF16).rearrange("p (b c) -> p b c", b=NB)
    wt, place = tok(E0), tok(E0)
    row = tok(1)
    row2 = tok(1)
    with ExitStack() as ctx:
        sem = sems
        w_here, experts_here, dve_own = sem("r0_here"), sem("experts0_here"), sem("dve_own_r0")

        def load(sp):
            n = dma_all(sp, [(wr, w["cls"]), (bias, w["bias"].broadcast_to([P, C])), (mask16, w["mask16"]),
                             (cst, w["const"])], w_here)
            dma_all(sp, [(w_gu, w["gate_up"]), (w_dn, w["down"])], experts_here)
            sp.wait_ge(w_here, n)

        norm_stage(nc, ps, sems, ident, x_tok, xn_tok,
                   lambda k, c: xn_t[:, k, c * BANK:(c + 1) * BANK].rearrange("p (b t) -> p b t", t=T),
                   small, "ffn0", load)
        logit_done, shifted, exp_done, chosen_done, prefix_done, pos_done = map(
            sem, ("r0_logit", "r0_shift", "r0_exp", "r0_chosen", "r0_prefix", "r0_pos"))
        with nc.Block() as block:
            @block.tensor
            def _(pe):
                for b in range(NB):
                    for k in range(KT):
                        ins = nc.tensor.matmul(ps[:, b // 8, (b % 8) * C:(b % 8 + 1) * C],
                                               xn_t[:, k, b * T:(b + 1) * T], wr[:, k, :],
                                               start=(k == 0), stop=(k == KT - 1))
                ins.then_inc(logit_done, 1)
                pe.wait_ge(prefix_done, 1)
                nc.tensor.matmul(ps[:, 2, :], mask16[:, 0, :], ch16.rearrange("p b c -> p (b c)"), start=True, stop=False)
                nc.tensor.matmul(ps[:, 2, :], mask16[:, 1, :], before.rearrange("p b c -> p (b c)"),
                                 start=False, stop=True).then_inc(pos_done, 1)

            @block.scalar
            def _(act):
                act.wait_ge(shifted, 1)
                nc.scalar.activation(sc, sc, ACT.Exp).then_inc(exp_done, 1)

            @block.vector
            def _(dve):
                own = Chain(dve, dve_own)
                dve.wait_ge(logit_done, 1)
                logits = ps[:, 0:2, :].rearrange("p a (b c) -> p (a b) c", c=C)
                over = lambda r: r.broadcast_to([P, NB, C])
                own(nc.vector.tensor_reduce(row, logits, AX.X, ALU.max))
                nc.vector.tensor_tensor(sc, logits, over(row), ALU.subtract).then_inc(shifted, 1)
                dve.wait_ge(exp_done, 1)
                own(nc.vector.tensor_reduce(row2, sc, AX.X, ALU.add))
                own(nc.vector.reciprocal(row, row2))
                own(nc.vector.tensor_tensor(sc, sc, over(row), ALU.mult))
                own(nc.vector.tensor_tensor(biased, sc, bias.rearrange("p (o c) -> p o c", o=1).broadcast_to([P, NB, C]),
                                            ALU.add))
                for b in range(NB):
                    ins = nc.vector.max(top8[:, b, :], biased[:, b, :])
                own(ins)
                for b in range(NB):
                    ins = nc.vector.match_replace(left[:, b, :], top8[:, b, :], biased[:, b, :], -1.0e30)
                own(ins)
                own(nc.vector.tensor_tensor(chosen, left, biased, ALU.not_equal))
                own(nc.vector.tensor_copy(ch16, chosen[:, :, 0:E0]))
                own(nc.vector.memset(before[:, 0, :], 0.0))
                for b in range(1, NB):
                    ins = nc.vector.tensor_tensor(before[:, b, :], before[:, b - 1, :], ch16[:, b - 1, :], ALU.add)
                    if b < NB - 1:
                        own(ins)
                    else:
                        ins.then_inc(prefix_done, 1)
                own(nc.vector.tensor_tensor(sc, sc, chosen, ALU.mult))
                own(nc.vector.tensor_reduce(row2, sc, AX.X, ALU.add))
                own(nc.vector.tensor_scalar(row2, row2, EPS0, None, ALU.add))
                own(nc.vector.reciprocal(row, row2))
                own(nc.vector.tensor_tensor(sc, sc, over(row), ALU.mult))
                own(nc.vector.tensor_scalar(sc, sc, SCALE0, None, ALU.mult))
                own(nc.vector.tensor_reduce(row, sc[:, :, E0:], AX.X, ALU.add))
                own(nc.vector.tensor_scalar(row, row, 1.0, None, ALU.add))
                own(nc.vector.tensor_tensor(wt, sc[:, :, 0:E0], row.broadcast_to([P, NB, E0]), ALU.mult))
                dve.wait_ge(pos_done, 1)
                own(nc.vector.scalar_tensor_tensor(out=place, in0=ps[:, 2, :].rearrange("p (b c) -> p b c", b=NB),
                                                   scalar=1.0, in1=chosen[:, :, 0:E0], op0=ALU.add, op1=ALU.mult))
                own(nc.vector.tensor_scalar(place, place, -1.0, None, ALU.add))

            @block.sync
            def _(sp):
                sp.wait_ge(experts_here, 32)
        assert CAP0 == P
        sparse_experts(nc, ps, sems, ident, A, x_tok, xn_tok, wt, place, E0, 1, E0, H0, I0, 1,
                       {"w_gu": w_gu, "w_dn": w_dn, "dummy": cst[:, 1:2], "spare": xn_t.rearrange("p k t -> p (k t)")},
                       expert_const(cst), "e0")



H0, H1 = 16, 64
CONST = 20 + 3 * P + 8
ROUND = 12582912.0


def expert_const(cst):
    wide = lambda j: cst[:, 20 + j * P:20 + (j + 1) * P]
    return cst[:, 0:1], cst[:, 2:19], wide(0), wide(1), wide(2), cst[:, 20 + 3 * P:]


def sparse_experts(nc, ps, sems, ident, A, x_tok, xn_tok, wt, place, n_exp, blocks, n_tiles, H, inner, f_n, w, const, tag,
                   out=None):
    fw = inner // f_n
    L, G = P // H, P // H
    W = blocks * L
    NG = n_exp // G
    M = NB * n_exp
    assert G * 2 * W == P
    Q = n_exp * blocks
    ROWS = NT + P
    WIDTH = D + n_exp
    dynamic = blocks > 1
    w_gu = w["w_gu"]
    w_dn = w["w_dn"]
    tok_no, starts, iota, diagonal, spread, low_mask = const
    table = nc.dram_tensor(f"table_{tag}", (ROWS, WIDTH), F32, kind="Internal").ap()
    sums = [nc.dram_tensor(f"sums{j}_{tag}", (ROWS, D), F32, kind="Internal").ap() for j in range(2)]
    idx = A.take(n_tiles).bitcast(mybir.dt.uint32)
    tile_map = A.take(P).bitcast(mybir.dt.int32)
    at0 = A.at
    later = A.take(M * H // 4)
    ups = [r.bitcast(BF16).rearrange("p (b e h) -> p b e h", b=NB, h=H)
           for r in (w["spare"][:, 0:M * H // 4], later)]
    rhs = A.take(M * W).bitcast(BF16).rearrange("p (b e v h) -> p b e v h", b=NB, v=2, h=W)
    cuts = A.take(4 * M)
    S = Arena(later)
    block_no, within, up, code = (cuts[:, j * M:(j + 1) * M] for j in range(4))
    masked = cuts[:, 0:NG * P].rearrange("p (g c) -> p g c", g=NG)
    picked = S.take(NG * P)
    vals = S.take(2 * Q).rearrange("p (e v h) -> p e v h", v=2, h=blocks)
    free_of = S.take(Q).rearrange("p (e h) -> p e h", h=blocks)
    ids = S.take(Q).rearrange("p (e h) -> p e h", h=blocks)
    zero = A.take(WIDTH)
    tiles_of, ends, begins, cmp = (A.take(n_exp) for _ in range(4))
    mp = A.take(8)
    if dynamic:
        owns = A.take(Q)
        col_hot, ids_t, col_t = (r.take(2 * P).rearrange("p (a c) -> p a c", a=2) for r in (A, S, S))
    A.at = at0
    xe = [A.take(WIDTH) for _ in range(RING)]
    xe_t = [A.take(KT * P).rearrange("p (k s) -> p k s", k=KT) for _ in range(2)]
    sg = [A.take(inner) for _ in range(2)]
    av = [A.take(inner) for _ in range(2)]
    av_t = [A.take(f_n * P).rearrange("p (f s) -> p f s", f=f_n) for _ in range(2)]
    ye = [A.take(D) for _ in range(RING)]
    ixb = A.take(2 * RING).bitcast(mybir.dt.uint32)
    back = xn_tok

    with ExitStack() as ctx:
        sem = lambda n: sems(f"{n}_{tag}")
        own_sem, hot_done, rhs_done, ups_done, found, masked_done, spread_done, zero_done, table_here = map(
            sem, ("own_ix", "hot_done", "rhs_done", "ups_done", "found", "masked_done", "spread_done", "zero_done",
                  "table_here"))
        map_done, map_turned, map_taken, sorted_done = map(sem, ("map_done", "map_turned", "map_taken", "sorted_done"))
        MB = NG * P // BANK
        halves = [slice(0, n_exp // 2), slice(n_exp // 2, n_exp)]
        with nc.Block() as block:
            @block.vector
            def _(dve):
                own = Chain(dve, own_sem)
                nc.vector.memset(zero, 0.0).then_inc(zero_done, 1)
                pl = place.rearrange("p b e -> p (b e)")

                def whole_part(out, src, step):
                    own(nc.vector.tensor_scalar(out, src, 1.0 / step, -(step - 1) / (2.0 * step), ALU.mult, ALU.add))
                    own(nc.vector.tensor_scalar(out, out, ROUND, None, ALU.add))
                    own(nc.vector.tensor_scalar(out, out, ROUND, None, ALU.subtract))

                def rest(out, whole, step, src):
                    own(nc.vector.scalar_tensor_tensor(out=out, in0=whole, scalar=float(-step), in1=src,
                                                       op0=ALU.mult, op1=ALU.add))

                whole_part(block_no, pl, P)
                rest(within, block_no, P, pl)
                whole_part(up, within, L)
                rest(within, up, L, within)
                rest(code, block_no, -L, within)

                def one_hot(out, v, half, n):
                    shape = [P, NB, n_exp // 2, n]
                    v = v.rearrange("p (b e o) -> p b e o", b=NB, o=1)[:, :, halves[half]]
                    return nc.vector.tensor_tensor(out, v.broadcast_to(shape), iota[:, 0:n]
                                                   .rearrange("p (o q h) -> p o q h", o=1, q=1).broadcast_to(shape),
                                                   ALU.is_equal)

                for half in range(2):
                    one_hot(rhs[:, :, halves[half], 0, :], code, half, W).then_inc(hot_done, 1)
                    one_hot(ups[half], up, half, H).then_inc(ups_done, 1)
                if dynamic:
                    t3 = owns.rearrange("p (e h) -> p e h", h=blocks)
                    own(nc.vector.tensor_tensor(t3, w["queue"].rearrange("p (e o) -> p e o", o=1)
                                                .broadcast_to([P, n_exp, blocks]),
                                                starts[:, 0:blocks].rearrange("p (o h) -> p o h", o=1)
                                                .broadcast_to([P, n_exp, blocks]), ALU.is_gt))
                    own(nc.vector.tensor_reduce(tiles_of, t3, AX.X, ALU.add))
                    own(nc.vector.memset(cmp, 1.0))
                    own(nc.vector.tensor_tensor_scan(ends, cmp, tiles_of, 0.0, ALU.mult, ALU.add))
                    own(nc.vector.tensor_tensor(begins, ends, tiles_of, ALU.subtract))
                    own(nc.vector.tensor_scalar(cmp, begins, tok_no, None, ALU.is_le))
                    own(nc.vector.tensor_reduce(mp[:, 0:1], cmp, AX.X, ALU.add))
                    own(nc.vector.tensor_scalar(mp[:, 0:1], mp[:, 0:1], -1.0, None, ALU.add))
                    own(nc.vector.tensor_tensor(cmp, cmp, begins, ALU.mult))
                    own(nc.vector.tensor_reduce(mp[:, 2:3], cmp, AX.X, ALU.max))
                    own(nc.vector.tensor_scalar(mp[:, 3:4], mp[:, 0:1], float(blocks), tok_no, ALU.mult, ALU.add))
                    own(nc.vector.tensor_tensor(mp[:, 3:4], mp[:, 3:4], mp[:, 2:3], ALU.subtract))
                    own(nc.vector.tensor_tensor(mp[:, 4:5], tok_no, ends[:, n_exp - 1:n_exp], ALU.is_lt))
                    own(nc.vector.tensor_scalar(mp[:, 1:2], mp[:, 3:4], -float(P), None, ALU.add))
                    for a, at in ((0, 3), (1, 1)):
                        own(nc.vector.tensor_scalar(col_hot[:, a, :], iota, mp[:, at:at + 1], mp[:, 4:5],
                                                    ALU.is_equal, ALU.mult))
                dve.wait_ge(found, 1)
                own(nc.vector.tensor_tensor(masked, ps[:, 4:4 + MB, :].rearrange("p a (g c) -> p (a g) c", c=P),
                                            diagonal.rearrange("p (o c) -> p o c", o=1).broadcast_to([P, NG, P]),
                                            ALU.mult))
                dve.sem_inc(masked_done, 1)
                dve.wait_ge(spread_done, 1)
                own(nc.vector.tensor_tensor(picked.rearrange("p (c l) -> p c l", l=L),
                                            ps[:, 6:6 + MB, :].rearrange("p a (c l) -> p (a c) l", l=L),
                                            low_mask[:, 0:L].rearrange("p (o l) -> p o l", o=1)
                                            .broadcast_to([P, NG * P // L, L]), ALU.mult))
                own(nc.vector.tensor_reduce(vals.rearrange("p e v h -> p (e v h)"),
                                            picked.rearrange("p (c l) -> p c l", l=L), AX.X, ALU.add))
                own(nc.vector.tensor_scalar(free_of, vals[:, :, 1, :], 0.0, w["dummy"], ALU.is_equal, ALU.mult))
                own(nc.vector.scalar_tensor_tensor(out=ids, in0=vals[:, :, 1, :], scalar=float(T), in1=vals[:, :, 0, :],
                                                   op0=ALU.mult, op1=ALU.add))
                if not dynamic:
                    own(nc.vector.scalar_tensor_tensor(out=idx.rearrange("p (e h) -> p e h", h=blocks), in0=ids,
                                                       scalar=-float(T), in1=free_of, op0=ALU.add, op1=ALU.add))
                else:
                    own(nc.vector.tensor_tensor(ids, ids, free_of, ALU.add))
                    own(nc.vector.tensor_scalar(ids, ids, w["dummy"], None, ALU.subtract))
                    dve.sem_inc(map_done, 1)
                    dve.wait_ge(map_turned, 1)
                    own(nc.vector.tensor_copy(tile_map[0:1, :], ps[0:1, 0, 0:P]))
                    own(nc.vector.tensor_copy(ids_t.rearrange("p a c -> p (a c)"), ps[:, 1, 0:2 * P]))
                    own(nc.vector.tensor_copy(col_t.rearrange("p a c -> p (a c)"), ps[:, 2, 0:2 * P]))
                    dve.sem_inc(map_taken, 1)
                    dve.wait_ge(sorted_done, 1)
                    own(nc.vector.tensor_scalar(idx, ps[:, 3, 0:n_tiles], w["dummy"], -float(T), ALU.add, ALU.add))

            @block.scalar
            def _(act):
                for half, es in enumerate(halves):
                    act.wait_ge(hot_done, half + 1)
                    for b in range(NB):
                        nc.scalar.activation(rhs[:, b, es, 1, :], rhs[:, b, es, 0, :], ACT.Copy, scale=float(b + 1))\
                            .then_inc(rhs_done, 1)
                    act.wait_ge(rhs_done, (NB + 1) * (half + 1) - 1)
                    nc.scalar.activation(rhs[:, :, es, 0, :], rhs[:, :, es, 0, :], ACT.Copy, scale=tok_no).then_inc(rhs_done, 1)

            @block.tensor
            def _(pe):
                for g in range(NG):
                    half, g0 = divmod(g, NG // 2)
                    if g0 == 0:
                        pe.wait_ge(ups_done, half + 1)
                        pe.wait_ge(rhs_done, (NB + 1) * (half + 1))
                    c = g * P % BANK
                    for b in range(NB):
                        ins = nc.tensor.matmul(ps[:, 4 + g * P // BANK, c:c + P],
                                               ups[half][:, b, g0 * G:(g0 + 1) * G, :].rearrange("p e h -> p (e h)"),
                                               rhs[:, b, g * G:(g + 1) * G].rearrange("p e v h -> p (e v h)"),
                                               start=(b == 0), stop=(b == NB - 1))
                ins.then_inc(found, 1)
                pe.wait_ge(masked_done, 1)
                for a in range(MB):
                    ins = nc.tensor.matmul(ps[:, 6 + a, :], spread, masked.rearrange("p g c -> p (g c)")
                                           [:, a * BANK:(a + 1) * BANK], start=True, stop=True)
                ins.then_inc(spread_done, 1)
                if dynamic:
                    pe.wait_ge(map_done, 1)
                    nc.tensor.transpose(ps[0:1, 0, 0:P], mp[:, 0:1], ident)
                    for a in range(2):
                        nc.tensor.transpose(ps[:, 1, a * P:(a + 1) * P],
                                            ids.rearrange("p e h -> p (e h)")[:, a * P:(a + 1) * P], ident)
                        ins = nc.tensor.transpose(ps[:, 2, a * P:(a + 1) * P], col_hot[:, a, :], ident)
                    ins.then_inc(map_turned, 1)
                    pe.wait_ge(map_taken, 1)
                    for a in range(2):
                        ins = nc.tensor.matmul(ps[:, 3, 0:n_tiles], ids_t[:, a, :], col_t[:, a, 0:n_tiles],
                                               start=(a == 0), stop=(a == 1))
                    ins.then_inc(sorted_done, 1)

            @block.sync
            def _(sp):
                by_seq = lambda t: t[0:NT].rearrange("(b t) d -> t b d", t=T)
                n = dma_all(sp, [(by_seq(table)[:, :, 0:D], xn_tok), (by_seq(table)[:, :, D:], wt),
                                 (by_seq(sums[0]), x_tok)], table_here)
                sp.wait_ge(zero_done, 1)
                z3 = zero[:, 0:D].rearrange("p (o d) -> p o d", o=1)
                n += dma_all(sp, [(table[NT:], zero), (sums[0][NT:], zero[:, 0:D]), (sums[1][NT:], zero[:, 0:D]),
                                  (by_seq(sums[1]), z3.broadcast_to([P, NB, D]))], table_here)
                sp.wait_ge(table_here, n)

        idx_here, turned, xt_taken, gu_done, silu_done, av_done, a_turned, a_taken, down_done, y_taken = map(
            sem, ("idx_here", "turned", "xt_taken", "gu_done", "silu_done", "av_done", "a_turned", "a_taken",
                  "down_done", "y_taken"))
        gathered = [sem(f"gathered{r}") for r in range(RING)]
        added = [sem("added0"), sem("added1")]
        paced = sem("paced")
        n = n_tiles
        assert n % (2 * RING) == 0 and fw <= P

        def expert(eng, i):
            return eng.value_load(tile_map[0:1, bass.ds(i, 1)], min_val=0, max_val=n_exp - 1) if dynamic else i

        with nc.Block() as block:
            @block.gpsimd
            def _(pool):
                def take_index(i, k):
                    nc.gpsimd.tensor_copy(ixb[:, k * RING:(k + 1) * RING], idx[:, bass.ds(i, RING)])\
                        .then_inc(idx_here, 1)

                def gather(r, k):
                    pool.sem_inc(paced, 1)
                    nc.gpsimd.indirect_dma_start(xe[r], None, table, bass.IndirectOffsetOnAxis(ap=ixb[:, k:k + 1], axis=0))\
                        .then_inc(gathered[r], 16)

                def add(i, r, k, before):
                    pool.wait_ge(y_taken, i + 1)
                    if not isinstance(before, int) or before:
                        pool.wait_ge(added[r % 2], before * 16)
                    pool.sem_inc(paced, 1)
                    nc.gpsimd.indirect_dma_start(sums[r % 2], bass.IndirectOffsetOnAxis(ap=ixb[:, k:k + 1], axis=0),
                                                 ye[r], None, compute_op=ALU.add)\
                        .then_inc(added[r % 2], 16)

                R2 = 2 * RING
                for k in range(R2):
                    r = k % RING
                    if r == 0:
                        take_index(k, k // RING)
                        pool.wait_ge(idx_here, k // RING + 1)
                    if k >= RING:
                        pool.wait_ge(turned, k - RING + 1)
                        pool.wait_ge(av_done, k - RING + 1)
                        pool.wait_ge(added[r % 2], ((k - RING) // 2 + 1) * 16)
                    gather(r, k)
                    if k >= LAG:
                        add(k - LAG, (k - LAG) % RING, k - LAG, (k - LAG) // 2)
                with pool.Fori(1, n // R2) as j:
                    for k in range(R2):
                        i, r = R2 * j + k, k % RING
                        if r == 0:
                            take_index(i, k // RING)
                            pool.wait_ge(idx_here, 2 * j + k // RING + 1)
                        pool.wait_ge(turned, i - RING + 1)
                        pool.wait_ge(av_done, i - RING + 1)
                        pool.wait_ge(added[r % 2], (RING * j + (k - RING) // 2 + 1) * 16)
                        gather(r, k)
                        add(i - LAG, (r - LAG) % RING, (k - LAG) % R2, RING * j + (k - LAG) // 2)
                for i in range(n - LAG, n):
                    add(i, i % RING, i % R2, i // 2)
                for q in range(2):
                    pool.wait_ge(added[q], n // 2 * 16)

            @block.tensor
            def _(pe):
                def turn(q, r, fills):
                    pe.wait_ge(gathered[r], fills * 16)
                    for k in range(KT):
                        ins = nc.tensor.transpose(ps[:, q, k * P:(k + 1) * P], xe[r][:, k * P:(k + 1) * P], ident)
                    ins.then_inc(turned, 1)

                def gate_up(i, q):
                    e = expert(pe, i)
                    pe.wait_ge(xt_taken, i + 1)
                    for k in range(KT):
                        ins = nc.tensor.matmul(ps[:, 2 + q, 0:2 * inner], xe_t[q][:, k, :],
                                               w_gu[:, bass.ds(e, 1), k, :].rearrange("p e f -> p (e f)"),
                                               start=(k == 0), stop=(k == KT - 1))
                    ins.then_inc(gu_done, 1)

                def turn_a(i, q):
                    pe.wait_ge(av_done, i + 1)
                    for f in range(f_n):
                        ins = nc.tensor.transpose(ps[0:fw, 4 + q, f * P:(f + 1) * P], av[q][:, f * fw:(f + 1) * fw], ident)
                    ins.then_inc(a_turned, 1)

                def down(i, q):
                    e = expert(pe, i)
                    pe.wait_ge(a_taken, i + 1)
                    for f in range(f_n):
                        ins = nc.tensor.matmul(ps[:, 6 + q, 0:D], av_t[q][0:fw, f, :],
                                               w_dn[0:fw, bass.ds(e, 1), f, :].rearrange("p e d -> p (e d)"),
                                               start=(f == 0), stop=(f == f_n - 1))
                    ins.then_inc(down_done, 1)

                def step(i, r, fills, first=False, last=False):
                    q = r % 2
                    gate_up(i, q)
                    turn_a(i - 1, 1 - q)
                    if not last:
                        turn(1 - q, (r + 1) % RING, fills)
                    if not first:
                        down(i - 2, q)

                turn(0, 0, 1)
                turn(1, 1, 1)
                gate_up(0, 0)
                for i in range(1, RING):
                    step(i, i, (i + 1) // RING + 1, first=(i == 1))
                with pe.Fori(1, n // RING - 1) as j:
                    for r in range(RING):
                        step(RING * j + r, r, j + 1 + (r + 1) // RING)
                for i in range(n - RING, n):
                    step(i, i % RING, (i + 1) // RING + 1, last=(i == n - 1))
                turn_a(n - 1, 1)
                down(n - 2, 0)
                down(n - 1, 1)

            @block.scalar
            def _(act):
                def gate(i, q):
                    act.wait_ge(gu_done, i + 1)
                    nc.scalar.activation(sg[q], ps[:, 2 + q, 0:inner], ACT.Silu).then_inc(silu_done, 1)

                def take_a(i, q):
                    act.wait_ge(a_turned, i + 1)
                    nc.scalar.activation(av_t[q][0:fw].rearrange("p f s -> p (f s)"), ps[0:fw, 4 + q, 0:f_n * P], ACT.Copy)\
                        .then_inc(a_taken, 1)

                def take_y(i, r):
                    act.wait_ge(down_done, i + 1)
                    nc.scalar.activation(ye[r], ps[:, 6 + r % 2, 0:D], ACT.Copy).then_inc(y_taken, 1)

                def step(i, r):
                    gate(i, r % 2)
                    take_a(i - 1, (r - 1) % 2)
                    take_y(i - 2, (r - 2) % RING)

                gate(0, 0)
                gate(1, 1)
                take_a(0, 0)
                for i in range(2, RING):
                    step(i, i)
                with act.Fori(1, n // RING) as j:
                    for r in range(RING):
                        step(RING * j + r, r)
                take_a(n - 1, 1)
                take_y(n - 2, RING - 2)
                take_y(n - 1, RING - 1)

            @block.vector
            def _(dve):
                def take(i, q):
                    dve.wait_ge(turned, i + 1)
                    nc.vector.tensor_copy(xe_t[q].rearrange("p k s -> p (k s)"), ps[:, q, 0:KT * P]).then_inc(xt_taken, 1)

                def product(i, q, r):
                    e = expert(dve, i)
                    dve.wait_ge(silu_done, i + 1)
                    nc.vector.scalar_tensor_tensor(out=av[q], in0=ps[:, 2 + q, inner:2 * inner],
                                                   scalar=xe[r][:, bass.ds(D + e, 1)], in1=sg[q],
                                                   op0=ALU.mult, op1=ALU.mult).then_inc(av_done, 1)

                take(0, 0)
                for i in range(RING):
                    take(i + 1, (i + 1) % 2)
                    product(i, i % 2, i)
                with dve.Fori(1, n // RING - 1) as j:
                    for r in range(RING):
                        take(RING * j + r + 1, (r + 1) % 2)
                        product(RING * j + r, r % 2, r)
                for i in range(n - RING, n):
                    if i < n - 1:
                        take(i + 1, (i + 1) % 2)
                    product(i, i % 2, i % RING)

        pieces = [slice(c * BPC, (c + 1) * BPC) for c in range(CH)]
        back_here, back_added, stored = [sem(f"back_here{c}") for c in range(CH)], sem("back_added"), sem("stored")
        with nc.Block() as block:
            @block.sync
            def _(sp):
                by_seq = lambda t: t[0:NT].rearrange("(b t) d -> t b d", t=T)
                for c, bs in enumerate(pieces):
                    dma_all(sp, [(x_tok[:, bs, :], by_seq(sums[0])[:, bs, :]), (back[:, bs, :], by_seq(sums[1])[:, bs, :])],
                            back_here[c])
                if out is not None:
                    for c, bs in enumerate(pieces):
                        sp.wait_ge(back_added, c + 1)
                        sp.dma_start(out.rearrange("b t d -> t b d")[:, bs, :], x_tok[:, bs, :]).then_inc(stored, 16)
                    sp.wait_ge(stored, 16 * CH)

            @block.vector
            def _(dve):
                for c, bs in enumerate(pieces):
                    dve.wait_ge(back_here[c], 32)
                    nc.vector.tensor_tensor(x_tok[:, bs, :], x_tok[:, bs, :], back[:, bs, :], ALU.add).then_inc(back_added, 1)


HEADS1, HD1, NS1 = 8, 64, 64
XT1 = HEADS1 * HD1 // P
RMS_EPS = 1e-5


def ssd_layer(nc, ps, sems, ident, arena_at, x_tok, small, w):
    A = Arena(arena_at.tensor)
    A.at = arena_at.at
    XC = HEADS1 * HD1
    xn_t = A.take(KT * NT).rearrange("p (k t) -> p k t", k=KT)
    w_z = A.take(KT * XC).rearrange("p (k o) -> p k o", k=KT)
    w_xbc = A.take(KT * (XC + 2 * NS1)).rearrange("p (k o) -> p k o", k=KT)
    w_dt = A.take(KT * HEADS1).rearrange("p (k o) -> p k o", k=KT)
    wo = A.take(XT1 * D).rearrange("p (i d) -> p i d", i=XT1)
    nw = A.take(XT1)
    cw = A.take((XT1 + 1) * TAPS).rearrange("p (m k) -> p m k", k=TAPS)
    cb = A.take(XT1 + 1)
    dtb, rate, skip = A.take(HEADS1), A.take(HEADS1), A.take(HEADS1)
    masks = A.take(2 * P).rearrange("p (j t) -> p j t", j=2)
    b_t, c_t = A.take(NT), A.take(NT)
    tok = lambda n: A.take(NB * n).rearrange("p (b c) -> p b c", b=NB)
    xh, zs = tok(XC), tok(XC)
    dt, da, e, g, ln = tok(HEADS1), tok(HEADS1), tok(HEADS1), tok(HEADS1), tok(HEADS1)
    sq, rstd = A.take(NB), A.take(NB)
    at0 = A.at
    xc = A.take(XT1 * NT).rearrange("p (m t) -> p m t", m=XT1)
    at1 = A.at
    pre = [A.take(NB * (T + TAPS - 1)).rearrange("p (b t) -> p b t", b=NB) for _ in range(2)]
    acc = [A.take(NT) for _ in range(2)]
    A.at = at1
    xn_tok = A.take(NB * D).rearrange("p (b d) -> p b d", d=D)
    A.at = at0
    two = lambda *d: A.take(2 * d[0] * d[1]).rearrange("p (q a c) -> p q a c", q=2, a=d[0])
    gm = two(1, T)
    seg_l, ex = two(HEADS1, T), two(HEADS1, T)
    xdt, dx, yz = two(HEADS1, HD1), two(HEADS1, HD1), two(HEADS1, HD1)
    yz_t = two(XT1, T)
    raw = A.take(NB * D).rearrange("p (b d) -> p b d", d=D)
    junk = A.take(XC)

    with ExitStack() as ctx:
        sem = sems
        w_here = sem("l1_weights")
        bc = lambda a: a.broadcast_to([P, HEADS1])

        def load(sp):
            n = dma_all(sp, [(w_z, w["z"]), (w_xbc, w["xbc"]), (w_dt, w["dt"]), (wo, w["out_proj"]), (nw, w["norm_w"]),
                             (cw, w["conv_w"]), (cb, w["conv_b"]), (dtb, bc(w["dt_bias"])), (rate, bc(w["a_log"])),
                             (skip, bc(w["d"])), (masks, w["masks"])], w_here)
            sp.wait_ge(w_here, n)

        norm_stage(nc, ps, sems, ident, x_tok, xn_tok,
                   lambda k, c: xn_t[:, k, c * BANK:(c + 1) * BANK].rearrange("p (b t) -> p b t", t=T), small, "ssd", load)
        def put_x(m):
            if m < XT1:
                return [(xc[:, m, :], acc[m % 2])]
            return [(b_t[0:NS1], acc[m % 2][0:NS1]), (c_t[0:NS1], acc[m % 2][NS1:])]

        z_done, z_taken, dtp_done, xt_done, xt_taken, dve_own, act_own, ab_done, one_e, ln_done = map(
            sem, ("z_done", "z_taken", "dt1_proj", "x1_turned", "x1_taken", "dve_own_s1", "act_own_s1",
                  "dt1_abs", "dt1_one_e", "dt1_ln"))
        conv_stage(nc, ps, sems, xn_t, w_xbc, XT1 + 1, put_x, 0, None, cw, cb, pre, acc, "m1",
                   (w_z, zs, w_dt, z_done, z_taken, dtp_done))

        v8 = lambda r: r.rearrange("p (o h) -> p o h", o=1).broadcast_to([P, NB, HEADS1])
        with nc.Block() as block:
            @block.tensor
            def _(pe):
                for b in range(NB):
                    if b >= 3:
                        pe.wait_ge(xt_taken, b - 2)
                    for m in range(XT1):
                        ins = nc.tensor.transpose(ps[:, 3 + b % 3, m * P:(m + 1) * P], xc[:, m, b * T:(b + 1) * T], ident)
                    ins.then_inc(xt_done, 1)

            @block.scalar
            def _(act):
                own = Chain(act, act_own)
                own(nc.scalar.activation(rate, rate, ACT.Exp))
                nc.scalar.mul(rate, rate, -1.0).then_inc(ab_done, 1)
                act.wait_ge(one_e, 1)
                own(nc.scalar.activation(e, dt, ACT.Abs))
                nc.scalar.activation(e, e, ACT.Exp, scale=-1.0).then_inc(ab_done, 1)
                act.wait_ge(one_e, 2)
                nc.scalar.activation(ln, g, ACT.Ln).then_inc(ln_done, 1)

            @block.vector
            def _(dve):
                own = Chain(dve, dve_own)

                def take_x(first, last):
                    for b in range(first, last):
                        dve.wait_ge(xt_done, b + 1)
                        nc.vector.tensor_copy(xh[:, b, :], ps[:, 3 + b % 3, :]).then_inc(xt_taken, 1)

                nc.vector.tensor_tensor(dt, ps[:, 7, 0:NB * HEADS1].rearrange("p (b h) -> p b h", b=NB), v8(dtb), ALU.add)\
                    .then_inc(one_e, 1)
                for m in range(XT1):
                    own(nc.vector.tensor_scalar(wo[:, m, :], wo[:, m, :], nw[:, m:m + 1], None, ALU.mult))
                take_x(0, 4)
                dve.wait_ge(ab_done, 2)
                nc.vector.tensor_scalar(g, e, 1.0, None, ALU.add).then_inc(one_e, 1)
                dve.wait_ge(one_e, 2)
                own(nc.vector.scalar_tensor_tensor(out=e, in0=g, scalar=1.0, in1=e, op0=ALU.subtract, op1=ALU.subtract))
                take_x(4, 8)
                dve.wait_ge(ln_done, 1)
                own(nc.vector.tensor_tensor(ln, ln, e, ALU.subtract))
                own(nc.vector.scalar_tensor_tensor(out=dt, in0=dt, scalar=0.0, in1=ln, op0=ALU.max, op1=ALU.add))
                own(nc.vector.tensor_tensor(da, dt, v8(rate), ALU.mult))
                take_x(8, NB)

        g_done, gm_done, lm_done, xd_done, dx_done, seg_done, ex_done, m_done, y_done, yz_done, sq_done, t_done, \
            t_taken, o_done, o_taken = map(sem, (
                "cb_done", "cb_masked", "seg_left", "xdt_done", "skip_done", "seg_done", "seg_exp", "mix_done", "ssd_y",
                "ssd_gated", "ssd_square", "ssd_turned", "ssd_turn_taken", "ssd_out", "ssd_out_taken"))
        flat = lambda r: r.rearrange("p a c -> p (a c)")
        with nc.Block() as block:
            @block.gpsimd
            def _(pool):
                for b in range(NB):
                    q = b % 2
                    if b >= 2:
                        pool.wait_ge(seg_done, b - 1)
                    nc.gpsimd.tensor_tensor(seg_l[:, q], masks[:, 0:1, :].broadcast_to([P, HEADS1, T]),
                                            da[:, b, :].rearrange("p (h o) -> p h o", o=1).broadcast_to([P, HEADS1, T]),
                                            ALU.mult).then_inc(lm_done, 1)
                    if b >= 2:
                        pool.wait_ge(y_done, b - 1)
                    x3 = xh[:, b, :].rearrange("p (h d) -> p h d", h=HEADS1)
                    nc.gpsimd.tensor_tensor(xdt[:, q], x3, dt[:, b, :].rearrange("p (h o) -> p h o", o=1)
                                            .broadcast_to([P, HEADS1, HD1]), ALU.mult).then_inc(xd_done, 1)
                    if b >= 2:
                        pool.wait_ge(yz_done, 2 * (b - 2) + 1)
                    nc.gpsimd.tensor_tensor(dx[:, q], x3, skip.rearrange("p (h o) -> p h o", o=1)
                                            .broadcast_to([P, HEADS1, HD1]), ALU.mult).then_inc(dx_done, 1)

            @block.tensor
            def _(pe):
                def scores(b):
                    q = b % 2
                    if b >= 1:
                        pe.wait_ge(gm_done, b)
                    nc.tensor.matmul(ps[:, 0, q * T:(q + 1) * T], b_t[0:NS1, b * T:(b + 1) * T],
                                     c_t[0:NS1, b * T:(b + 1) * T], start=True, stop=True).then_inc(g_done, 1)
                    pe.wait_ge(lm_done, b + 1)
                    if b >= 2:
                        pe.wait_ge(ex_done, b - 1)
                    for h in range(HEADS1):
                        ins = nc.tensor.matmul(ps[:, 1 + 2 * q + h // 4, (h % 4) * T:(h % 4 + 1) * T], seg_l[:, q, h, :],
                                               masks[:, 1, :], start=True, stop=True)
                    ins.then_inc(seg_done, 1)

                def mix(b):
                    q = b % 2
                    pe.wait_ge(m_done, b + 1)
                    pe.wait_ge(xd_done, b + 1)
                    if b >= 1:
                        pe.wait_ge(yz_done, 2 * (b - 1) + 1)
                    for h in range(HEADS1):
                        ins = nc.tensor.matmul(ps[:, 5, h * HD1:(h + 1) * HD1], ex[:, q, h, :], xdt[:, q, h, :],
                                               start=True, stop=True)
                    ins.then_inc(y_done, 1)

                def turn(b):
                    q = b % 2
                    pe.wait_ge(yz_done, 2 * b + 2)
                    if b >= 1:
                        pe.wait_ge(t_taken, b)
                    for m in range(XT1):
                        ins = nc.tensor.transpose(ps[:, 6, m * P:(m + 1) * P], flat(yz[:, q])[:, m * P:(m + 1) * P], ident)
                    ins.then_inc(t_done, 1)

                def project(b):
                    q = b % 2
                    pe.wait_ge(t_taken, b + 1)
                    if b >= 1:
                        pe.wait_ge(o_taken, b)
                    for m in range(XT1):
                        ins = nc.tensor.matmul(ps[:, 7, q * D:(q + 1) * D], yz_t[:, q, m, :], wo[:, m, :],
                                               start=(m == 0), stop=(m == XT1 - 1))
                    ins.then_inc(o_done, 1)
                for s in range(NB + 2):
                    if s < NB:
                        scores(s)
                    if s >= 2:
                        turn(s - 2)
                    if 1 <= s <= NB:
                        mix(s - 1)
                    if s >= 2:
                        project(s - 2)

            @block.scalar
            def _(act):
                for s in range(NB + 2):
                    if s < NB:
                        act.wait_ge(seg_done, s + 1)
                        if s >= 2:
                            act.wait_ge(y_done, s - 1)
                        nc.scalar.activation(flat(ex[:, s % 2]),
                                             ps[:, 1 + 2 * (s % 2):3 + 2 * (s % 2), :].rearrange("p a c -> p (a c)"),
                                             ACT.Exp).then_inc(ex_done, 1)
                    if s >= 2:
                        b = s - 2
                        act.wait_ge(t_done, b + 1)
                        if b >= 2:
                            act.wait_ge(o_done, b - 1)
                        nc.scalar.activation(flat(yz_t[:, b % 2]), ps[:, 6, :], ACT.Copy).then_inc(t_taken, 1)
                        if b >= 1:
                            act.wait_ge(sq_done, b)
                        nc.scalar.activation(junk, flat(yz[:, b % 2]), ACT.Square, accum_out=sq[:, b:b + 1])\
                            .then_inc(sq_done, 1)

            @block.vector
            def _(dve):
                for s in range(NB + 2):
                    if s < NB:
                        q = s % 2
                        dve.wait_ge(g_done, s + 1)
                        if s >= 2:
                            dve.wait_ge(m_done, s - 1)
                        nc.vector.tensor_tensor(gm[:, q, 0, :], ps[:, 0, q * T:(q + 1) * T], masks[:, 1, :], ALU.mult)\
                            .then_inc(gm_done, 1)
                        dve.wait_ge(gm_done, s + 1)
                        dve.wait_ge(ex_done, s + 1)
                        nc.vector.tensor_tensor(ex[:, q], ex[:, q], gm[:, q].broadcast_to([P, HEADS1, T]), ALU.mult)\
                            .then_inc(m_done, 1)
                    if 1 <= s <= NB:
                        b, q = s - 1, (s - 1) % 2
                        dve.wait_ge(y_done, b + 1)
                        dve.wait_ge(dx_done, b + 1)
                        if b >= 2:
                            dve.wait_ge(t_done, b - 1)
                            dve.wait_ge(sq_done, b - 1)
                        nc.vector.tensor_tensor(flat(yz[:, q]), ps[:, 5, :], flat(dx[:, q]), ALU.add).then_inc(yz_done, 1)
                        dve.wait_ge(yz_done, 2 * b + 1)
                        nc.vector.tensor_tensor(flat(yz[:, q]), flat(yz[:, q]), zs[:, b, :], ALU.mult).then_inc(yz_done, 1)
                    if s >= 2:
                        b = s - 2
                        dve.wait_ge(o_done, b + 1)
                        nc.vector.tensor_copy(raw[:, b, :], ps[:, 7, (b % 2) * D:(b % 2 + 1) * D]).then_inc(o_taken, 1)

        var_done, std_done, own_sem = sem("rms_var"), sem("rms_std"), sem("dve_own_rms")
        with nc.Block() as block:
            @block.vector
            def _(dve):
                own = Chain(dve, own_sem)
                nc.vector.tensor_scalar(sq, sq, 1.0 / XC, RMS_EPS, ALU.mult, ALU.add).then_inc(var_done, 1)
                dve.wait_ge(std_done, 1)
                own(nc.vector.reciprocal(rstd, sq))
                for b in range(NB):
                    ins = nc.vector.scalar_tensor_tensor(out=x_tok[:, b, :], in0=raw[:, b, :], scalar=rstd[:, b:b + 1],
                                                         in1=x_tok[:, b, :], op0=ALU.mult, op1=ALU.add)
                own(ins)

            @block.scalar
            def _(act):
                act.wait_ge(var_done, 1)
                nc.scalar.activation(sq, sq, ACT.Sqrt).then_inc(std_done, 1)


HEADS2, HD2 = 16, 8


def longconv_layer(nc, ps, sems, ident, arena_at, x_tok, small, w):
    A = Arena(arena_at.tensor)
    A.at = arena_at.at
    PAIRS, UP = HD2 * HD2, HD2 // 2
    xn_tok = A.take(NB * D).rearrange("p (b d) -> p b d", d=D)
    q_t = A.take(KT * NT).rearrange("p (k h i b) -> p k h i b", k=KT, h=HEADS2, i=HD2)
    c_rev = A.take(KT * NT).rearrange("p (k h i b) -> p k h i b", k=KT, h=HEADS2, i=HD2)
    toep = A.take(HEADS2 * 2 * P).rearrange("p (h m) -> p h m", h=HEADS2)
    kv = A.take(2 * KT * PAIRS * NB).rearrange("p (q k i j b) -> p q k i j b", q=2, k=KT, i=HD2, j=HD2)
    prod = A.take(2 * PAIRS * NB).rearrange("p (q i j b) -> p q i j b", q=2, i=HD2, j=HD2)
    y_t = A.take(KT * NT).rearrange("p (k h n) -> p k h n", k=KT, h=HEADS2)
    skip = A.take(HEADS2)
    anti = A.take(P)
    with ExitStack() as ctx:
        sem = sems
        w_here = sem("conv_here")
        src = w["kernel"]
        toep_src = bass.AP(tensor=src.tensor, offset=0, ap=[[1, P], [src.shape[1], HEADS2], [1, 2 * P]])

        def load(sp):
            n = dma_all(sp, [(c_rev.rearrange("p k h i b -> p k (h i b)"), w["ctx_rev"]), (toep, toep_src),
                             (skip, w["d"].broadcast_to([P, HEADS2])), (anti, w["anti"])], w_here)
            sp.wait_ge(w_here, n)

        norm_stage(nc, ps, sems, ident, x_tok, xn_tok,
                   lambda k, c: q_t[:, k].rearrange("p h i b -> p b (h i)")[:, c * BPC:(c + 1) * BPC, :], small, "conv", load)
        diag_done, kv_done, conv_done, prod_done, red_done = map(
            sem, ("toep_diag", "kv_done", "lconv_done", "lprod_done", "lred_done"))
        with nc.Block() as block:
            @block.gpsimd
            def _(pool):
                for h in range(HEADS2):
                    if h >= 2:
                        pool.wait_ge(conv_done, KT * (h - 1))
                    for k in range(KT):
                        c = c_rev[:, k, h]
                        for a in range(2):
                            i, j = slice(a * UP, (a + 1) * UP), slice(a * UP, HD2)
                            shape = [P, UP, HD2 - a * UP, NB]
                            ins = nc.gpsimd.tensor_tensor(
                                kv[:, h % 2, k, i, j],
                                c[:, i].rearrange("p i (o b) -> p i o b", o=1).broadcast_to(shape),
                                c[:, j].rearrange("p (o j) b -> p o j b", o=1).broadcast_to(shape), ALU.mult)
                        ins.then_inc(kv_done, 1)

            @block.tensor
            def _(pe):
                for h in range(HEADS2):
                    pe.wait_ge(kv_done, KT * (h + 1))
                    pe.wait_ge(diag_done, h + 1)
                    for l in range(KT):
                        s = KT * h + l
                        if s >= 4:
                            pe.wait_ge(prod_done, s - 3)
                        for a in range(2):
                            for k in range(l + 1):
                                cols = UP * (HD2 - a * UP) * NB
                                mv = kv[:, h % 2, k, a * UP:(a + 1) * UP, a * UP:, :]
                                dst = ps[:, 2 * (s % 4) + a, 0:cols]
                                if a:
                                    dst = dst.rearrange("p (i j b) -> p i (j b)", i=UP, b=NB)
                                    mv = mv.rearrange("p i j b -> p i (j b)")
                                else:
                                    mv = mv.rearrange("p i j b -> p (i j b)")
                                ins = nc.tensor.matmul(dst, toep[:, h, (l - k) * P:(l - k + 1) * P],
                                                       mv, start=(k == 0), stop=(k == l))
                        ins.then_inc(conv_done, 1)

            @block.vector
            def _(dve):
                for h in range(HEADS2):
                    nc.vector.scalar_tensor_tensor(out=toep[:, h, 0:P], in0=anti, scalar=skip[:, h:h + 1],
                                                   in1=toep[:, h, 0:P], op0=ALU.mult, op1=ALU.add).then_inc(diag_done, 1)
                for h in range(HEADS2):
                    for l in range(KT):
                        s = KT * h + l
                        dve.wait_ge(conv_done, s + 1)
                        if s >= 2:
                            dve.wait_ge(red_done, s - 1)
                        low = ps[:, 2 * (s % 4), :].rearrange("p (i j b) -> p i j b", i=UP, b=NB)
                        high = ps[:, 2 * (s % 4) + 1, 0:UP * UP * NB].rearrange("p (i j b) -> p i j b", i=UP, b=NB)
                        qv = lambda i, j: q_t[:, l, h, i].rearrange("p i (o b) -> p i o b", o=1).broadcast_to([P, UP, j, NB])
                        lower, upper = slice(0, UP), slice(UP, HD2)
                        nc.vector.tensor_tensor(prod[:, s % 2, lower], low, qv(lower, HD2), ALU.mult)
                        nc.vector.tensor_tensor(prod[:, s % 2, upper, lower],
                                                low[:, :, upper].rearrange("p j i b -> p i j b"), qv(upper, UP), ALU.mult)
                        nc.vector.tensor_tensor(prod[:, s % 2, upper, upper], high, qv(upper, UP), ALU.mult)\
                            .then_inc(prod_done, 1)
                        dve.wait_ge(prod_done, s + 1)
                        nc.vector.tensor_reduce(y_t[:, l, h, :], prod[:, s % 2].rearrange("p i j b -> p (j b) i"),
                                                AX.X, ALU.add).then_inc(red_done, 1)
        add_transposed_stage(nc, ps, sems, ident, x_tok,
                             lambda k, b: y_t[:, k].rearrange("p h (j b) -> p b (h j)", b=NB)[:, b, :], "conv")


def ffn1_layer(nc, ps, sems, ident, arena_at, x_tok, small, w, out):
    A = Arena(arena_at.tensor)
    A.at = arena_at.at
    C, CP, fw = E1, 24, I1 // 2
    BLOCKS, TILES = NT // P, K1 * NT // P + E1
    w_gu = A.take(E1 * KT * 2 * I1).rearrange("p (e k f) -> p e k f", e=E1, k=KT)
    w_dn = A.take(E1 * 2 * D).rearrange("p (e f d) -> p e f d", e=E1, f=2)
    cst = A.take(CONST)
    mask16 = A.take(P).bitcast(BF16).rearrange("p (j t) -> p j t", j=2)
    xn_tok = A.take(NB * D).rearrange("p (b d) -> p b d", d=D)
    xn_t = A.take(KT * NT).rearrange("p (k t) -> p k t", k=KT)
    wr = A.take(KT * C).rearrange("p (k c) -> p k c", k=KT)
    bias = A.take(C)
    tok = lambda n: A.take(NB * n).rearrange("p (b c) -> p b c", b=NB)
    sc, left, top8, wt, row, row2, place = tok(CP), tok(CP), tok(8), tok(C), tok(1), tok(1), tok(C)
    ch16, before = (A.take(NB * C // 2).bitcast(BF16).rearrange("p (b c) -> p b c", b=NB) for _ in range(2))
    all16 = A.take(C // 2).bitcast(BF16)
    queue = A.take(C)
    with ExitStack() as ctx:
        sem = sems
        w_here, experts_here, dve_own = sem("r1_here"), sem("experts1_here"), sem("dve_own_r1")

        def load(sp):
            n = dma_all(sp, [(wr, w["cls"]), (bias, w["bias"].broadcast_to([P, C])), (mask16, w["mask16"]),
                             (cst, w["const"])], w_here)
            dma_all(sp, [(w_gu, w["gate_up"]), (w_dn[0:fw], w["down"])], experts_here)
            sp.wait_ge(w_here, n)

        norm_stage(nc, ps, sems, ident, x_tok, xn_tok,
                   lambda k, c: xn_t[:, k, c * BANK:(c + 1) * BANK].rearrange("p (b t) -> p b t", t=T),
                   small, "ffn1", load)
        logit_done, shifted, exp_done, prefix_done, pos_done = map(
            sem, ("r1_logit", "r1_shift", "r1_exp", "r1_prefix", "r1_pos"))
        with nc.Block() as block:
            @block.tensor
            def _(pe):
                for b in range(NB):
                    for k in range(KT):
                        ins = nc.tensor.matmul(ps[:, 0, b * C:(b + 1) * C], xn_t[:, k, b * T:(b + 1) * T], wr[:, k, :],
                                               start=(k == 0), stop=(k == KT - 1))
                ins.then_inc(logit_done, 1)
                pe.wait_ge(prefix_done, 1)
                places = ps[:, 2, 0:NB * C]
                nc.tensor.matmul(places, mask16[:, 0, :], ch16.rearrange("p b c -> p (b c)"), start=True, stop=False)
                nc.tensor.matmul(places, mask16[:, 1, :], before.rearrange("p b c -> p (b c)"), start=False, stop=True)
                nc.tensor.matmul(ps[:, 3, 0:C], mask16[:, 1, :], all16, start=True, stop=True).then_inc(pos_done, 1)

            @block.scalar
            def _(act):
                act.wait_ge(shifted, 1)
                nc.scalar.activation(wt, wt, ACT.Exp).then_inc(exp_done, 1)

            @block.vector
            def _(dve):
                own = Chain(dve, dve_own)
                dve.wait_ge(logit_done, 1)
                over = lambda r: r.broadcast_to([P, NB, C])
                own(nc.vector.tensor_tensor(wt, ps[:, 0, 0:NB * C].rearrange("p (b c) -> p b c", b=NB),
                                            bias.rearrange("p (o c) -> p o c", o=1).broadcast_to([P, NB, C]), ALU.add))
                own(nc.vector.tensor_reduce(row, wt, AX.X, ALU.max))
                nc.vector.tensor_tensor(wt, wt, over(row), ALU.subtract).then_inc(shifted, 1)
                own(nc.vector.memset(sc[:, :, C:], -1.0))
                dve.wait_ge(exp_done, 1)
                own(nc.vector.tensor_reduce(row2, wt, AX.X, ALU.add))
                own(nc.vector.reciprocal(row, row2))
                own(nc.vector.tensor_tensor(sc[:, :, 0:C], wt, over(row), ALU.mult))
                for b in range(NB):
                    ins = nc.vector.max(top8[:, b, :], sc[:, b, :])
                own(ins)
                own(nc.vector.memset(top8[:, :, K1:], -1.0))
                for b in range(NB):
                    ins = nc.vector.match_replace(left[:, b, :], top8[:, b, :], sc[:, b, :], -2.0)
                own(ins)
                own(nc.vector.tensor_tensor(left, left, sc, ALU.not_equal))
                own(nc.vector.tensor_copy(ch16, left[:, :, 0:C]))
                own(nc.vector.memset(before[:, 0, :], 0.0))
                for b in range(1, NB):
                    own(nc.vector.tensor_tensor(before[:, b, :], before[:, b - 1, :], ch16[:, b - 1, :], ALU.add))
                nc.vector.tensor_tensor(all16, before[:, NB - 1, :], ch16[:, NB - 1, :], ALU.add).then_inc(prefix_done, 1)
                own(nc.vector.tensor_tensor(wt, sc[:, :, 0:C], left[:, :, 0:C], ALU.mult))
                own(nc.vector.tensor_reduce(row2, wt, AX.X, ALU.add))
                own(nc.vector.reciprocal(row, row2))
                own(nc.vector.tensor_tensor(wt, wt, over(row), ALU.mult))
                dve.wait_ge(pos_done, 1)
                own(nc.vector.scalar_tensor_tensor(out=place, in0=ps[:, 2, 0:NB * C].rearrange("p (b c) -> p b c", b=NB),
                                                   scalar=1.0, in1=left[:, :, 0:C], op0=ALU.add, op1=ALU.mult))
                own(nc.vector.tensor_scalar(place, place, -1.0, None, ALU.add))
                own(nc.vector.tensor_copy(queue, ps[:, 3, 0:C]))

            @block.sync
            def _(sp):
                sp.wait_ge(experts_here, 32)
        sparse_experts(nc, ps, sems, ident, A, x_tok, xn_tok, wt, place, E1, BLOCKS, TILES, H1, I1, 2,
                       {"w_gu": w_gu, "w_dn": w_dn, "dummy": cst[:, 1:2], "spare": xn_t.rearrange("p k t -> p (k t)"),
                        "queue": queue}, expert_const(cst), "e1", out)


def build(nc, ins, out):
    with ExitStack() as ctx:
        sbuf = ctx.enter_context(nc.sbuf_tensor("sbuf", [P, 52900], F32))
        ps = ctx.enter_context(nc.psum_tensor("ps", [P, NBANK, BANK], F32))
        A = Arena(sbuf)
        ident = A.take(P)
        small = A.take(176)
        x_tok = A.take(NB * D).rearrange("p (b d) -> p b d", d=D)
        sems = Semaphores(nc)
        in_here = nc.alloc_semaphore(name="in_here")
        with nc.Block() as block:
            @block.sync
            def _(sp):
                n = dma_all(sp, [(x_tok, ins["x"].rearrange("b t d -> t b d")), (ident, ins["ident"])], in_here)
                sp.wait_ge(in_here, n)
        scan_layer(nc, ps, sems, ident, A, x_tok, small, {k[3:]: v for k, v in ins.items() if k.startswith("m0_")})
        sems.clear()
        wkv_layer(nc, ps, sems, ident, A, x_tok, small, {k[3:]: v for k, v in ins.items() if k.startswith("c0_")})
        sems.clear()
        ffn0_layer(nc, ps, sems, ident, A, x_tok, small, {k[3:]: v for k, v in ins.items() if k.startswith("f0_")})
        sems.clear()
        ssd_layer(nc, ps, sems, ident, A, x_tok, small, {k[3:]: v for k, v in ins.items() if k.startswith("m1_")})
        sems.clear()
        longconv_layer(nc, ps, sems, ident, A, x_tok, small, {k[3:]: v for k, v in ins.items() if k.startswith("c1_")})
        sems.clear()
        ffn1_layer(nc, ps, sems, ident, A, x_tok, small, {k[3:]: v for k, v in ins.items() if k.startswith("f1_")}, out)


def _layout(inputs):
    import numpy as np

    def tiles(a):
        return a.reshape(-1, P, a.shape[-1]).transpose(1, 0, 2)

    g = {k: np.asarray(v) for k, v in inputs.items()}
    o = {"x": g["x"], "ident": np.eye(P, dtype=np.float32)}
    w = g["L0_attn_in_proj_w"].reshape(INNER, 2, D)
    o["m0_in_proj"] = tiles(np.concatenate([w[:, 0].T, w[:, 1].T], axis=1))
    o["m0_conv_w"] = tiles(g["L0_attn_conv_w"])
    o["m0_conv_b"] = g["L0_attn_conv_b"].reshape(MT, P).T
    xp = g["L0_attn_x_proj_weight"].transpose(0, 2, 1).reshape(INNER, RANK + BC)
    o["m0_x_dt"] = tiles(xp[:, :RANK])
    o["m0_x_bc"] = tiles(xp[:, RANK:])
    o["m0_dt_proj"] = g["L0_attn_dt_proj_weight"].transpose(2, 0, 1).reshape(RANK, MT, P)
    o["m0_dt_bias"] = g["L0_attn_dt_proj_bias"].reshape(MT, P).T
    o["m0_a_log"] = g["L0_attn_A_log"].reshape(HEADS0, MH, P, NS).transpose(2, 0, 1, 3).reshape(P, HEADS0, MH * NS)
    o["m0_d"] = g["L0_attn_D"].reshape(HEADS0, MH, P).transpose(2, 0, 1)
    o["m0_out_proj"] = tiles(g["L0_attn_out_proj_w"].T)
    sel = np.zeros((P, BC), "bfloat16")
    sel[:3 * BC] = np.arange(3 * BC)[:, None] % BC == np.arange(BC)[None, :]
    o["m0_sel"] = sel
    ctx = g["ctx_2048"].reshape(NT, D)
    o["c0_ctx_t"] = tiles(ctx.T)
    o["c0_decay"] = g["L0_xattn_time_decay"].reshape(KT, P).T
    o["c0_first"] = g["L0_xattn_time_first"].reshape(KT, P).T
    o["f0_cls"] = tiles(g["L0_ffn_w_cls"].T)
    o["f0_bias"] = g["L0_ffn_bias"].reshape(1, -1)
    before = np.arange(P)[:, None] < np.arange(P)[None, :]
    o["f0_mask16"] = np.stack([before, np.ones((P, P))], axis=1).astype("bfloat16")
    o["f0_gate_up"] = g["L0_ffn_w_gate_up"].reshape(E0, KT, P, 2 * I0).transpose(2, 0, 1, 3)
    o["f0_down"] = g["L0_ffn_w_down"].reshape(E0, 1, I0, D).transpose(2, 0, 1, 3)
    def expert_table(up_values, blocks):
        low_values, part = P // up_values, np.arange(P)
        const = np.zeros((P, CONST), np.float32)
        const[:, 0] = part
        const[:, 1] = part + NT + P
        const[:, 2:19] = np.arange(17) * P
        const[:, 20:20 + P] = part
        cols = part // (2 * blocks * low_values)
        const[:, 20 + P:20 + 2 * P] = (part // up_values)[:, None] == cols
        const[:, 20 + 2 * P:20 + 3 * P] = (part % up_values)[:, None] == part // low_values
        const[:, 20 + 3 * P:20 + 3 * P + low_values] = (part % low_values)[:, None] == np.arange(low_values)
        return const

    o["f0_const"] = expert_table(H0, 1)
    o["f1_const"] = expert_table(H1, NT // P)
    win = g["L1_attn_W_in"]
    xc = HEADS1 * HD1
    o["m1_z"] = tiles(win[:xc].T)
    o["m1_xbc"] = tiles(win[xc:2 * xc + 2 * NS1].T)
    o["m1_dt"] = tiles(win[2 * xc + 2 * NS1:].T)
    o["m1_out_proj"] = tiles(g["L1_attn_W_out"].T)
    o["m1_norm_w"] = g["L1_attn_norm_w"].reshape(XT1, P).T
    o["m1_conv_w"] = tiles(g["L1_attn_conv_w"])
    o["m1_conv_b"] = g["L1_attn_conv_b"].reshape(XT1 + 1, P).T
    for name, key in (("dt_bias", "dt_bias"), ("a_log", "A_log"), ("d", "D")):
        o[f"m1_{name}"] = g[f"L1_attn_{key}"].reshape(1, -1)
    lower = np.arange(P)[:, None] > np.arange(P)[None, :]
    o["m1_masks"] = np.stack([lower, ~lower], axis=1).astype(np.float32)
    o["c1_ctx_rev"] = g["ctx_2048"].transpose(2, 1, 0).reshape(KT, P, NT)[:, ::-1].transpose(1, 0, 2)
    o["c1_kernel"] = np.pad(g["L1_xattn_ssm_kernel"], ((0, 0), (P - 1, 0)))
    o["c1_d"] = g["L1_xattn_D"].reshape(1, -1)
    o["c1_anti"] = np.eye(P, dtype=np.float32)[::-1]
    o["f1_cls"] = tiles(g["L1_ffn_router_w"].T)
    o["f1_bias"] = g["L1_ffn_expert_bias"].reshape(1, -1)
    gu = np.concatenate([g["L1_ffn_gate_proj"], g["L1_ffn_up_proj"]], axis=2)
    o["f1_gate_up"] = gu.reshape(E1, KT, P, 2 * I1).transpose(2, 0, 1, 3)
    o["f1_down"] = g["L1_ffn_down_proj"].reshape(E1, 2, I1 // 2, D).transpose(2, 0, 1, 3)
    o["f1_mask16"] = o["f0_mask16"]
    return {k: np.ascontiguousarray(v) for k, v in o.items()}


def kernel(**inputs):
    import numpy as np
    import concourse.bacc as _bacc
    from concourse.bass_utils import run_bass_kernel_spmd as _run

    nc = _bacc.Bacc("TRN2", target_bir_lowering=False, num_devices=1)
    arrays = _layout(inputs)
    aps = {k: nc.dram_tensor(f"in_{k}", a.shape, mybir.dt.from_np(a.dtype), kind="ExternalInput").ap()
           for k, a in arrays.items()}
    out = nc.dram_tensor("out", (NB, T, D), F32, kind="ExternalOutput").ap()
    build(nc, aps, out)
    got = _run(nc, [{f"in_{k}": a for k, a in arrays.items()}], core_ids=[0])
    return got.results[0]["out"]
```
